# Optimizing a Trainium2 kernel written in Bass

```python
import numpy as np
import jax
import jax.numpy as jnp

def _softmax(x, axis=-1):
    return jax.nn.softmax(x, axis=axis)

def _gelu(x):
    return jax.nn.gelu(x, approximate=True)

def _silu(x):
    return jax.nn.silu(x)

def _sigmoid(x):
    return jax.nn.sigmoid(x)

def _layernorm(x, axis=-1, eps=1e-05):
    m = jnp.mean(x, axis=axis, keepdims=True)
    v = jnp.var(x, axis=axis, keepdims=True)
    return (x - m) / jnp.sqrt(v + eps)

def _scatter_add(tgt, idx, src, axis=0):
    return tgt.at[idx].add(src)

def _segment_sum(src, seg, n):
    return jax.ops.segment_sum(src, seg, n)
kernel_name = 'mk_recurrent_d2_jaxref_r8_57fc0e'

def setup_inputs(seed: int=0):
    np.random.seed(seed)
    _w = jnp.asarray

    def _L0_attn_setup():
        import math
        import jax, jax.numpy as jnp
        import numpy as np
        CHUNK = 32
        EPS = 1e-05

        def l2norm(x):
            return x * jax.lax.rsqrt(jnp.sum(x * x, -1, keepdims=True))

        def causal_dwconv(x, w):
            C, K = w.shape
            return jax.lax.conv_general_dilated(x, w[:, None, :], (1,), [(K - 1, 0)], feature_group_count=C)

        def per_head_stats(x):
            mean = jnp.mean(x, -1, keepdims=True)
            var = jnp.mean(x * x, -1, keepdims=True) - mean * mean
            abs_mean = jnp.mean(jnp.abs(x), -1, keepdims=True)
            l2 = jnp.sqrt(jnp.sum(x * x, -1, keepdims=True))
            return jnp.concatenate([mean, var, abs_mean, l2], -1)

        def delta_rule_chunkwise(q, k, v, beta, chunk=CHUNK):
            b, h, L, dk = q.shape
            dv = v.shape[-1]
            pad = -L % chunk
            if pad:
                pc = ((0, 0), (0, 0), (0, pad), (0, 0))
                q, k, v = (jnp.pad(t, pc) for t in (q, k, v))
                beta = jnp.pad(beta, ((0, 0), (0, 0), (0, pad)))
            Lp = L + pad
            n = Lp // chunk
            q = l2norm(q)
            k = l2norm(k)
            v = v * beta[..., None]
            kb = k * beta[..., None]
            resh = lambda t: t.reshape(b, h, n, chunk, t.shape[-1])
            q, k, v, kb = map(resh, (q, k, v, kb))
            tri = jnp.triu(jnp.ones((chunk, chunk), bool))
            strict = jnp.triu(jnp.ones((chunk, chunk), bool), 1)
            A = jnp.where(tri, 0.0, -jnp.einsum('bhncd,bhned->bhnce', kb, k))
            for i in range(1, chunk):
                upd = jnp.einsum('...k,...kj->...j', A[..., i, :], A[..., :, :i])
                A = A.at[..., i, :i].add(upd)
            inv = A + jnp.eye(chunk, dtype=A.dtype)
            u = inv @ v
            w = inv @ kb

            def step(S, xs):
                qi, ki, ui, wi = xs
                attn = jnp.where(strict, 0.0, qi @ jnp.swapaxes(ki, -1, -2))
                u_adj = ui - wi @ S
                out_i = qi @ S + attn @ u_adj
                S = S + jnp.swapaxes(ki, -1, -2) @ u_adj
                return (S, out_i)
            xs = tuple((jnp.moveaxis(t, 2, 0) for t in (q, k, u, w)))
            S0 = jnp.zeros((b, h, dk, dv), q.dtype)
            S, outs = jax.lax.scan(step, S0, xs)
            out = jnp.moveaxis(outs, 0, 2).reshape(b, h, Lp, dv)[:, :, :L]
            return (out, S)
        key = jax.random.key(seed)
        ks = jax.random.split(key, 16)
        B, L, D, H = (2, 512, 128, 4)
        dk, dv = (D, D)
        dh = dv // H
        gate_in_dim = D + 16
        gate_hidden = D * 2 // 2
        s = 0.02
        f32 = jnp.float32
        return {'hidden_states': jax.random.normal(ks[0], (B, L, D), f32), 'q_proj_w': jax.random.normal(ks[1], (dk, D), f32) * s, 'k_proj_w': jax.random.normal(ks[2], (dk, D), f32) * s, 'v_proj_w': jax.random.normal(ks[3], (dv, D), f32) * s, 'b_proj_w': jax.random.normal(ks[4], (H, D), f32) * s, 'q_conv_w': jax.random.normal(ks[5], (dk, 4), f32) * 0.1, 'k_conv_w': jax.random.normal(ks[6], (dk, 4), f32) * 0.1, 'v_conv_w': jax.random.normal(ks[7], (dv, 4), f32) * 0.1, 'fir_short_w': jax.random.normal(ks[8], (H, dh, 5), f32) * 0.02, 'fir_long_w': jax.random.normal(ks[9], (H, dh, 64), f32) * 0.02, 'fuse_w1': jax.random.normal(ks[10], (gate_hidden, gate_in_dim), f32) * s, 'fuse_b1': jnp.zeros((gate_hidden,), f32), 'fuse_w2': jax.random.normal(ks[11], (4, gate_hidden), f32) * s, 'fuse_b2': jnp.array([-1.0, -1.0, 1.0, 3.0], f32), 'logit_temp': jnp.full((1,), math.log(math.expm1(0.7)), f32), 'res_scale_short': jnp.full((1,), 0.1, f32), 'res_scale_long': jnp.full((1,), 0.1, f32), 'o_norm_w': jnp.ones((dh,), f32), 'o_proj_w': jax.random.normal(ks[12], (D, dv), f32) * s}
    _L0_attn_in = _L0_attn_setup()

    def _L0_ffn_setup():
        import jax, jax.numpy as jnp
        import numpy as np
        TOPK = 4
        key = jax.random.key(seed)
        ks = jax.random.split(key, 9)
        B, T, D = (4, 256, 128)
        E, H = (32, 128)
        HS = H * TOPK
        s = lambda k, shape, fan: jax.random.normal(k, shape, dtype=jnp.float32) / np.sqrt(fan)
        return {'x': jax.random.normal(ks[0], (B, T, D), dtype=jnp.float32), 'router_w': s(ks[1], (E, D), D), 'router_bias': jnp.zeros((E,), dtype=jnp.float32), 'gate_w': s(ks[2], (E, H, D), D), 'up_w': s(ks[3], (E, H, D), D), 'down_w': s(ks[4], (E, D, H), H), 'sgate_w': s(ks[5], (HS, D), D), 'sup_w': s(ks[6], (HS, D), D), 'sdown_w': s(ks[7], (D, HS), HS)}
    _L0_ffn_in = _L0_ffn_setup()

    def _L1_attn_setup():
        import jax, jax.numpy as jnp
        import numpy as np
        B, N, D, H = (4, 512, 128, 16)
        GN_EPS = 0.00064
        key = jax.random.key(seed)
        ks = jax.random.split(key, 12)
        x = jax.random.normal(ks[0], (B, N, D), jnp.float32)
        ddd = jnp.linspace(0.0, 1.0, D).reshape(1, 1, D)
        s = 1.0 / np.sqrt(D)
        w = lambda k: jax.random.normal(k, (D, D), jnp.float32) * s
        return {'x': x, 'x_r': 1.0 - ddd ** 0.2, 'x_w': 1.0 - ddd ** 0.9, 'x_k': 1.0 - ddd ** 0.7, 'x_v': 1.0 - ddd ** 0.7, 'x_a': 1.0 - ddd ** 0.9, 'x_g': 1.0 - ddd ** 0.2, 'W_r': w(ks[1]), 'W_w': w(ks[2]), 'W_k': w(ks[3]), 'W_v': w(ks[4]), 'W_a': w(ks[5]), 'W_g': w(ks[6]), 'W_out': jax.random.normal(ks[7], (D, D), jnp.float32) * s, 'b_out': jax.random.normal(ks[8], (D,), jnp.float32) * 0.01, 'gn_w': 1.0 + 0.1 * jax.random.normal(ks[9], (D,), jnp.float32), 'gn_b': 0.1 * jax.random.normal(ks[10], (D,), jnp.float32)}
    _L1_attn_in = _L1_attn_setup()

    def _L1_ffn_setup():
        import jax, jax.numpy as jnp
        import numpy as np
        D_IN, D_HID = (128, 512)

        def _ternary(key, shape):
            return jax.random.randint(key, shape, -1, 2).astype(jnp.float32)

        def _tlin(x, w, s):
            return jnp.einsum('bsi,oi->bso', x, w) * s
        key = jax.random.key(seed)
        ks = jax.random.split(key, 12)
        inv = lambda fan: 1.0 / np.sqrt(fan).astype(np.float32)
        return {'x': jax.random.normal(ks[0], (4, 256, D_IN), dtype=jnp.float32), 'w1_w': _ternary(ks[1], (D_HID, D_IN)), 'w1_s': jax.random.uniform(ks[2], (D_HID,), dtype=jnp.float32) * inv(D_IN), 'w2_w': _ternary(ks[3], (D_HID, D_IN)), 'w2_s': jax.random.uniform(ks[4], (D_HID,), dtype=jnp.float32) * inv(D_IN), 'h1_w': _ternary(ks[5], (D_HID, D_HID)), 'h1_s': jax.random.uniform(ks[6], (D_HID,), dtype=jnp.float32) * inv(D_HID), 'h2_w': _ternary(ks[7], (D_HID, D_HID)), 'h2_s': jax.random.uniform(ks[8], (D_HID,), dtype=jnp.float32) * inv(D_HID), 'w3_w': _ternary(ks[9], (D_IN, D_HID)), 'w3_s': jax.random.uniform(ks[10], (D_IN,), dtype=jnp.float32) * inv(D_HID)}
    _L1_ffn_in = _L1_ffn_setup()
    _d = {'L0_attn_hidden_states': _L0_attn_in['hidden_states'], 'L0_attn_q_proj_w': _L0_attn_in['q_proj_w'], 'L0_attn_k_proj_w': _L0_attn_in['k_proj_w'], 'L0_attn_v_proj_w': _L0_attn_in['v_proj_w'], 'L0_attn_b_proj_w': _L0_attn_in['b_proj_w'], 'L0_attn_q_conv_w': _L0_attn_in['q_conv_w'], 'L0_attn_k_conv_w': _L0_attn_in['k_conv_w'], 'L0_attn_v_conv_w': _L0_attn_in['v_conv_w'], 'L0_attn_fir_short_w': _L0_attn_in['fir_short_w'], 'L0_attn_fir_long_w': _L0_attn_in['fir_long_w'], 'L0_attn_fuse_w1': _L0_attn_in['fuse_w1'], 'L0_attn_fuse_b1': _L0_attn_in['fuse_b1'], 'L0_attn_fuse_w2': _L0_attn_in['fuse_w2'], 'L0_attn_fuse_b2': _L0_attn_in['fuse_b2'], 'L0_attn_logit_temp': _L0_attn_in['logit_temp'], 'L0_attn_res_scale_short': _L0_attn_in['res_scale_short'], 'L0_attn_res_scale_long': _L0_attn_in['res_scale_long'], 'L0_attn_o_norm_w': _L0_attn_in['o_norm_w'], 'L0_attn_o_proj_w': _L0_attn_in['o_proj_w'], 'L0_ffn_router_w': _L0_ffn_in['router_w'], 'L0_ffn_router_bias': _L0_ffn_in['router_bias'], 'L0_ffn_gate_w': _L0_ffn_in['gate_w'], 'L0_ffn_up_w': _L0_ffn_in['up_w'], 'L0_ffn_down_w': _L0_ffn_in['down_w'], 'L0_ffn_sgate_w': _L0_ffn_in['sgate_w'], 'L0_ffn_sup_w': _L0_ffn_in['sup_w'], 'L0_ffn_sdown_w': _L0_ffn_in['sdown_w'], 'L1_attn_x_r': _L1_attn_in['x_r'], 'L1_attn_x_w': _L1_attn_in['x_w'], 'L1_attn_x_k': _L1_attn_in['x_k'], 'L1_attn_x_v': _L1_attn_in['x_v'], 'L1_attn_x_a': _L1_attn_in['x_a'], 'L1_attn_x_g': _L1_attn_in['x_g'], 'L1_attn_W_r': _L1_attn_in['W_r'], 'L1_attn_W_w': _L1_attn_in['W_w'], 'L1_attn_W_k': _L1_attn_in['W_k'], 'L1_attn_W_v': _L1_attn_in['W_v'], 'L1_attn_W_a': _L1_attn_in['W_a'], 'L1_attn_W_g': _L1_attn_in['W_g'], 'L1_attn_W_out': _L1_attn_in['W_out'], 'L1_attn_b_out': _L1_attn_in['b_out'], 'L1_attn_gn_w': _L1_attn_in['gn_w'], 'L1_attn_gn_b': _L1_attn_in['gn_b'], 'L1_ffn_w1_w': _L1_ffn_in['w1_w'], 'L1_ffn_w1_s': _L1_ffn_in['w1_s'], 'L1_ffn_w2_w': _L1_ffn_in['w2_w'], 'L1_ffn_w2_s': _L1_ffn_in['w2_s'], 'L1_ffn_h1_w': _L1_ffn_in['h1_w'], 'L1_ffn_h1_s': _L1_ffn_in['h1_s'], 'L1_ffn_h2_w': _L1_ffn_in['h2_w'], 'L1_ffn_h2_s': _L1_ffn_in['h2_s'], 'L1_ffn_w3_w': _L1_ffn_in['w3_w'], 'L1_ffn_w3_s': _L1_ffn_in['w3_s']}
    _x0 = _d['L0_attn_hidden_states']
    _d['L0_attn_hidden_states'] = jax.random.normal(jax.random.fold_in(jax.random.key(seed), 1), (16, 512, 128), dtype=_x0.dtype)
    del _x0
    return _d

def reference(L0_attn_hidden_states, L0_attn_q_proj_w, L0_attn_k_proj_w, L0_attn_v_proj_w, L0_attn_b_proj_w, L0_attn_q_conv_w, L0_attn_k_conv_w, L0_attn_v_conv_w, L0_attn_fir_short_w, L0_attn_fir_long_w, L0_attn_fuse_w1, L0_attn_fuse_b1, L0_attn_fuse_w2, L0_attn_fuse_b2, L0_attn_logit_temp, L0_attn_res_scale_short, L0_attn_res_scale_long, L0_attn_o_norm_w, L0_attn_o_proj_w, L0_ffn_router_w, L0_ffn_router_bias, L0_ffn_gate_w, L0_ffn_up_w, L0_ffn_down_w, L0_ffn_sgate_w, L0_ffn_sup_w, L0_ffn_sdown_w, L1_attn_x_r, L1_attn_x_w, L1_attn_x_k, L1_attn_x_v, L1_attn_x_a, L1_attn_x_g, L1_attn_W_r, L1_attn_W_w, L1_attn_W_k, L1_attn_W_v, L1_attn_W_a, L1_attn_W_g, L1_attn_W_out, L1_attn_b_out, L1_attn_gn_w, L1_attn_gn_b, L1_ffn_w1_w, L1_ffn_w1_s, L1_ffn_w2_w, L1_ffn_w2_s, L1_ffn_h1_w, L1_ffn_h1_s, L1_ffn_h2_w, L1_ffn_h2_s, L1_ffn_w3_w, L1_ffn_w3_s):

    def _L0_attn_ref(hidden_states, q_proj_w, k_proj_w, v_proj_w, b_proj_w, q_conv_w, k_conv_w, v_conv_w, fir_short_w, fir_long_w, fuse_w1, fuse_b1, fuse_w2, fuse_b2, logit_temp, res_scale_short, res_scale_long, o_norm_w, o_proj_w):
        import math
        import jax, jax.numpy as jnp
        import numpy as np
        CHUNK = 32
        EPS = 1e-05

        def l2norm(x):
            return x * jax.lax.rsqrt(jnp.sum(x * x, -1, keepdims=True))

        def causal_dwconv(x, w):
            C, K = w.shape
            return jax.lax.conv_general_dilated(x, w[:, None, :], (1,), [(K - 1, 0)], feature_group_count=C)

        def per_head_stats(x):
            mean = jnp.mean(x, -1, keepdims=True)
            var = jnp.mean(x * x, -1, keepdims=True) - mean * mean
            abs_mean = jnp.mean(jnp.abs(x), -1, keepdims=True)
            l2 = jnp.sqrt(jnp.sum(x * x, -1, keepdims=True))
            return jnp.concatenate([mean, var, abs_mean, l2], -1)

        def delta_rule_chunkwise(q, k, v, beta, chunk=CHUNK):
            b, h, L, dk = q.shape
            dv = v.shape[-1]
            pad = -L % chunk
            if pad:
                pc = ((0, 0), (0, 0), (0, pad), (0, 0))
                q, k, v = (jnp.pad(t, pc) for t in (q, k, v))
                beta = jnp.pad(beta, ((0, 0), (0, 0), (0, pad)))
            Lp = L + pad
            n = Lp // chunk
            q = l2norm(q)
            k = l2norm(k)
            v = v * beta[..., None]
            kb = k * beta[..., None]
            resh = lambda t: t.reshape(b, h, n, chunk, t.shape[-1])
            q, k, v, kb = map(resh, (q, k, v, kb))
            tri = jnp.triu(jnp.ones((chunk, chunk), bool))
            strict = jnp.triu(jnp.ones((chunk, chunk), bool), 1)
            A = jnp.where(tri, 0.0, -jnp.einsum('bhncd,bhned->bhnce', kb, k))
            for i in range(1, chunk):
                upd = jnp.einsum('...k,...kj->...j', A[..., i, :], A[..., :, :i])
                A = A.at[..., i, :i].add(upd)
            inv = A + jnp.eye(chunk, dtype=A.dtype)
            u = inv @ v
            w = inv @ kb

            def step(S, xs):
                qi, ki, ui, wi = xs
                attn = jnp.where(strict, 0.0, qi @ jnp.swapaxes(ki, -1, -2))
                u_adj = ui - wi @ S
                out_i = qi @ S + attn @ u_adj
                S = S + jnp.swapaxes(ki, -1, -2) @ u_adj
                return (S, out_i)
            xs = tuple((jnp.moveaxis(t, 2, 0) for t in (q, k, u, w)))
            S0 = jnp.zeros((b, h, dk, dv), q.dtype)
            S, outs = jax.lax.scan(step, S0, xs)
            out = jnp.moveaxis(outs, 0, 2).reshape(b, h, Lp, dv)[:, :, :L]
            return (out, S)
        B, L, D = hidden_states.shape
        H = fir_short_w.shape[0]

        def shortconv(x, w):
            y = causal_dwconv(jnp.swapaxes(x, 1, 2), w)
            return jax.nn.silu(jnp.swapaxes(y, 1, 2))
        q = shortconv(hidden_states @ q_proj_w.T, q_conv_w)
        k = shortconv(hidden_states @ k_proj_w.T, k_conv_w)
        v = shortconv(hidden_states @ v_proj_w.T, v_conv_w)
        q = q.reshape(B, L, H, -1)
        k = k.reshape(B, L, H, -1)
        v_direct = v.reshape(B, L, H, -1)
        beta = jax.nn.sigmoid(hidden_states @ b_proj_w.T)
        delta_out, _S = delta_rule_chunkwise(jnp.transpose(q, (0, 2, 1, 3)), jnp.transpose(k, (0, 2, 1, 3)), jnp.transpose(v_direct, (0, 2, 1, 3)), jnp.transpose(beta, (0, 2, 1)))
        delta_out = jnp.transpose(delta_out, (0, 2, 1, 3))

        def fir(x, filt):
            hh, dd, kk = filt.shape
            xf = jnp.swapaxes(x.reshape(B, L, hh * dd), 1, 2)
            y = causal_dwconv(xf, filt.reshape(hh * dd, kk))
            return jnp.swapaxes(y, 1, 2).reshape(B, L, hh, dd)
        local_short = fir(v_direct, fir_short_w)
        local_long = fir(v_direct, fir_long_w)
        stats = jnp.concatenate([per_head_stats(t) for t in (local_short, local_long, delta_out, v_direct)], -1)
        hs_exp = jnp.broadcast_to(hidden_states[:, :, None, :], (B, L, H, D))
        gate_in = jnp.concatenate([hs_exp, stats], -1)
        hdn = jax.nn.gelu(gate_in @ fuse_w1.T + fuse_b1, approximate=False)
        logits = hdn @ fuse_w2.T + fuse_b2
        temp = jax.nn.softplus(logit_temp) + 0.0001
        fw = jax.nn.softmax(logits / temp, -1)
        o = fw[..., 0:1] * local_short + fw[..., 1:2] * local_long + fw[..., 2:3] * delta_out + fw[..., 3:4] * v_direct
        o = o + res_scale_short * local_short + res_scale_long * local_long
        o = o * jax.lax.rsqrt(jnp.mean(o * o, -1, keepdims=True) + EPS) * o_norm_w
        return o.reshape(B, L, -1) @ o_proj_w.T

    def _L0_ffn_ref(x, router_w, router_bias, gate_w, up_w, down_w, sgate_w, sup_w, sdown_w):
        import jax, jax.numpy as jnp
        import numpy as np
        TOPK = 4
        B, T, D = x.shape
        flat = x.reshape(B * T, D)
        logits = flat.astype(jnp.float32) @ router_w.T + router_bias
        scores = jax.nn.softmax(logits, axis=-1)
        topk_scores, topk_idx = jax.lax.top_k(scores, TOPK)
        topk_scores = topk_scores / jnp.clip(topk_scores.sum(axis=-1, keepdims=True), 1e-12, None)
        h = jax.nn.silu(jnp.einsum('nd,ehd->neh', flat, gate_w)) * jnp.einsum('nd,ehd->neh', flat, up_w)
        expert_out = jnp.einsum('neh,edh->ned', h, down_w)
        sel = jnp.take_along_axis(expert_out, topk_idx[:, :, None], axis=1)
        out = (sel * topk_scores.astype(flat.dtype)[:, :, None]).sum(axis=1)
        out = out + jax.nn.silu(flat @ sgate_w.T) * (flat @ sup_w.T) @ sdown_w.T
        return out.reshape(B, T, D)

    def _L1_attn_ref(x, x_r, x_w, x_k, x_v, x_a, x_g, W_r, W_w, W_k, W_v, W_a, W_g, W_out, b_out, gn_w, gn_b):
        import jax, jax.numpy as jnp
        import numpy as np
        B, N, D, H = (4, 512, 128, 16)
        GN_EPS = 0.00064
        b, n, d = x.shape
        prev = jnp.concatenate([jnp.zeros_like(x[:, :1]), x[:, :-1]], axis=1)
        xx = prev - x
        lin = lambda mix, W: (x + xx * mix) @ W.T
        r = jax.nn.sigmoid(lin(x_r, W_r))
        decay = jnp.exp(-jax.nn.softplus(lin(x_w, W_w)))
        k = jnp.tanh(lin(x_k, W_k))
        v = lin(x_v, W_v)
        alpha = jax.nn.sigmoid(lin(x_a, W_a))
        g = jax.nn.sigmoid(lin(x_g, W_g))
        u = alpha * k * v

        def step(state, inp):
            d_t, u_t, r_t = inp
            state = state * d_t + u_t
            return (state, r_t * state)
        inputs_tm = (jnp.swapaxes(decay, 0, 1), jnp.swapaxes(u, 0, 1), jnp.swapaxes(r, 0, 1))
        state0 = jnp.zeros((b, d), x.dtype)
        _, mixed_tm = jax.lax.scan(step, state0, inputs_tm)
        mixed = jnp.swapaxes(mixed_tm, 0, 1)
        m = mixed.reshape(b * n, H, d // H)
        mu = m.mean(-1, keepdims=True)
        var = ((m - mu) ** 2).mean(-1, keepdims=True)
        mn = ((m - mu) / jnp.sqrt(var + GN_EPS)).reshape(b, n, d)
        mn = mn * gn_w + gn_b
        return mn * g @ W_out.T + b_out

    def _L1_ffn_ref(x, w1_w, w1_s, w2_w, w2_s, h1_w, h1_s, h2_w, h2_s, w3_w, w3_s):
        import jax, jax.numpy as jnp
        import numpy as np
        D_IN, D_HID = (128, 512)

        def _ternary(key, shape):
            return jax.random.randint(key, shape, -1, 2).astype(jnp.float32)

        def _tlin(x, w, s):
            return jnp.einsum('bsi,oi->bso', x, w) * s
        h = jax.nn.silu(_tlin(x, w1_w, w1_s)) * _tlin(x, w2_w, w2_s)
        h = jax.nn.gelu(_tlin(h, h1_w, h1_s), approximate=False)
        h = jax.nn.gelu(_tlin(h, h2_w, h2_s), approximate=False)
        return _tlin(h, w3_w, w3_s)
    x = L0_attn_hidden_states
    xn = _layernorm(x, axis=-1)
    s = _L0_attn_ref(xn, L0_attn_q_proj_w, L0_attn_k_proj_w, L0_attn_v_proj_w, L0_attn_b_proj_w, L0_attn_q_conv_w, L0_attn_k_conv_w, L0_attn_v_conv_w, L0_attn_fir_short_w, L0_attn_fir_long_w, L0_attn_fuse_w1, L0_attn_fuse_b1, L0_attn_fuse_w2, L0_attn_fuse_b2, L0_attn_logit_temp, L0_attn_res_scale_short, L0_attn_res_scale_long, L0_attn_o_norm_w, L0_attn_o_proj_w)
    g = _silu(_L0_ffn_ref(xn, L0_ffn_router_w, L0_ffn_router_bias, L0_ffn_gate_w, L0_ffn_up_w, L0_ffn_down_w, L0_ffn_sgate_w, L0_ffn_sup_w, L0_ffn_sdown_w))
    x = x + s * g
    xn = _layernorm(x, axis=-1)
    s = _L1_attn_ref(xn, L1_attn_x_r, L1_attn_x_w, L1_attn_x_k, L1_attn_x_v, L1_attn_x_a, L1_attn_x_g, L1_attn_W_r, L1_attn_W_w, L1_attn_W_k, L1_attn_W_v, L1_attn_W_a, L1_attn_W_g, L1_attn_W_out, L1_attn_b_out, L1_attn_gn_w, L1_attn_gn_b)
    g = _silu(_L1_ffn_ref(xn, L1_ffn_w1_w, L1_ffn_w1_s, L1_ffn_w2_w, L1_ffn_w2_s, L1_ffn_h1_w, L1_ffn_h1_s, L1_ffn_h2_w, L1_ffn_h2_s, L1_ffn_w3_w, L1_ffn_w3_s))
    x = x + s * g
    return x

_drawn_inputs = setup_inputs


def setup_inputs(seed=0):
    import zlib

    import numpy as np

    out = dict(_drawn_inputs(seed))
    spreads = {'L0_attn_fuse_b1': (0.0, 0.1),
     'L0_attn_o_norm_w': (1.0, 0.2),
     'L0_ffn_router_bias': (0.0, 0.1)}
    factors = {}
    for name, (base, spread) in spreads.items():
        noise = np.random.default_rng([zlib.crc32(name.encode()), seed]).standard_normal(out[name].shape)
        drawn = base * np.exp(spread * noise) if base else spread * noise
        out[name] = jnp.asarray(drawn.astype(out[name].dtype))
    for name, factor in factors.items():
        out[name] = (out[name] * factor).astype(out[name].dtype)
    return out
```

```python
import numpy as np
import concourse.bass as bass
from concourse import mybir
from contextlib import ExitStack

P = 128
B, L, D = 16, 512, 128
NT = L // P
H = 4
DH = D // H
CH = 32
NCH = L // CH
HT = H * NT
E, TOPK = 32, 4
ES = 4
EA = E + ES
KS, KL, KC = 5, 64, 4
NST = 16
FF = 4
LEVELS = 5
LN_EPS, RMS_EPS, GN_EPS = 1e-5, 1e-5, 0.00064

FILL = {"proj": 5, "tok": 5, "norm": 4, "L": 3, "A": 3, "inv": 1, "uw": 2, "au": 1, "fir": 3, "st": 3, "hid": 3}
for _l in range(1, LEVELS):
    FILL[f"lv{_l}a"] = 4
    FILL[f"lv{_l}b"] = 3
for _c in range(NCH):
    FILL[f"sc{_c}a"] = 1
    FILL[f"sc{_c}b"] = 2 if _c % 4 == 0 else 1
UNITS = 3 * EA + 1
FILL["hid"] += UNITS - sum(FILL.values())
assert FILL["hid"] >= 0
DVE_LINKS = 176

COLS = {}
_at = 0
for _n, _w in (("qc", KC), ("kc", KC), ("vc", KC), ("fs", KS), ("fl", KL), ("b1", 1), ("mix", 6), ("gnw", 1), ("gnb", 1),
               ("s1", FF), ("s2", FF), ("hs1", FF), ("hs2", FF), ("temp", 1), ("rss", 1), ("rsl", 1), ("b2", 4),
               ("onorm", DH), ("rbias", E), ("bout", D), ("w3s", D), ("w2T", 4)):
    COLS[_n] = (_at, _at + _w)
    _at += _w
NCOL = _at

CONS = {}
_at = 0
for _n, _w in (("ident", P), ("bd", P), ("avg", P), ("strict", P), ("causal", P), ("eye", CH), ("lvl", LEVELS * CH)):
    CONS[_n] = (_at, _at + _w)
    _at += _w
NCON = _at

WNAMES = ["wq", "wk", "wv", "w1x", "wo", "Wr", "Ww", "Wk", "Wv", "Wa", "Wg", "Wout"]


def build(nc, x, small, cons, wsq, wrb, w1s, moe_g, moe_u, moe_d, f1, f2, h1w, h2w, w3, out):
    f32 = mybir.dt.float32
    ACT = mybir.ActivationFunctionType
    ALU = mybir.AluOpType
    X = mybir.AxisListType.X

    x_v = x.rearrange("b (t p) d -> b p t d", p=P)
    out_v = out.rearrange("b (t p) d -> b p t d", p=P)

    ctx = ExitStack()
    with ctx:
        def sb(name, shape):
            return ctx.enter_context(nc.sbuf_tensor(name, shape, f32))

        def sem(name):
            return ctx.enter_context(nc.semaphore(name))

        sm = sb("sm", [P, NCOL])
        cn = sb("cn", [P, NCON])
        wm = sb("wm", [P, len(WNAMES), D])
        wrb_sb = sb("wrb_sb", [P, E + H])
        w1s_sb = sb("w1s_sb", [NST * H, H, P])
        eg = sb("eg", [P, EA, P])
        eu = sb("eu", [P, EA, P])
        ed = sb("ed", [P, EA, P])
        f1_sb = sb("f1_sb", [P, FF, P])
        f2_sb = sb("f2_sb", [P, FF, P])
        h1_sb = sb("h1_sb", [P, FF, FF * P])
        h2_sb = sb("h2_sb", [P, FF, FF * P])
        w3_sb = sb("w3_sb", [P, FF, D])

        def col(name, j=0, w=1):
            a, b = COLS[name]
            return sm[:, a + j:a + j + w]

        def con(name):
            a, b = CONS[name]
            return cn[:, a:b]

        def weight(name):
            return wm[:, WNAMES.index(name), :]

        ident = con("ident")

        xt = sb("xt", [P, L])
        xn = sb("xn", [P, L])
        xnT = sb("xnT", [P, L])
        vs, qs, ks = sb("vs", [P, L]), sb("qs", [P, L]), sb("ks", [P, L])
        vtok, qtok, ktok = sb("vtok", [P, L]), sb("qtok", [P, L]), sb("ktok", [P, L])
        vb, kb = sb("vb", [P, L]), sb("kb", [P, L])
        qnT, knT, kbT = sb("qnT", [P, L]), sb("knT", [P, L]), sb("kbT", [P, L])
        LT, AT = sb("LT", [P, HT, P]), sb("AT", [P, HT, P])
        Tbd = sb("Tbd", [P, HT, P])
        Xi, Ti, Yi, Zm = sb("Xi", [P, HT * CH]), sb("Ti", [P, HT * CH]), sb("Yi", [P, HT * CH]), sb("Zm", [P, HT * CH])
        U, WT, uadj = sb("U", [P, L]), sb("WT", [P, L]), sb("uadj", [P, L])
        Sbd = sb("Sbd", [P, P])
        dl = sb("dl", [P, L])
        fs, fl = sb("fs", [P, L]), sb("fl", [P, L])
        lstok, lltok = sb("lstok", [P, L]), sb("lltok", [P, L])
        sq4 = [sb(f"sq4_{j}", [P, L]) for j in range(4)]
        sg = [sb(f"sg{j}", [P, L]) for j in range(2)]
        hx = [sb(f"hx{j}", [P, L]) for j in range(2)]
        dt = sb("dt", [P, L])
        acc, accp = sb("acc", [P, L]), sb("accp", [P, L])
        gs = sb("gs", [P, L])
        x1 = sb("x1", [P, L])
        x2 = sb("x2", [P, L])
        yv, yq, yk = sq4[0], sq4[1], sq4[2]
        dq = Zm
        hdn = [Xi, Ti, Yi, Zm]
        pr = [qs, ks, qtok, ktok]
        o = U
        osq = WT
        oT = uadj
        xn1 = xn
        xn1p = sb("xn1p", [P, L + 4])
        dT = vs
        mixd = [fs, fl, lstok, lltok, vb, kb]
        sgf = [LT[:, 4 * c:4 * c + 4, :].rearrange("p a b -> p (a b)") for c in range(FF)]
        fh = [AT[:, 4 * c:4 * c + 4, :].rearrange("p a b -> p (a b)") for c in range(FF)]
        g1 = [Tbd[:, 4 * c:4 * c + 4, :].rearrange("p a b -> p (a b)") for c in range(FF)]
        g2 = sgf
        rg, dec, kt, al, gg = qnT, knT, kbT, qs, ks
        ak, uu, stt, mixed = qtok, ktok, vtok, U
        cen, sqc, rvar, mn, mg = WT, uadj, dl, Xi, Ti
        s1, g2r, g2s = Yi, Zm, gs

        bst = sb("bst", [P, NT, 6])
        mv = sb("mv", [P, NT, 2])
        vr = sb("vr", [P, NT])
        rstd = sb("rstd", [P, NT])
        lg = sb("lg", [P, NT, E])
        mx = sb("mx", [P, NT])
        sc = sb("sc", [P, NT, E + TOPK])
        ssum = sb("ssum", [P, NT])
        m8 = sb("m8", [P, NT, 8])
        m4 = sb("m4", [P, NT, 8])
        rep = sb("rep", [P, NT, E + TOPK])
        wsc = sb("wsc", [P, NT, E])
        beta = sb("beta", [P, NT, H])
        ss = sb("ss", [P, 2, HT])
        ssr = sb("ssr", [P, 2, HT])
        rn = sb("rn", [P, 2, HT])
        st_s, st_a, st_q = sb("st_s", [P, 4, HT]), sb("st_a", [P, 4, HT]), sb("st_q", [P, 4, HT])
        mean_c, m2_c, var_c = sb("mean_c", [P, 4, HT]), sb("m2_c", [P, 4, HT]), sb("var_c", [P, 4, HT])
        stats = sb("stats", [P, NT, 4, 4, H])
        statsT = sb("statsT", [NST * H, L])
        lgx = sb("lgx", [P, HT, 4])
        lmx = sb("lmx", [P, HT])
        fe = sb("fe", [P, HT, 4])
        fsum = sb("fsum", [P, HT])
        fw = sb("fw", [P, HT, 4])
        ms = sb("ms", [P, HT])
        msr = sb("msr", [P, HT])
        rms = sb("rms", [P, HT])
        spare = sb("spare", [P, 2])
        unit = sb("unit", [P, 2])
        tmp1 = sb("tmp1", [P, 4])
        invt = sb("invt", [P, 1])
        b2t = sb("b2t", [P, 4])

        ps = ctx.enter_context(nc.psum_tensor("ps", [P, 8, L], f32))
        G, Ub, Db, C0, C1, C2, C3, C4 = range(8)

        def bank(b):
            return ps[:, b, :]

        def tile(ap, t):
            return ap[:, t * P:(t + 1) * P]

        def byhead(ap):
            return ap.rearrange("p (a d) -> p a d", d=DH)

        def on_vector(d):
            return d % 2 == 0

        s_w = sem("weights_loaded")
        s_moe = sem("expert_weights_loaded")
        s_l1 = sem("layer1_weights_loaded")
        unit_ready = sem("unit_ready")
        pre_act, pre_dve, pre_pool = sem("pre_act"), sem("pre_dve"), sem("pre_pool")
        x_loaded, x_free, x2_ready, x2_stored = sem("x_loaded"), sem("x_free"), sem("x2_ready"), sem("x2_stored")
        vr0_ready, rstd0_ready, xn_ready, xT_ps, xnT_ready = sem("vr0_ready"), sem("rstd0_ready"), sem("xn_ready"), sem("xT_ps"), sem("xnT_ready")
        proj = {c: sem(f"proj_{c}") for c in "vqk"}
        tap = {c: sem(f"tap_{c}") for c in "vqk"}
        conv = {c: sem(f"conv_{c}") for c in "vqk"}
        silu = {c: sem(f"silu_{c}") for c in "vqk"}
        tok_ps = {c: sem(f"tok_ps_{c}") for c in "vqk"}
        tok = {c: sem(f"tok_{c}") for c in "vqk"}
        rb_ps, beta_ready, lgs_ready, ex_ready, wsc_ready = sem("rb_ps"), sem("beta_ready"), sem("lgs_ready"), sem("ex_ready"), sem("wsc_ready")
        sq_ready = {c: sem(f"sq_{c}") for c in "qk"}
        ssr_ready, rn_ready, qn_ready, kn_ready, kb_ready, vb_ready = (sem(n) for n in ("ssr_ready", "rn_ready", "qn_ready", "kn_ready", "kb_ready", "vb_ready"))
        nT_ps = {c: sem(f"nT_ps_{c}") for c in "qkb"}
        nT = {c: sem(f"nT_{c}") for c in "qkb"}
        l_ps, lt_ready, a_ps, at_ready = sem("l_ps"), sem("lt_ready"), sem("a_ps"), sem("at_ready")
        xi_ready, ti_ready, tbd_ready, y_ps = sem("xi_ready"), sem("ti_ready"), sem("tbd_ready"), sem("y_ps")
        y_ready, z_ps = sem("y_ready"), sem("z_ps")
        u_ps, wt_ps, u_ready, wt_ready, s0_ready = sem("u_ps"), sem("wt_ps"), sem("u_ready"), sem("wt_ready"), sem("s0_ready")
        ws_ps, uadj_ready = sem("ws_ps"), sem("uadj_ready")
        s_ps, s_ready = sem("s_ps"), sem("s_ready")
        au_ps, dq_ready, dl_ready = sem("au_ps"), sem("dq_ready"), sem("dl_ready")
        fir0 = sem("fir0")
        fs_ready, fl_ready, fsT_ps, flT_ps, ls_ready, ll_ready = (sem(n) for n in ("fs_ready", "fl_ready", "fsT_ps", "flT_ps", "ls_ready", "ll_ready"))
        sq4_ready = sem("sq4_ready")
        stq_ready, l2_ready, mvar_ready, stats_ready, stT_ps, stT_ready = (sem(n) for n in ("stq_ready", "l2_ready", "mvar_ready", "stats_ready", "stT_ps", "stT_ready"))
        hid_ps, hdn_ready = sem("hid_ps"), sem("hdn_ready")
        lgt_ps, lgx_ready, fe_ready, fw_ready, p23_ready, o_sum, osq_ready, msr_ready, rms_ready, on_ready, o_ready, oT_ps, oT_ready, sp_ps = (
            sem(n) for n in ("lgt_ps", "lgx_ready", "fe_ready", "fw_ready", "p23_ready", "o_sum", "osq_ready", "msr_ready", "rms_ready", "on_ready", "o_ready", "oT_ps", "oT_ready", "sp_ps"))
        asum_ready = sem("asum_ready")
        gs_ready = sem("gs_ready")
        g_ps, up_ps, d_ps, sg_ready, h_ready, dacc, dt_ready, pacc = (sem(n) for n in ("g_ps", "up_ps", "d_ps", "sg_ready", "h_ready", "dacc", "dt_ready", "pacc"))
        vr1_ready, rstd1_ready, xn1_ready, x1T_ps, x1T_ready = (sem(n) for n in ("vr1_ready", "rstd1_ready", "xn1_ready", "x1T_ps", "x1T_ready"))
        ffg_ps, ffu_ps, sgf_ready, fh_ready, h1_ps, g1_ready, h2_ps, g2_ready = (sem(n) for n in ("ffg_ps", "ffu_ps", "sgf_ready", "fh_ready", "h1_ps", "g1_ready", "h2_ps", "g2_ready"))
        mix_ready, pj_ps, pj_act = sem("mix_ready"), sem("pj_ps"), sem("pj_act")
        ak_ready, st_ready, mixed_ready, mu_ps, cen_ready, sqc_ready, var_ps, rvar_ready, rsd_ready, mn_ready, mg_ready, op_ps, w3_ps, g2r_ready, g2s_ready = (
            sem(n) for n in ("ak_ready", "st_ready", "mixed_ready", "mu_ps", "cen_ready", "sqc_ready", "var_ps", "rvar_ready", "rsd_ready", "mn_ready", "mg_ready", "op_ps", "w3_ps", "g2r_ready", "g2s_ready"))
        dve_link = sem("dve_link")

        block = ctx.enter_context(nc.Block())

        @block.sync
        def _(sp):
            for dst, src in ((sm[:, :], small), (cn[:, :], cons), (wm[:, :, :], wsq), (wrb_sb[:, :], wrb), (w1s_sb[:, :, :], w1s)):
                sp.dma_start(dst, src).then_inc(s_w, 16)
            sp.dma_start(xt[:, :].rearrange("p (t d) -> p t d", d=D), x_v[0]).then_inc(x_loaded, 16)
            for e0 in range(0, EA, 12):
                for dst, src in ((eg, moe_g), (eu, moe_u), (ed, moe_d)):
                    sp.dma_start(dst[:, e0:e0 + 12, :], src[:, e0:e0 + 12, :]).then_inc(s_moe, 16)
            for dst, src in ((f1_sb, f1), (f2_sb, f2), (h1_sb, h1w), (h2_sb, h2w), (w3_sb, w3)):
                sp.dma_start(dst[:, :, :], src).then_inc(s_l1, 16)
            with sp.Fori(1, B) as i:
                sp.wait_ge(x_free, i)
                sp.dma_start(xt[:, :].rearrange("p (t d) -> p t d", d=D),
                             x_v[bass.ds(i, 1), :, :, :].rearrange("b p t d -> p (b t) d")).then_inc(x_loaded, 16)
                sp.wait_ge(x2_ready, i)
                sp.dma_start(out_v[bass.ds(i - 1, 1), :, :, :].rearrange("b p t d -> p (b t) d"),
                             x2[:, :].rearrange("p (t d) -> p t d", d=D)).then_inc(x2_stored, 16)
            sp.wait_ge(x2_ready, B)
            sp.dma_start(out_v[B - 1], x2[:, :].rearrange("p (t d) -> p t d", d=D)).then_inc(x2_stored, 16)
            sp.wait_ge(x2_stored, 16 * (B + 1))

        @block.tensor
        def _(pe):
            mm = nc.tensor.matmul
            pe.wait_ge(s_w, 16 * 5)
            pe.wait_ge(s_moe, 16 * 9)
            pe.wait_ge(s_l1, 16 * 5)
            with pe.Fori(0, B) as i:
                n = pe.snap(i + 1)
                ie = pe.snap(i * EA)
                iq = pe.snap(i * (EA // 2))
                at = [0]

                def expert_unit(k):
                    e, kind = divmod(k, 3)
                    if kind == 0 and e < EA:
                        if e:
                            pe.wait_ge(sg_ready, ie + e)
                        mm(bank(G), eg[:, e, :], xnT[:, :], start=True, stop=True).then_inc(g_ps, 1)
                    elif kind == 1:
                        if e:
                            pe.wait_ge(h_ready, ie + e)
                        mm(bank(Ub), eu[:, e, :], xnT[:, :], start=True, stop=True).then_inc(up_ps, 1)
                    elif e > 0 or kind == 0:
                        d = e - 1
                        pe.wait_ge(h_ready, ie + d + 1)
                        if d:
                            pe.wait_ge(dacc if on_vector(d - 1) else dt_ready, iq + (d + 1) // 2)
                        for t in range(NT):
                            last = mm(tile(bank(Db), t), tile(hx[d % 2], t), ed[:, d, :], start=True, stop=True)
                        last.then_inc(d_ps, 1)

                def fill(name):
                    for _ in range(FILL[name]):
                        expert_unit(at[0])
                        at[0] += 1

                def transposes(b, src, done, w=P):
                    for t in range(NT):
                        last = nc.tensor.transpose(ps[0:w, b, t * P:(t + 1) * P], src[:, t * w:(t + 1) * w], ident)
                    last.then_inc(done, 1)

                pe.wait_ge(xn_ready, n)
                transposes(C0, xn, xT_ps)
                pe.wait_ge(xnT_ready, n)
                for c, b, w in (("v", C4, "wv"), ("q", C2, "wq"), ("k", C3, "wk")):
                    mm(bank(b), weight(w), xnT[:, :], start=True, stop=True).then_inc(proj[c], 1)
                for t in range(NT):
                    last = mm(ps[:, C1, t * (E + H):(t + 1) * (E + H)], tile(xnT, t), wrb_sb[:, :], start=True, stop=True)
                last.then_inc(rb_ps, 1)
                fill("proj")
                for c, b, src in (("v", C4, vs), ("q", C2, qs), ("k", C3, ks)):
                    pe.wait_ge(silu[c], n)
                    transposes(b, src, tok_ps[c])
                fill("tok")
                for c, b, src, ready in (("q", C2, qtok, qn_ready), ("k", C3, ktok, kn_ready), ("b", C4, kb, kb_ready)):
                    pe.wait_ge(ready, n)
                    transposes(b, src, nT_ps[c])
                fill("norm")
                for c in "qkb":
                    pe.wait_ge(nT[c], n)
                for h in range(H):
                    r = slice(DH * h, DH * h + DH)
                    for t in range(NT):
                        last = mm(tile(bank(C0 + h), t), tile(knT, t)[r, :], tile(kbT, t)[r, :], start=True, stop=True)
                last.then_inc(l_ps, 1)
                fill("L")
                pe.wait_ge(lt_ready, n)
                for h in range(H):
                    r = slice(DH * h, DH * h + DH)
                    for t in range(NT):
                        last = mm(tile(bank(C0 + h), t), tile(knT, t)[r, :], tile(qnT, t)[r, :], start=True, stop=True)
                last.then_inc(a_ps, 1)
                fill("A")
                for a in range(HT):
                    last = mm(ps[:, C4, a * CH:(a + 1) * CH], LT[:, a, :], con("eye"), start=True, stop=True)
                last.then_inc(y_ps, 1)
                pe.wait_ge(at_ready, n)
                for l in range(1, LEVELS):
                    fill(f"lv{l}a")
                    pe.wait_ge(xi_ready, i * LEVELS + l)
                    for a in range(HT):
                        last = mm(ps[:, C4, a * CH:(a + 1) * CH], LT[:, a, :], Xi[:, a * CH:(a + 1) * CH], start=True, stop=True)
                    last.then_inc(y_ps, 1)
                    fill(f"lv{l}b")
                    pe.wait_ge(y_ready, i * (LEVELS - 1) + l)
                    pe.wait_ge(tbd_ready, i * LEVELS + l)
                    for a in range(HT):
                        last = mm(ps[:, C3, a * CH:(a + 1) * CH], Tbd[:, a, :], Yi[:, a * CH:(a + 1) * CH], start=True, stop=True)
                    last.then_inc(z_ps, 1)
                fill("inv")
                pe.wait_ge(tbd_ready, i * LEVELS + LEVELS)
                pe.wait_ge(vb_ready, n)
                for h in range(H):
                    for t in range(NT):
                        c = slice(t * P + DH * h, t * P + DH * h + DH)
                        last = mm(ps[:, C2, c], Tbd[:, h * NT + t, :], vb[:, c], start=True, stop=True)
                last.then_inc(u_ps, 1)
                for h in range(H):
                    for t in range(NT):
                        c = slice(t * P + DH * h, t * P + DH * h + DH)
                        last = mm(ps[DH * h:DH * h + DH, C1, t * P:(t + 1) * P], kb[:, c], Tbd[:, h * NT + t, :], start=True, stop=True)
                last.then_inc(wt_ps, 1)
                fill("uw")
                pe.wait_ge(u_ready, n)
                pe.wait_ge(wt_ready, n)
                for c in range(NCH):
                    t, g = divmod(c, NT)
                    r = slice(CH * g, CH * g + CH)
                    if c == 0:
                        pe.wait_ge(s0_ready, n)
                    else:
                        pe.wait_ge(s_ready, i * (NCH - 1) + c)
                    mm(ps[r, C0, t * P:(t + 1) * P], WT[:, c * CH:(c + 1) * CH], Sbd[:, :], start=True, stop=True).then_inc(ws_ps, 1)
                    mm(ps[r, C2, t * P:(t + 1) * P], qnT[:, c * CH:(c + 1) * CH], Sbd[:, :], start=True, stop=True)
                    fill(f"sc{c}a")
                    if c < NCH - 1:
                        pe.wait_ge(uadj_ready, i * NCH + c + 1)
                        mm(ps[:, C3, 0:P], tile(ktok, t)[r, :], tile(uadj, t)[r, :], start=(c == 0), stop=True, skip_group_check=True).then_inc(s_ps, 1)
                    fill(f"sc{c}b")
                pe.wait_ge(uadj_ready, i * NCH + NCH)
                for h in range(H):
                    for t in range(NT):
                        c = slice(t * P + DH * h, t * P + DH * h + DH)
                        last = mm(ps[:, C4, c], AT[:, h * NT + t, :], uadj[:, c], start=True, stop=True)
                last.then_inc(au_ps, 1)
                fill("au")
                pe.wait_ge(fs_ready, n)
                transposes(C0, fs, fsT_ps)
                pe.wait_ge(fl_ready, n)
                transposes(C1, fl, flT_ps)
                fill("fir")
                pe.wait_ge(stats_ready, n)
                HB = (C0, C1, C3, C4)
                for b in HB:
                    mm(bank(b), weight("w1x"), xnT[:, :], start=True, stop=False)
                transposes(C2, stats[:, :, :, :, :].rearrange("p t j s h -> p (t j s h)"), stT_ps, w=NST * H)
                fill("st")
                pe.wait_ge(stT_ready, n)
                for h, b in enumerate(HB):
                    mm(bank(b), w1s_sb[:, h, :], statsT[:, :], start=False, stop=True).then_inc(hid_ps, 1)
                fill("hid")
                pe.wait_ge(hdn_ready, i * H + H)
                for h in range(H):
                    for t in range(NT):
                        a = (t * H + h) * 4
                        last = mm(ps[:, C2, a:a + 4], tile(hdn[h], t), col("w2T", 0, 4), start=True, stop=True)
                last.then_inc(lgt_ps, 1)
                pe.wait_ge(o_ready, n)
                transposes(C0, o, oT_ps)
                pe.wait_ge(oT_ready, n)
                for t in range(NT):
                    last = mm(tile(bank(C1), t), tile(oT, t), weight("wo"), start=True, stop=True)
                last.then_inc(sp_ps, 1)

                pe.wait_ge(xn1_ready, n)
                transposes(C0, xn1, x1T_ps)
                pe.wait_ge(x1T_ready, n)
                x1T = xn1p[:, 4:4 + L]
                FB = [(G, Ub), (Db, C1), (C2, C3), (C4, C0)]
                for c in range(FF):
                    mm(bank(FB[c][0]), f1_sb[:, c, :], x1T, start=True, stop=True).then_inc(ffg_ps, 1)
                    mm(bank(FB[c][1]), f2_sb[:, c, :], x1T, start=True, stop=True).then_inc(ffu_ps, 1)
                for j, (w, b) in enumerate((("Wr", G), ("Ww", Ub), ("Wk", Db), ("Wv", C1), ("Wa", C2), ("Wg", C3))):
                    if j % 2 == 0:
                        pe.wait_ge(fh_ready, i * FF + j // 2 + 1)
                    pe.wait_ge(mix_ready, i * 6 + j + 1)
                    mm(bank(b), weight(w), mixd[j][:, :], start=True, stop=True).then_inc(pj_ps, 1)

                def hidden(w_sb, src, done, used, ready, outs):
                    pe.wait_ge(ready, i * FF + FF)
                    for c in outs:
                        b = (C4, C0)[c % 2]
                        if c >= 2:
                            pe.wait_ge(used, i * FF + c - 1)
                        for k in range(FF):
                            last = mm(bank(b), w_sb[:, k, c * P:(c + 1) * P], src[k], start=(k == 0), stop=(k == FF - 1))
                        last.then_inc(done, 1)

                hidden(h1_sb, fh, h1_ps, g1_ready, fh_ready, range(FF))
                pe.wait_ge(mixed_ready, n)
                mm(bank(G), con("avg"), mixed[:, :], start=True, stop=True).then_inc(mu_ps, 1)
                hidden(h2_sb, g1, h2_ps, g2_ready, g1_ready, (0, 1))
                pe.wait_ge(sqc_ready, n)
                mm(bank(Ub), con("avg"), sqc[:, :], start=True, stop=True).then_inc(var_ps, 1)
                hidden(h2_sb, g1, h2_ps, g2_ready, g1_ready, (2, 3))
                pe.wait_ge(g2_ready, i * FF + FF)
                for t in range(NT):
                    for k in range(FF):
                        last = mm(tile(bank(C1), t), g2[k][:, t * P:(t + 1) * P], w3_sb[:, k, :], start=(k == 0), stop=(k == FF - 1))
                last.then_inc(w3_ps, 1)
                pe.wait_ge(mg_ready, n)
                for t in range(NT):
                    last = mm(tile(bank(Db), t), tile(mg, t), weight("Wout"), start=True, stop=True)
                last.then_inc(op_ps, 1)

        @block.scalar
        def _(act):
            f = nc.scalar.activation
            act.wait_ge(s_w, 16 * 5)
            f(tmp1[:, 0:1], col("temp"), ACT.Abs).then_inc(pre_act, 1)
            act.wait_ge(pre_act, 1)
            f(tmp1[:, 1:2], tmp1[:, 0:1], ACT.Exp, scale=-1.0).then_inc(pre_act, 1)
            act.wait_ge(pre_act, 2)
            f(tmp1[:, 2:3], tmp1[:, 1:2], ACT.Ln, bias=1.0).then_inc(pre_act, 1)
            f(tmp1[:, 3:4], col("temp"), ACT.Relu).then_inc(pre_act, 1)
            with act.Fori(0, B) as i:
                n = act.snap(i + 1)
                ie = act.snap(i * EA)
                iq = act.snap(i * (EA // 2))
                at = [0]

                def expert_unit(k):
                    e, kind = divmod(k, 3)
                    if kind == 0 and e < EA:
                        act.wait_ge(g_ps, ie + e + 1)
                        f(sg[e % 2][:, :], bank(G), ACT.Silu).then_inc(sg_ready, 1)
                    elif kind == 2 and e > 0 or k == UNITS - 1:
                        d = e - 1
                        if on_vector(d):
                            return
                        if d == 1:
                            act.wait_ge(wsc_ready, n)
                        act.wait_ge(d_ps, ie + d + 1)
                        if d >= 3:
                            act.wait_ge(pacc, iq + d // 2)
                        for t in range(NT):
                            s = wsc[:, t, d:d + 1] if d < E else 1.0
                            last = f(tile(dt, t), tile(bank(Db), t), ACT.Copy, scale=s)
                        last.then_inc(dt_ready, 1)

                def fill(name):
                    for _ in range(FILL[name]):
                        expert_unit(at[0])
                        at[0] += 1

                def copy(dst, b, src_ready, done):
                    act.wait_ge(src_ready, n)
                    f(dst[:, 0:L], bank(b), ACT.Copy).then_inc(done, 1)

                act.wait_ge(vr0_ready, n)
                f(rstd[:, :], vr[:, :], ACT.Sqrt).then_inc(rstd0_ready, 1)
                copy(xnT, C0, xT_ps, xnT_ready)
                for c, b, w, y in (("v", C4, "vc", yv), ("q", C2, "qc", yq), ("k", C3, "kc", yk)):
                    act.wait_ge(proj[c], n)
                    f(y[:, :], bank(b), ACT.Copy, scale=col(w, KC - 1)).then_inc(tap[c], 1)
                act.wait_ge(lgs_ready, n)
                f(sc[:, :, 0:E], lg[:, :, :], ACT.Exp).then_inc(ex_ready, 1)
                f(beta[:, :, :], ps[:, C1, 0:NT * (E + H)].rearrange("p (t c) -> p t c", t=NT)[:, :, E:E + H], ACT.Sigmoid).then_inc(beta_ready, 1)
                fill("proj")
                for c, y, dst in (("v", yv, vs), ("q", yq, qs), ("k", yk, ks)):
                    act.wait_ge(conv[c], n)
                    f(dst[:, :], y[:, :], ACT.Silu).then_inc(silu[c], 1)
                act.wait_ge(silu["v"], n)
                f(fs[:, :], vs[:, :], ACT.Copy, scale=col("fs", KS - 1)).then_inc(fir0, 1)
                f(fl[:, :], vs[:, :], ACT.Copy, scale=col("fl", KL - 1)).then_inc(fir0, 1)
                for c, b, dst in (("v", C4, vtok), ("q", C2, qtok), ("k", C3, ktok)):
                    copy(dst, b, tok_ps[c], tok[c])
                fill("tok")
                act.wait_ge(ssr_ready, n)
                f(rn[:, :, :], ssr[:, :, :], ACT.Sqrt).then_inc(rn_ready, 1)
                for c, b, dst in (("q", C2, qnT), ("k", C3, knT), ("b", C4, kbT)):
                    copy(dst, b, nT_ps[c], nT[c])
                fill("norm")
                fill("L")
                fill("A")
                for l in range(1, LEVELS):
                    fill(f"lv{l}a")
                    act.wait_ge(y_ps, i * LEVELS + l + 1)
                    f(Yi[:, :], bank(C4), ACT.Copy).then_inc(y_ready, 1)
                    fill(f"lv{l}b")
                fill("inv")
                copy(U, C2, u_ps, u_ready)
                copy(WT, C1, wt_ps, wt_ready)
                fill("uw")
                for c in range(NCH):
                    fill(f"sc{c}a")
                    fill(f"sc{c}b")
                act.wait_ge(au_ps, n)
                f(dq[:, :], bank(C2), ACT.Copy).then_inc(dq_ready, 1)
                fill("au")
                copy(lstok, C0, fsT_ps, ls_ready)
                copy(lltok, C1, flT_ps, ll_ready)
                fill("fir")
                act.wait_ge(stq_ready, n)
                f(stats[:, :, :, 3, :].rearrange("p t j h -> p j t h"), st_q[:, :, :].rearrange("p j (t h) -> p j t h", h=H), ACT.Sqrt).then_inc(l2_ready, 1)
                act.wait_ge(stT_ps, n)
                f(statsT[:, :], ps[0:NST * H, C2, :], ACT.Copy).then_inc(stT_ready, 1)
                fill("st")
                for h, b in enumerate((C0, C1, C3, C4)):
                    act.wait_ge(hid_ps, i * H + h + 1)
                    f(hdn[h][:, :], bank(b), ACT.Gelu, bias=col("b1")).then_inc(hdn_ready, 1)
                fill("hid")
                act.wait_ge(lgx_ready, n)
                f(fe[:, :, :], lgx[:, :, :], ACT.Exp).then_inc(fe_ready, 1)
                act.wait_ge(msr_ready, n)
                f(rms[:, :], msr[:, :], ACT.Sqrt).then_inc(rms_ready, 1)
                act.wait_ge(asum_ready, n)
                f(gs[:, :], accp[:, :], ACT.Silu).then_inc(gs_ready, 1)
                copy(oT, C0, oT_ps, oT_ready)

                act.wait_ge(vr1_ready, n)
                f(rstd[:, :], vr[:, :], ACT.Sqrt).then_inc(rstd1_ready, 1)
                act.wait_ge(x1T_ps, n)
                f(xn1p[:, 4:4 + L], bank(C0), ACT.Copy).then_inc(x1T_ready, 1)
                FB = [(G, Ub), (Db, C1), (C2, C3), (C4, C0)]
                for c in range(FF):
                    act.wait_ge(ffg_ps, i * FF + c + 1)
                    f(sgf[c], bank(FB[c][0]), ACT.Silu, scale=col("s1", c)).then_inc(sgf_ready, 1)
                for j, (b, dst, fn, s) in enumerate(((G, rg, ACT.Sigmoid, 1.0), (Ub, dec, ACT.Sigmoid, -1.0), (Db, kt, ACT.Tanh, 1.0),
                                                     (C2, al, ACT.Sigmoid, 1.0), (C3, gg, ACT.Sigmoid, 1.0))):
                    act.wait_ge(pj_ps, i * 6 + (j + 1 if j < 3 else j + 2))
                    f(dst[:, :], bank(b), fn, scale=s).then_inc(pj_act, 1)
                for c in range(FF):
                    act.wait_ge(h1_ps, i * FF + c + 1)
                    f(g1[c], bank((C4, C0)[c % 2]), ACT.Gelu, scale=col("hs1", c)).then_inc(g1_ready, 1)
                act.wait_ge(cen_ready, n)
                f(sqc[:, :], cen[:, :], ACT.Square).then_inc(sqc_ready, 1)
                for c in range(FF):
                    act.wait_ge(h2_ps, i * FF + c + 1)
                    f(g2[c], bank((C4, C0)[c % 2]), ACT.Gelu, scale=col("hs2", c)).then_inc(g2_ready, 1)
                act.wait_ge(rvar_ready, n)
                f(rvar[:, :], rvar[:, :], ACT.Sqrt).then_inc(rsd_ready, 1)
                act.wait_ge(g2r_ready, n)
                f(g2s[:, :], g2r[:, :], ACT.Silu).then_inc(g2s_ready, 1)

        @block.vector
        def _(dve):
            v = nc.vector
            tt, ts, stt_ = v.tensor_tensor, v.tensor_scalar, v.scalar_tensor_tensor
            dve.wait_ge(s_w, 16 * 5)
            v.memset(sc[:, :, E:E + TOPK], -1.0)
            v.memset(m4[:, :, TOPK:8], -1.0)
            v.memset(xn1p[:, 0:4], 0.0)
            v.memset(unit[:, 0:1], 0.0).then_inc(x2_stored, 16)
            v.memset(unit[:, 1:2], 1.0).then_inc(unit_ready, 1)
            dve.wait_ge(pre_act, 4)
            tt(tmp1[:, 0:1], tmp1[:, 2:3], tmp1[:, 3:4], ALU.add).then_inc(pre_dve, 1)
            dve.wait_ge(pre_dve, 1)
            ts(tmp1[:, 1:2], tmp1[:, 0:1], 0.0001, None, ALU.add).then_inc(pre_dve, 1)
            dve.wait_ge(pre_dve, 2)
            v.reciprocal(invt[:, :], tmp1[:, 1:2]).then_inc(pre_dve, 1)
            dve.wait_ge(pre_dve, 3)
            ts(b2t[:, :], col("b2", 0, 4), invt[:, :], None, ALU.mult).then_inc(pre_dve, 1)
            dve.wait_ge(pre_dve, 4)
            with dve.Fori(0, B) as i:
                n = dve.snap(i + 1)
                ie = dve.snap(i * EA)
                iq = dve.snap(i * (EA // 2))
                il = dve.snap(i * DVE_LINKS)
                at, links = [0], [0]
                taps = [("s", j) for j in range(1, KS)] + [("l", j) for j in range(1, KL)]
                tap_at = [0]

                def link(ins):
                    links[0] += 1
                    ins.then_inc(dve_link, 1)
                    dve.wait_ge(dve_link, il + links[0])

                def expert_unit(k):
                    e, kind = divmod(k, 3)
                    if kind == 1 and e < EA:
                        dve.wait_ge(sg_ready, ie + e + 1)
                        dve.wait_ge(up_ps, ie + e + 1)
                        tt(hx[e % 2][:, :], bank(Ub), sg[e % 2][:, :], ALU.mult).then_inc(h_ready, 1)
                    elif kind == 2 and e > 0 or k == UNITS - 1:
                        d = e - 1
                        if not on_vector(d):
                            return
                        dve.wait_ge(d_ps, ie + d + 1)
                        if d:
                            dve.wait_ge(dacc, iq + d // 2)
                        for t in range(NT):
                            s = wsc[:, t, d:d + 1] if d < E else 1.0
                            if d == 0:
                                last = ts(tile(acc, t), tile(bank(Db), t), s, None, ALU.mult)
                            else:
                                last = stt_(tile(acc, t), tile(bank(Db), t), s, tile(acc, t), ALU.mult, ALU.add)
                        last.then_inc(dacc, 1)

                def fir(m):
                    for _ in range(m):
                        if tap_at[0] == len(taps):
                            return
                        kind, lag = taps[tap_at[0]]
                        y, w, last_tap, done = (fs, "fs", KS - 1, fs_ready) if kind == "s" else (fl, "fl", KL - 1, fl_ready)
                        if tap_at[0] == 0:
                            dve.wait_ge(fir0, i * 2 + 2)
                        tap_at[0] += 1
                        ins = stt_(y[:, lag:L], vs[:, 0:L - lag], col(w, last_tap - lag), y[:, lag:L], ALU.mult, ALU.add)
                        if lag == last_tap:
                            ins.then_inc(done, 1)
                        else:
                            link(ins)

                def fill(name, taps_per_unit=0.0):
                    for u in range(FILL[name]):
                        expert_unit(at[0])
                        at[0] += 1
                        fir(int((u + 1) * taps_per_unit) - int(u * taps_per_unit))

                def layernorm(src, dst, vr_ready, rstd_ready, done):
                    for t in range(NT):
                        last = v.bn_stats(bst[:, t, :], tile(src, t))
                    link(last)
                    v.memset(spare[:, 0:1], 0.0)
                    for t in range(NT):
                        last = v.bn_aggr(mv[:, t, :], bst[:, t, :])
                    link(last)
                    link(ts(vr[:, :], mv[:, :, 1], LN_EPS, None, ALU.add))
                    v.reciprocal(vr[:, :], vr[:, :]).then_inc(vr_ready, 1)
                    dve.wait_ge(rstd_ready, n)
                    for t in range(NT):
                        last = ts(tile(dst, t), tile(src, t), mv[:, t, 0:1], rstd[:, t:t + 1], ALU.subtract, ALU.mult)
                    last.then_inc(done, 1)

                def over(ap, shape):
                    return ap.unsqueeze(2).to_broadcast(shape)

                dve.wait_ge(x_loaded, 16 * n)
                layernorm(xt, xn, vr0_ready, rstd0_ready, xn_ready)
                dve.wait_ge(rb_ps, n)
                lgp = ps[:, C1, 0:NT * (E + H)].rearrange("p (t c) -> p t c", t=NT)[:, :, 0:E]
                link(tt(lg[:, :, :], lgp, col("rbias", 0, E).unsqueeze(1).to_broadcast([P, NT, E]), ALU.add))
                link(v.tensor_reduce(mx[:, :], lg[:, :, :], X, ALU.max))
                tt(lg[:, :, :], lg[:, :, :], over(mx[:, :], [P, NT, E]), ALU.subtract).then_inc(lgs_ready, 1)
                for c, b, w, y in (("v", C4, "vc", yv), ("q", C2, "qc", yq), ("k", C3, "kc", yk)):
                    dve.wait_ge(tap[c], n)
                    for lag in range(1, KC):
                        ins = stt_(y[:, lag:L], ps[:, b, 0:L - lag], col(w, KC - 1 - lag), y[:, lag:L], ALU.mult, ALU.add)
                        if lag < KC - 1:
                            link(ins)
                    ins.then_inc(conv[c], 1)
                dve.wait_ge(ex_ready, n)
                link(v.tensor_reduce(ssum[:, :], sc[:, :, 0:E], X, ALU.add))
                link(v.reciprocal(ssum[:, :], ssum[:, :]))
                link(tt(sc[:, :, 0:E], sc[:, :, 0:E], over(ssum[:, :], [P, NT, E]), ALU.mult))
                v.memset(spare[:, 1:2], 0.0)
                for t in range(NT):
                    last = v.max(m8[:, t, :], sc[:, t, 0:E])
                link(last)
                v.tensor_copy(m4[:, :, 0:TOPK], m8[:, :, 0:TOPK])
                link(v.tensor_reduce(mx[:, :], m8[:, :, 0:TOPK], X, ALU.add))
                link(ts(mx[:, :], mx[:, :], 1e-12, None, ALU.max))
                v.reciprocal(mx[:, :], mx[:, :])
                for t in range(NT):
                    last = v.match_replace(rep[:, t, :], m4[:, t, :], sc[:, t, :], -2.0)
                link(last)
                link(tt(rep[:, :, 0:E], rep[:, :, 0:E], sc[:, :, 0:E], ALU.not_equal))
                link(tt(wsc[:, :, :], rep[:, :, 0:E], sc[:, :, 0:E], ALU.mult))
                tt(wsc[:, :, :], wsc[:, :, :], over(mx[:, :], [P, NT, E]), ALU.mult).then_inc(wsc_ready, 1)
                dve.wait_ge(wsc_ready, n)
                fill("proj")
                for j, c in enumerate("qk"):
                    dve.wait_ge(sq_ready[c], n)
                    last = v.tensor_reduce(ss[:, j, :], byhead(sq4[1 + j][:, :]), X, ALU.add)
                link(last)
                v.reciprocal(ssr[:, :, :], ss[:, :, :]).then_inc(ssr_ready, 1)
                fill("tok", 0.5)
                dve.wait_ge(rn_ready, n)
                for j, (buf, done) in enumerate(((qtok, qn_ready), (ktok, kn_ready))):
                    tt(byhead(buf[:, :]), byhead(buf[:, :]), over(rn[:, j, :], [P, HT, DH]), ALU.mult).then_inc(done, 1)
                fill("norm", 0.7)
                dve.wait_ge(l_ps, n)
                for h in range(H):
                    last = tt(LT[:, h * NT:(h + 1) * NT, :], bank(C0 + h).rearrange("p (t s) -> p t s", t=NT),
                              con("strict").unsqueeze(1).to_broadcast([P, NT, P]), ALU.mult)
                last.then_inc(lt_ready, 1)
                fill("L", 0.7)
                dve.wait_ge(a_ps, n)
                for h in range(H):
                    last = tt(AT[:, h * NT:(h + 1) * NT, :], bank(C0 + h).rearrange("p (t s) -> p t s", t=NT),
                              con("causal").unsqueeze(1).to_broadcast([P, NT, P]), ALU.mult)
                last.then_inc(at_ready, 1)
                fill("A", 0.7)
                chunks = "p (a j) -> p a j"

                def masked(b, l):
                    a = CONS["lvl"][0] + l * CH
                    link(tt(Zm[:, :].rearrange(chunks, j=CH), bank(b).rearrange(chunks, j=CH),
                            cn[:, a:a + CH].unsqueeze(1).to_broadcast([P, HT, CH]), ALU.mult))

                dve.wait_ge(y_ps, i * LEVELS + 1)
                masked(C4, 0)
                tt(Xi[:, :].rearrange(chunks, j=CH), con("eye").unsqueeze(1).to_broadcast([P, HT, CH]),
                   Zm[:, :].rearrange(chunks, j=CH), ALU.subtract).then_inc(xi_ready, 1)
                for l in range(1, LEVELS):
                    dve.wait_ge(xi_ready, i * LEVELS + l)
                    v.transpose(Ti[:, :], Xi[:, :]).then_inc(ti_ready, 1)
                    fill(f"lv{l}a", 0.7)
                    fill(f"lv{l}b", 0.7)
                    dve.wait_ge(z_ps, i * (LEVELS - 1) + l)
                    masked(C3, l)
                    tt(Xi[:, :], Xi[:, :], Zm[:, :], ALU.subtract).then_inc(xi_ready, 1)
                dve.wait_ge(xi_ready, i * LEVELS + LEVELS)
                v.transpose(Ti[:, :], Xi[:, :]).then_inc(ti_ready, 1)
                fill("inv", 0.7)
                fill("uw", 0.7)
                dve.wait_ge(u_ready, n)
                for c in range(NCH):
                    t, g = divmod(c, NT)
                    r = slice(CH * g, CH * g + CH)
                    dve.wait_ge(ws_ps, i * NCH + c + 1)
                    tt(tile(uadj, t)[r, :], tile(U, t)[r, :], ps[r, C0, t * P:(t + 1) * P], ALU.subtract).then_inc(uadj_ready, 1)
                    fill(f"sc{c}a", 1.0)
                    if c < NCH - 1:
                        dve.wait_ge(s_ps, i * (NCH - 1) + c + 1)
                        tt(Sbd[:, :], ps[:, C3, 0:P], con("bd"), ALU.mult).then_inc(s_ready, 1)
                    fill(f"sc{c}b", 1.0)
                fir(len(taps))
                dve.wait_ge(dq_ready, n)
                tt(dl[:, :], bank(C4), dq[:, :], ALU.add).then_inc(dl_ready, 1)
                fill("au")
                dve.wait_ge(dl_ready, n)
                srcs = (lstok, lltok, dl, vtok)
                for j in (3, 2, 0, 1):
                    if j < 2:
                        dve.wait_ge((ls_ready, ll_ready)[j], n)
                    v.tensor_reduce(st_s[:, j, :], byhead(srcs[j][:, :]), X, ALU.add)
                    v.tensor_reduce(st_a[:, j, :], byhead(srcs[j][:, :]), X, ALU.add, apply_absolute_value=True)
                    dve.wait_ge(sq4_ready, i * 4 + (3, 2, 0, 1).index(j) + 1)
                    last = v.tensor_reduce(st_q[:, j, :], byhead(sq4[j][:, :]), X, ALU.add)
                last.then_inc(stq_ready, 1)
                dve.wait_ge(stq_ready, n)
                link(ts(mean_c[:, :, :], st_s[:, :, :], 1.0 / DH, None, ALU.mult))
                link(tt(m2_c[:, :, :], mean_c[:, :, :], mean_c[:, :, :], ALU.mult))
                stt_(var_c[:, :, :], st_q[:, :, :], 1.0 / DH, m2_c[:, :, :], ALU.mult, ALU.subtract).then_inc(mvar_ready, 1)
                fill("fir")
                fill("st")
                fill("hid")
                dve.wait_ge(lgt_ps, n)
                link(stt_(lgx[:, :, :], ps[:, C2, 0:HT * 4].rearrange("p (a k) -> p a k", k=4), invt[:, :],
                          b2t[:, :].unsqueeze(1).to_broadcast([P, HT, 4]), ALU.mult, ALU.add))
                link(v.tensor_reduce(lmx[:, :], lgx[:, :, :], X, ALU.max))
                tt(lgx[:, :, :], lgx[:, :, :], over(lmx[:, :], [P, HT, 4]), ALU.subtract).then_inc(lgx_ready, 1)
                dve.wait_ge(fe_ready, n)
                link(v.tensor_reduce(fsum[:, :], fe[:, :, :], X, ALU.add))
                link(v.reciprocal(fsum[:, :], fsum[:, :]))
                link(tt(fw[:, :, :], fe[:, :, :], over(fsum[:, :], [P, HT, 4]), ALU.mult))
                ts(fw[:, :, 0], fw[:, :, 0], col("rss"), None, ALU.add)
                ts(fw[:, :, 1], fw[:, :, 1], col("rsl"), None, ALU.add).then_inc(fw_ready, 1)
                dve.wait_ge(fw_ready, n)
                for j in (0, 1):
                    last = tt(byhead(pr[j][:, :]), byhead(srcs[j][:, :]), over(fw[:, :, j], [P, HT, DH]), ALU.mult)
                link(last)
                link(tt(o[:, :], pr[0][:, :], pr[1][:, :], ALU.add))
                dve.wait_ge(p23_ready, n)
                tt(o[:, :], o[:, :], pr[2][:, :], ALU.add).then_inc(o_sum, 1)
                dve.wait_ge(osq_ready, n)
                link(v.tensor_reduce(ms[:, :], byhead(osq[:, :]), X, ALU.add))
                link(ts(ms[:, :], ms[:, :], 1.0 / DH, RMS_EPS, ALU.mult, ALU.add))
                v.reciprocal(msr[:, :], ms[:, :]).then_inc(msr_ready, 1)
                dve.wait_ge(rms_ready, n)
                tt(byhead(o[:, :]), byhead(o[:, :]), over(rms[:, :], [P, HT, DH]), ALU.mult).then_inc(on_ready, 1)
                dve.wait_ge(sp_ps, n)
                dve.wait_ge(gs_ready, n)
                link(tt(x1[:, :], bank(C1), gs[:, :], ALU.mult))
                tt(x1[:, :], x1[:, :], xt[:, :], ALU.add).then_inc(x_free, 1)
                dve.wait_ge(x_free, n)

                layernorm(x1, xn1, vr1_ready, rstd1_ready, xn1_ready)
                dve.wait_ge(x1T_ready, n)
                link(tt(dT[:, :], xn1p[:, 3:3 + L], xn1p[:, 4:4 + L], ALU.subtract))
                FB = [(G, Ub), (Db, C1), (C2, C3), (C4, C0)]

                def ffn_up(c):
                    dve.wait_ge(sgf_ready, i * FF + c + 1)
                    dve.wait_ge(ffu_ps, i * FF + c + 1)
                    stt_(fh[c], bank(FB[c][1]), col("s2", c), sgf[c], ALU.mult, ALU.mult).then_inc(fh_ready, 1)

                for j in range(6):
                    stt_(mixd[j][:, :], dT[:, :], col("mix", j), xn1p[:, 4:4 + L], ALU.mult, ALU.add).then_inc(mix_ready, 1)
                    if j >= 2:
                        ffn_up(j - 2)
                dve.wait_ge(ak_ready, n)
                dve.wait_ge(pj_ps, i * 6 + 4)
                link(tt(uu[:, :], bank(C1), ak[:, :], ALU.mult))
                v.tensor_tensor_scan(stt[:, :], dec[:, :], uu[:, :], 0.0, ALU.mult, ALU.add).then_inc(st_ready, 1)
                dve.wait_ge(mu_ps, n)
                tt(cen[:, :], mixed[:, :], bank(G), ALU.subtract).then_inc(cen_ready, 1)
                dve.wait_ge(var_ps, n)
                link(ts(rvar[:, :], bank(Ub), GN_EPS, None, ALU.add))
                v.reciprocal(rvar[:, :], rvar[:, :]).then_inc(rvar_ready, 1)
                dve.wait_ge(rsd_ready, n)
                link(tt(mn[:, :], cen[:, :], rvar[:, :], ALU.mult))
                ts(mn[:, :], mn[:, :], col("gnw"), col("gnb"), ALU.mult, ALU.add).then_inc(mn_ready, 1)
                dve.wait_ge(w3_ps, n)
                rows = "p (t d) -> p t d"
                tt(g2r[:, :].rearrange(rows, d=D), bank(C1).rearrange(rows, d=D),
                   col("w3s", 0, D).unsqueeze(1).to_broadcast([P, NT, D]), ALU.mult).then_inc(g2r_ready, 1)
                dve.wait_ge(op_ps, n)
                link(tt(s1[:, :].rearrange(rows, d=D), bank(Db).rearrange(rows, d=D),
                        col("bout", 0, D).unsqueeze(1).to_broadcast([P, NT, D]), ALU.add))
                dve.wait_ge(g2s_ready, n)
                link(tt(s1[:, :], s1[:, :], g2s[:, :], ALU.mult))
                dve.wait_ge(x2_stored, 16 * n)
                tt(x2[:, :], x1[:, :], s1[:, :], ALU.add).then_inc(x2_ready, 1)
                dve.wait_ge(x2_ready, n)
                assert links[0] <= DVE_LINKS, links[0]
                dve.engine_nop().then_inc(dve_link, DVE_LINKS - links[0])

        @block.gpsimd
        def _(pool):
            g = nc.gpsimd
            tt = g.tensor_tensor
            pool.wait_ge(s_w, 16 * 5)
            pool.wait_ge(unit_ready, 1)
            with pool.Fori(0, B) as i:
                n = pool.snap(i + 1)
                iq = pool.snap(i * (EA // 2))
                at = [0]

                def expert_unit(k):
                    e, kind = divmod(k, 3)
                    if kind == 2 and e > 0 or k == UNITS - 1:
                        d = e - 1
                        if on_vector(d):
                            return
                        pool.wait_ge(dt_ready, iq + d // 2 + 1)
                        if d == 1:
                            tt(accp[:, :], dt[:, :], unit[:, 0:1].to_broadcast([P, L]), ALU.add).then_inc(pacc, 1)
                        else:
                            pool.wait_ge(pacc, iq + d // 2)
                            tt(accp[:, :], accp[:, :], dt[:, :], ALU.add).then_inc(pacc, 1)

                def fill(name):
                    for _ in range(FILL[name]):
                        expert_unit(at[0])
                        at[0] += 1

                def per_head(dst, src, scale, done):
                    tt(byhead(dst[:, :]), byhead(src[:, :]), scale.unsqueeze(2).to_broadcast([P, HT, DH]), ALU.mult).then_inc(done, 1)

                betas = beta[:, :, :].rearrange("p t h -> p (t h)")
                fill("proj")
                for j, c, src in ((1, "q", qtok), (2, "k", ktok)):
                    pool.wait_ge(tok[c], n)
                    tt(sq4[j][:, :], src[:, :], src[:, :], ALU.mult).then_inc(sq_ready[c], 1)
                pool.wait_ge(beta_ready, n)
                pool.wait_ge(tok["v"], n)
                per_head(vb, vtok, betas, vb_ready)
                fill("tok")
                pool.wait_ge(kn_ready, n)
                per_head(kb, ktok, betas, kb_ready)
                g.memset(Sbd[:, :], 0.0).then_inc(s0_ready, 1)
                fill("norm")
                fill("L")
                fill("A")

                def expand(l):
                    pool.wait_ge(ti_ready, i * LEVELS + l)
                    tt(Tbd[:, :, :].rearrange("p a (c j) -> p a c j", j=CH),
                       Ti[:, :].rearrange("p (a j) -> p a j", j=CH).unsqueeze(2).to_broadcast([P, HT, P // CH, CH]),
                       con("bd").rearrange("p (c j) -> p c j", j=CH).unsqueeze(1).to_broadcast([P, HT, P // CH, CH]), ALU.mult).then_inc(tbd_ready, 1)

                for l in range(1, LEVELS):
                    expand(l)
                    fill(f"lv{l}a")
                    fill(f"lv{l}b")
                expand(LEVELS)
                fill("inv")
                fill("uw")
                for c in range(NCH):
                    fill(f"sc{c}a")
                    fill(f"sc{c}b")
                for j, src, ready in ((3, vtok, None), (2, dl, dl_ready), (0, lstok, ls_ready), (1, lltok, ll_ready)):
                    if ready is not None:
                        pool.wait_ge(ready, n)
                    tt(sq4[j][:, :], src[:, :], src[:, :], ALU.mult).then_inc(sq4_ready, 1)
                    if j == 2:
                        fill("au")
                pool.wait_ge(mvar_ready, n)
                pool.wait_ge(l2_ready, n)
                four = "p j (t h) -> p j t h"
                for t in range(NT):
                    for s, src in ((0, mean_c), (1, var_c)):
                        tt(stats[:, t, :, s, :], src[:, :, t * H:(t + 1) * H], unit[:, 1:2].unsqueeze(2).to_broadcast([P, 4, H]), ALU.mult)
                g.tensor_scalar(stats[:, :, :, 2, :].rearrange("p t j h -> p j t h"), st_a[:, :, :].rearrange(four, h=H),
                                1.0 / DH, None, ALU.mult).then_inc(stats_ready, 1)
                fill("fir")
                fill("st")
                fill("hid")
                pool.wait_ge(dacc, iq + EA // 2)
                pool.wait_ge(pacc, iq + EA // 2)
                tt(accp[:, :], accp[:, :], acc[:, :], ALU.add).then_inc(asum_ready, 1)
                pool.wait_ge(fw_ready, n)
                for j, src in ((2, dl), (3, vtok)):
                    last = tt(byhead(pr[j][:, :]), byhead(src[:, :]), fw[:, :, j].unsqueeze(2).to_broadcast([P, HT, DH]), ALU.mult)
                last.then_inc(pre_pool, 1)
                pool.wait_ge(pre_pool, i * 1 + 1)
                tt(pr[2][:, :], pr[2][:, :], pr[3][:, :], ALU.add).then_inc(p23_ready, 1)
                pool.wait_ge(o_sum, n)
                tt(osq[:, :], o[:, :], o[:, :], ALU.mult).then_inc(osq_ready, 1)
                pool.wait_ge(on_ready, n)
                tt(byhead(o[:, :]), byhead(o[:, :]), col("onorm", 0, DH).unsqueeze(1).to_broadcast([P, HT, DH]), ALU.mult).then_inc(o_ready, 1)

                pool.wait_ge(pj_act, i * 5 + 4)
                tt(ak[:, :], al[:, :], kt[:, :], ALU.mult).then_inc(ak_ready, 1)
                pool.wait_ge(st_ready, n)
                tt(mixed[:, :], rg[:, :], stt[:, :], ALU.mult).then_inc(mixed_ready, 1)
                pool.wait_ge(mn_ready, n)
                pool.wait_ge(pj_act, i * 5 + 5)
                tt(mg[:, :], mn[:, :], gg[:, :], ALU.mult).then_inc(mg_ready, 1)


def constants():
    p = np.arange(P)
    same = p[:, None] // CH == p[None, :] // CH
    c = np.zeros((P, NCON), np.float32)

    def put(name, a):
        c[:, CONS[name][0]:CONS[name][1]] = a

    put("ident", np.eye(P))
    put("bd", same)
    put("avg", (p[:, None] // 8 == p[None, :] // 8) / 8.0)
    put("strict", same & (p[:, None] < p[None, :]))
    put("causal", same & (p[:, None] <= p[None, :]))
    r, j = p[:, None] % CH, np.arange(CH)[None, :]
    put("eye", r == j)
    put("lvl", np.concatenate([(r // (2 * s) == j // (2 * s)) & (r // s % 2 == 1) & (j // s % 2 == 0)
                               for s in (1 << l for l in range(LEVELS))], axis=1))
    return c


def kernel(**inputs):
    import concourse.bacc as _bacc
    from concourse.bass_utils import run_bass_kernel_spmd as _run

    a = {k: np.asarray(v) for k, v in inputs.items()}
    l0, ff0, l1, ff1 = (lambda k, p=p: a[p + k] for p in ("L0_attn_", "L0_ffn_", "L1_attn_", "L1_ffn_"))

    def rows(vec, n=P):
        return np.broadcast_to(vec.reshape(1, -1), (n, vec.size))

    small = np.zeros((P, NCOL), np.float32)
    for name, val in (("qc", l0("q_conv_w")), ("kc", l0("k_conv_w")), ("vc", l0("v_conv_w")), ("fs", l0("fir_short_w").reshape(D, KS)),
                      ("fl", l0("fir_long_w").reshape(D, KL)), ("b1", l0("fuse_b1").reshape(P, 1)),
                      ("mix", np.stack([l1(f"x_{c}").reshape(D) for c in "rwkvag"], axis=1)),
                      ("gnw", l1("gn_w").reshape(D, 1)), ("gnb", l1("gn_b").reshape(D, 1)),
                      ("s1", ff1("w1_s").reshape(FF, P).T), ("s2", ff1("w2_s").reshape(FF, P).T),
                      ("hs1", ff1("h1_s").reshape(FF, P).T), ("hs2", ff1("h2_s").reshape(FF, P).T),
                      ("temp", rows(l0("logit_temp"))), ("rss", rows(l0("res_scale_short"))), ("rsl", rows(l0("res_scale_long"))),
                      ("b2", rows(l0("fuse_b2"))), ("onorm", rows(l0("o_norm_w"))), ("rbias", rows(ff0("router_bias"))),
                      ("bout", rows(l1("b_out"))), ("w3s", rows(ff1("w3_s"))), ("w2T", l0("fuse_w2").T)):
        small[:, COLS[name][0]:COLS[name][1]] = val
    w1 = l0("fuse_w1")
    w1s = np.zeros((NST, H, H, P), np.float32)
    for h in range(H):
        w1s[:, h, h, :] = w1[:, D:].T
    arrays = {
        "x": l0("hidden_states"),
        "small": small,
        "cons": constants(),
        "wsq": np.stack([l0("q_proj_w").T, l0("k_proj_w").T, l0("v_proj_w").T, w1[:, :D].T, l0("o_proj_w").T]
                        + [l1(f"W_{c}").T for c in ("r", "w", "k", "v", "a", "g", "out")], axis=1),
        "wrb": np.concatenate([ff0("router_w").T, l0("b_proj_w").T], axis=1),
        "w1s": w1s.reshape(NST * H, H, P),
        "moe_g": np.concatenate([ff0("gate_w").transpose(2, 0, 1), ff0("sgate_w").T.reshape(D, ES, P)], axis=1),
        "moe_u": np.concatenate([ff0("up_w").transpose(2, 0, 1), ff0("sup_w").T.reshape(D, ES, P)], axis=1),
        "moe_d": np.concatenate([ff0("down_w").transpose(2, 0, 1), ff0("sdown_w").T.reshape(ES, P, D).transpose(1, 0, 2)], axis=1),
        "f1": ff1("w1_w").T.reshape(D, FF, P),
        "f2": ff1("w2_w").T.reshape(D, FF, P),
        "h1w": ff1("h1_w").T.reshape(FF, P, FF * P).transpose(1, 0, 2),
        "h2w": ff1("h2_w").T.reshape(FF, P, FF * P).transpose(1, 0, 2),
        "w3": ff1("w3_w").T.reshape(FF, P, D).transpose(1, 0, 2),
    }
    arrays = {k: np.ascontiguousarray(v) for k, v in arrays.items()}
    nc = _bacc.Bacc("TRN2", target_bir_lowering=False, num_devices=1)
    args = [nc.dram_tensor(k, v.shape, mybir.dt.float32, kind="ExternalInput").ap() for k, v in arrays.items()]
    args.append(nc.dram_tensor("out", (B, L, D), mybir.dt.float32, kind="ExternalOutput").ap())
    build(nc, *args)
    r = _run(nc, [arrays], core_ids=[0])
    return r.results[0]["out"]
```

```python
import numpy as np
import concourse.bass as bass
from concourse import mybir
from contextlib import ExitStack

P = 128
B, L, D = 16, 512, 128
NT = L // P
H = 4
DH = D // H
CH = 32
NCH = L // CH
HT = H * NT
E, TOPK = 32, 4
ES = 4
EA = E + ES
KS, KL, KC = 5, 64, 4
NST = 16
FF = 4
LEVELS = 5
LN_EPS, RMS_EPS, GN_EPS = 1e-5, 1e-5, 0.00064

FILL = {"start": "eeeee", "tok0": "e", "tok": "eeeee", "norm": "eeeeeee", "L": "ee", "L3": "eee", "A": "eee", "inv": "eeeee", "uw": "meeee",
        "au": "eeeee", "fir": "eeeeee", "st": "eee", "hid": "meeem", "lgt": "eeee", "front1": "eee", "front2": "eeeee"}
for _l in range(1, LEVELS):
    FILL[f"lv{_l}a"] = "eee"
    FILL[f"lv{_l}b"] = "eee"
for _c in range(NCH):
    FILL[f"sc{_c}a"] = "m" if _c < 16 else "e"
    FILL[f"sc{_c}b"] = "e"
UNITS = 3 * EA + 1
STEPS = 19
FILL["oT"] = "e" * (UNITS - sum(f.count("e") for f in FILL.values()))
assert sum(f.count("e") for f in FILL.values()) == UNITS
assert sum(f.count("m") for f in FILL.values()) == STEPS
DVE_LINKS = 192

COLS = {}
_at = 0
for _n, _w in (("qc", KC), ("kc", KC), ("vc", KC), ("fs", KS), ("fl", KL), ("b1", 1), ("mix", 6), ("gnw", 1), ("gnb", 1),
               ("s1", FF), ("s2", FF), ("hs1", FF), ("hs2", FF), ("temp", 1), ("rss", 1), ("rsl", 1), ("b2", 4),
               ("onorm", 1), ("rbias", E), ("bout", D), ("w3s", D), ("w2T", 4)):
    COLS[_n] = (_at, _at + _w)
    _at += _w
NCOL = _at

CONS = {}
_at = 0
for _n, _w in (("ident", P), ("bd", P), ("avg", P), ("strict", P), ("causal", P), ("eye", CH), ("lvl", LEVELS * CH)):
    CONS[_n] = (_at, _at + _w)
    _at += _w
NCON = _at

WNAMES = ["wq", "wk", "wv", "w1x", "wo", "Wr", "Ww", "Wk", "Wv", "Wa", "Wg", "Wout"]


def build(nc, x, small, cons, wsq, wrb, w1s, moe_g, moe_u, moe_d, f1, f2, h1w, h2w, w3, out):
    f32 = mybir.dt.float32
    ACT = mybir.ActivationFunctionType
    ALU = mybir.AluOpType
    X = mybir.AxisListType.X

    x_v = x.rearrange("b (t p) d -> b p t d", p=P)
    out_v = out.rearrange("b (t p) d -> b p t d", p=P)

    ctx = ExitStack()
    with ctx:
        def sb(name, shape):
            return ctx.enter_context(nc.sbuf_tensor(name, shape, f32))

        def sem(name):
            return ctx.enter_context(nc.semaphore(name))

        sm = sb("sm", [P, NCOL])
        cn = sb("cn", [P, NCON])
        wm = sb("wm", [P, len(WNAMES), D])
        wrb_sb = sb("wrb_sb", [P, E + H])
        w1s_sb = sb("w1s_sb", [NST * H, H, P])
        eg = sb("eg", [P, EA, P])
        eu = sb("eu", [P, EA, P])
        ed = sb("ed", [P, EA, P])
        f1_sb = sb("f1_sb", [P, FF, P])
        f2_sb = sb("f2_sb", [P, FF, P])
        h1_sb = sb("h1_sb", [P, FF, FF * P])
        h2_sb = sb("h2_sb", [P, FF, FF * P])
        w3_sb = sb("w3_sb", [P, FF, D])

        def col(name, j=0, w=1):
            a, b = COLS[name]
            return sm[:, a + j:a + j + w]

        def con(name):
            a, b = CONS[name]
            return cn[:, a:b]

        def weight(name):
            return wm[:, WNAMES.index(name), :]

        ident = con("ident")

        xin = sb("xin", [P, L])
        xt = sb("xt", [P, L])
        xnT = sb("xnT", [P, L])
        vs = sb("vs", [P, L])
        Xi, ks, Yi = sb("Xi", [P, HT * CH]), sb("ks", [P, L]), sb("Yi", [P, HT * CH])
        vtok, qtok, ktok = sb("vtok", [P, L]), sb("qtok", [P, L]), sb("ktok", [P, L])
        vb, kb = sb("vb", [P, L]), sb("kb", [P, L])
        WQ = sb("WQ", [P, NCH, 2 * CH])
        knT, kbT = sb("knT", [P, L]), sb("kbT", [P, L])
        LT, Tbd = sb("LT", [P, HT, P]), sb("Tbd", [P, HT, P])
        U, uadj = sb("U", [P, L]), sb("uadj", [P, L])
        Sbd = sb("Sbd", [P, P])
        fs, fl = sb("fs", [P, L]), sb("fl", [P, L])
        sg = [sb(f"sg{j}", [P, L]) for j in range(2)]
        hx = [sb(f"hx{j}", [P, L]) for j in range(2)]
        dt = sb("dt", [P, L])
        acc, accp = sb("acc", [P, L]), sb("accp", [P, L])
        x1 = sb("x1", [P, L])
        x2 = sb("x2", [P, L])
        quarter = lambda ap, c: ap[:, 4 * c:4 * c + 4, :].rearrange("p a b -> p (a b)")
        sq4 = [quarter(LT, c) for c in range(4)]
        yv, yq, yk = sq4[0], sq4[1], sq4[2]
        qs, xn, xnN, AT, dl, dq = Xi, knT, ks, Tbd, qtok, Yi
        lstok, lltok, gs = kb, vb, kbT
        hdn = [Xi, ks, Yi, fs]
        WQf = WQ[:, :, :].rearrange("p c k -> p (c k)")
        pr = [WQf[:, 0:L], WQf[:, L:2 * L], fl[:, :], ktok[:, :]]
        o, osq, oT = U, fl, uadj
        statsT = ktok[0:NST * H, :]
        xn1 = sb("xn1", [P, L])
        xn1p = sb("xn1p", [P, L + 4])
        mixd = [sb(f"mixd{j}", [P, L]) for j in range(6)]
        fh = [sb(f"fh{c}", [P, L]) for c in range(FF)]
        rg, dec, kt, al, gg, vv = (sb(n, [P, L]) for n in ("rg", "dec", "kt", "al", "gg", "vv"))
        dT, g1, g2, g2r = xn1, mixd[0:4], fh, rg
        uu, stt, mixed, cen, sqc, rvar, mg, s1 = vv, al, kt, al, vv, dec, mixd[4], mixd[5]

        bst = [sb(f"bst{j}", [P, NT, 6]) for j in range(2)]
        mv = [sb(f"mv{j}", [P, NT, 2]) for j in range(2)]
        vr = [sb(f"vr{j}", [P, NT]) for j in range(2)]
        rstd = [sb(f"rstd{j}", [P, NT]) for j in range(2)]
        lg = sb("lg", [P, NT, E])
        mx = sb("mx", [P, NT])
        sc = sb("sc", [P, NT, E + TOPK])
        ssum = sb("ssum", [P, NT])
        m8 = sb("m8", [P, NT, 8])
        m4 = sb("m4", [P, NT, 8])
        rep = sb("rep", [P, NT, E + TOPK])
        wsc = sb("wsc", [P, NT, E])
        beta = sb("beta", [P, NT, H])
        ss = sb("ss", [P, 2, HT])
        rn = sb("rn", [P, 2, HT])
        st_s, st_a, st_q = (sb(n, [P, NT, 4, H]) for n in ("st_s", "st_a", "st_q"))
        m2_c = sb("m2_c", [P, NT, 4 * H])
        stats = sb("stats", [P, NT, 4, 4, H])
        lgx = sb("lgx", [P, HT, 4])
        lmx = sb("lmx", [P, HT])
        fe = sb("fe", [P, HT, 4])
        fsum = sb("fsum", [P, HT])
        fw = sb("fw", [P, HT, 4])
        ms = sb("ms", [P, HT])
        rms = sb("rms", [P, HT])
        spare = sb("spare", [P, 2])
        unit = sb("unit", [P, 2])
        tmp1 = sb("tmp1", [P, 4])
        invt = sb("invt", [P, 1])
        b2t = sb("b2t", [P, 4])

        ps = ctx.enter_context(nc.psum_tensor("ps", [P, 8, L], f32))
        G, Ub, Db, M0, M1, C0, C1, C2 = range(8)

        def bank(b):
            return ps[:, b, :]

        def tile(ap, t):
            return ap[:, t * P:(t + 1) * P]

        def byhead(ap):
            return ap.rearrange("p (a d) -> p a d", d=DH)

        def tilehead(ap):
            return ap.rearrange("p (t h d) -> p t h d", h=H, d=DH)

        def flat(ap):
            return ap.rearrange("p t j h -> p t (j h)")

        def stat(s):
            return flat(stats[:, :, s, :, :])

        def on_vector(d):
            return d % 2 == 0

        s_w = sem("weights_loaded")
        s_moe = sem("expert_weights_loaded")
        s_l1 = sem("layer1_weights_loaded")
        unit_ready = sem("unit_ready")
        pre_act, pre_dve, tbd_clear, x1_clear = sem("pre_act"), sem("pre_dve"), sem("tbd_clear"), sem("x1_clear")
        x_loaded, x_copied, x1_ready, x2_ready, x2_stored = sem("x_loaded"), sem("x_copied"), sem("x1_ready"), sem("x2_ready"), sem("x2_stored")
        xnT_ready = sem("xnT_ready")
        vr0_ready, rstd0_ready, xn_ready, xT_ps, xnN_ready = sem("vr0_ready"), sem("rstd0_ready"), sem("xn_ready"), sem("xT_ps"), sem("xnN_ready")
        proj = {c: sem(f"proj_{c}") for c in "vqk"}
        tap = {c: sem(f"tap_{c}") for c in "vqk"}
        conv = {c: sem(f"conv_{c}") for c in "vqk"}
        silu = {c: sem(f"silu_{c}") for c in "vqk"}
        tok_ps = {c: sem(f"tok_ps_{c}") for c in "vqk"}
        tok = {c: sem(f"tok_{c}") for c in "vqk"}
        rb_ps, rb_read, beta_ready, lgs_ready, ex_ready, wsc_ready = sem("rb_ps"), sem("rb_read"), sem("beta_ready"), sem("lgs_ready"), sem("ex_ready"), sem("wsc_ready")
        sq_ready = {c: sem(f"sq_{c}") for c in "qk"}
        ss_ready, rn_ready, qn_ready, kn_ready, kb_ready, vb_ready = (sem(n) for n in ("ss_ready", "rn_ready", "qn_ready", "kn_ready", "kb_ready", "vb_ready"))
        nT_ps = {c: sem(f"nT_ps_{c}") for c in "qkb"}
        nT = {c: sem(f"nT_{c}") for c in "qkb"}
        l_ps, lt_ready, a_ps, at_ready = sem("l_ps"), sem("lt_ready"), sem("a_ps"), sem("at_ready")
        xi_ready, tbd_ready, y_ps = sem("xi_ready"), sem("tbd_ready"), sem("y_ps")
        y_ready, z_ps = sem("y_ready"), sem("z_ps")
        u_ps, wt_ps, u_ready, wt_ready, s0_ready = sem("u_ps"), sem("wt_ps"), sem("u_ready"), sem("wt_ready"), sem("s0_ready")
        ws_ps, uadj_ready, dq_ready = sem("ws_ps"), sem("uadj_ready"), sem("dq_ready")
        s_ps, s_ready = sem("s_ps"), sem("s_ready")
        au_ps, dl_ready = sem("au_ps"), sem("dl_ready")
        fir0 = sem("fir0")
        fs_ready, fl_ready, fsT_ps, flT_ps, ls_ready, ll_ready = (sem(n) for n in ("fs_ready", "fl_ready", "fsT_ps", "flT_ps", "ls_ready", "ll_ready"))
        sq4_ready = sem("sq4_ready")
        stq_ready, l2_ready, stats_ready, stT_ps, stT_ready = (sem(n) for n in ("stq_ready", "l2_ready", "stats_ready", "stT_ps", "stT_ready"))
        hid_ps, hdn_ready = sem("hid_ps"), sem("hdn_ready")
        lgt_ps, lgx_ready, fe_ready, fw_ready, p23_one, p23_ready, o_sum, osq_ready, ms_ready, rms_ready, on_ready, oT_ps, oT_ready, sp_ps = (
            sem(n) for n in ("lgt_ps", "lgx_ready", "fe_ready", "fw_ready", "p23_one", "p23_ready", "o_sum", "osq_ready", "ms_ready", "rms_ready", "on_ready", "oT_ps", "oT_ready", "sp_ps"))
        asum_one, gs_ready = sem("asum_one"), sem("gs_ready")
        g_ps, up_ps, d_ps, sg_ready, h_ready, dacc, dt_ready, pacc = (sem(n) for n in ("g_ps", "up_ps", "d_ps", "sg_ready", "h_ready", "dacc", "dt_ready", "pacc"))
        vr1_ready, rstd1_ready, xn1_ready, x1T_ps, x1T_ready = (sem(n) for n in ("vr1_ready", "rstd1_ready", "xn1_ready", "x1T_ps", "x1T_ready"))
        ffg_ps, ffu_ps, sgf_ready, fh_ready, h1_ps, g1_ready, h2_ps, g2_ready = (sem(n) for n in ("ffg_ps", "ffu_ps", "sgf_ready", "fh_ready", "h1_ps", "g1_ready", "h2_ps", "g2_ready"))
        mix_ready, pj_ps, pj_act = sem("mix_ready"), sem("pj_ps"), sem("pj_act")
        ak_ready, uu_ready, st_ready, mixed_ready, mu_ps, cen_ready, sqc_ready, var_ps, rvar_ready, rsd_ready, mn_ready, mg_ready, op_ps, w3_ps, g2r_ready, g2s_ready = (
            sem(n) for n in ("ak_ready", "uu_ready", "st_ready", "mixed_ready", "mu_ps", "cen_ready", "sqc_ready", "var_ps", "rvar_ready", "rsd_ready", "mn_ready", "mg_ready", "op_ps", "w3_ps", "g2r_ready", "g2s_ready"))
        dve_link = sem("dve_link")

        block = ctx.enter_context(nc.Block())

        @block.sync
        def _(sp):
            xin_v = xin[:, :].rearrange("p (t d) -> p t d", d=D)
            x2_v = x2[:, :].rearrange("p (t d) -> p t d", d=D)
            sp.dma_start(xin_v, x_v[0]).then_inc(x_loaded, 16)
            for dst, src in ((sm[:, :], small), (cn[:, :], cons), (wm[:, :, :], wsq), (wrb_sb[:, :], wrb), (w1s_sb[:, :, :], w1s)):
                sp.dma_start(dst, src).then_inc(s_w, 16)
            for e0 in range(0, EA, 12):
                for dst, src in ((eg, moe_g), (eu, moe_u), (ed, moe_d)):
                    sp.dma_start(dst[:, e0:e0 + 12, :], src[:, e0:e0 + 12, :]).then_inc(s_moe, 16)
            for dst, src in ((f1_sb, f1), (f2_sb, f2), (h1_sb, h1w), (h2_sb, h2w), (w3_sb, w3)):
                sp.dma_start(dst[:, :, :], src).then_inc(s_l1, 16)
            sp.wait_ge(x_copied, 1)
            sp.dma_start(xin_v, x_v[1]).then_inc(x_loaded, 16)
            with sp.Fori(1, B) as i:
                n = sp.snap(i + 1)
                sp.wait_ge(x_copied, n)
                sp.dma_start(xin_v, x_v[bass.ds(n, 1), :, :, :].rearrange("b p t d -> p (b t) d")).then_inc(x_loaded, 16)
                sp.wait_ge(x2_ready, n)
                sp.dma_start(out_v[bass.ds(i - 1, 1), :, :, :].rearrange("b p t d -> p (b t) d"), x2_v).then_inc(x2_stored, 16)
            sp.wait_ge(x2_ready, B + 1)
            sp.dma_start(out_v[B - 1], x2_v).then_inc(x2_stored, 16)
            sp.wait_ge(x2_stored, 16 * (B + 2))

        @block.tensor
        def _(pe):
            mm = nc.tensor.matmul

            def transposes(b, src, done, w=P):
                for t in range(NT):
                    last = nc.tensor.transpose(ps[0:w, b, t * P:(t + 1) * P], src[:, t * w:(t + 1) * w], ident)
                last.then_inc(done, 1)

            def front(m):
                pe.wait_ge(xn_ready, m)
                transposes(M0, xn, xT_ps)
                pe.wait_ge(xnN_ready, m)
                for t in range(NT):
                    last = mm(ps[:, C0, t * (E + H):(t + 1) * (E + H)], tile(xnN, t), wrb_sb[:, :], start=True, stop=True)
                last.then_inc(rb_ps, 1)
                for c, b, w in (("v", C1, "wv"), ("q", M0, "wq"), ("k", M1, "wk")):
                    mm(bank(b), weight(w), xnN[:, :], start=True, stop=True).then_inc(proj[c], 1)

            def layer1_step(k, i, n):
                x1T = xn1p[:, 4:4 + L]

                def hidden(b, w_sb, src, c, done):
                    for kk in range(FF):
                        last = mm(bank(b), w_sb[:, kk, c * P:(c + 1) * P], src[kk][:, :], start=(kk == 0), stop=(kk == FF - 1))
                    last.then_inc(done, 1)

                if k == 1:
                    pe.wait_ge(xn1_ready, n)
                    transposes(M0, xn1, x1T_ps)
                elif 2 <= k <= 5:
                    c = k - 2
                    if c == 0:
                        pe.wait_ge(x1T_ready, n)
                    else:
                        pe.wait_ge(sgf_ready, i * FF + c)
                    mm(bank(M0), f1_sb[:, c, :], x1T, start=True, stop=True).then_inc(ffg_ps, 1)
                    if c:
                        pe.wait_ge(fh_ready, i * FF + c)
                    mm(bank(M1), f2_sb[:, c, :], x1T, start=True, stop=True).then_inc(ffu_ps, 1)
                elif 6 <= k <= 8:
                    for j, b, w in (((0, M0, "Wr"), (1, M1, "Ww")), ((2, M0, "Wk"), (3, M1, "Wv")), ((4, M0, "Wa"), (5, M1, "Wg")))[k - 6]:
                        if k == 6:
                            pe.wait_ge(fh_ready, i * FF + FF)
                        else:
                            pe.wait_ge(pj_act, i * 6 + j - 1)
                        pe.wait_ge(mix_ready, i * 6 + j + 1)
                        mm(bank(b), weight(w), mixd[j][:, :], start=True, stop=True).then_inc(pj_ps, 1)
                elif k in (9, 10):
                    for c, b in ((2 * k - 18, M0), (2 * k - 17, M1)):
                        if k == 9:
                            pe.wait_ge(pj_act, i * 6 + 5 + c)
                        else:
                            pe.wait_ge(g1_ready, i * FF + c - 1)
                        hidden(b, h1_sb, fh, c, h1_ps)
                elif k == 11:
                    pe.wait_ge(g1_ready, i * FF + FF)
                    hidden(M0, h2_sb, g1, 0, h2_ps)
                    hidden(M1, h2_sb, g1, 1, h2_ps)
                elif k == 12:
                    pe.wait_ge(g2_ready, i * FF + 1)
                    pe.wait_ge(mixed_ready, n)
                    mm(bank(M0), con("avg"), mixed[:, :], start=True, stop=True).then_inc(mu_ps, 1)
                    pe.wait_ge(g2_ready, i * FF + 2)
                    hidden(M1, h2_sb, g1, 2, h2_ps)
                elif k == 13:
                    pe.wait_ge(g2_ready, i * FF + 3)
                    hidden(M1, h2_sb, g1, 3, h2_ps)
                elif k == 14:
                    pe.wait_ge(sqc_ready, n)
                    mm(bank(M0), con("avg"), sqc[:, :], start=True, stop=True).then_inc(var_ps, 1)
                elif k == 15:
                    pe.wait_ge(g2_ready, i * FF + FF)
                    for t in range(NT):
                        for kk in range(FF):
                            last = mm(tile(bank(M1), t), g2[kk][:, t * P:(t + 1) * P], w3_sb[:, kk, :], start=(kk == 0), stop=(kk == FF - 1))
                    last.then_inc(w3_ps, 1)
                elif k == 17:
                    pe.wait_ge(mg_ready, n)
                    for t in range(NT):
                        last = mm(tile(bank(M0), t), tile(mg, t), weight("Wout"), start=True, stop=True)
                    last.then_inc(op_ps, 1)

            pe.wait_ge(s_w, 16 * 5)
            front(1)
            pe.wait_ge(s_moe, 16 * 9)
            pe.wait_ge(s_l1, 16 * 5)
            with pe.Fori(0, B) as i:
                n = pe.snap(i + 1)
                n2 = pe.snap(i + 2)
                ie = pe.snap(i * EA)
                iq = pe.snap(i * (EA // 2))
                at = {"e": 0, "m": 0}

                def expert_unit(k):
                    e, kind = divmod(k, 3)
                    if kind == 0 and e < EA:
                        if e:
                            pe.wait_ge(sg_ready, ie + e)
                        else:
                            pe.wait_ge(xnT_ready, n)
                        mm(bank(G), eg[:, e, :], xnT[:, :], start=True, stop=True).then_inc(g_ps, 1)
                    elif kind == 1:
                        if e:
                            pe.wait_ge(h_ready, ie + e)
                        mm(bank(Ub), eu[:, e, :], xnT[:, :], start=True, stop=True).then_inc(up_ps, 1)
                    elif e > 0 or kind == 0:
                        d = e - 1
                        pe.wait_ge(h_ready, ie + d + 1)
                        if d:
                            pe.wait_ge(dacc if on_vector(d - 1) else dt_ready, iq + (d + 1) // 2)
                        for t in range(NT):
                            last = mm(tile(bank(Db), t), tile(hx[d % 2], t), ed[:, d, :], start=True, stop=True)
                        last.then_inc(d_ps, 1)

                def fill(name):
                    for c in FILL[name]:
                        if c == "e":
                            expert_unit(at[c])
                        else:
                            layer1_step(at[c], i, n)
                        at[c] += 1

                fill("start")
                for c, b, src in (("v", C1, vs), ("q", C2, qs), ("k", C0, ks)):
                    pe.wait_ge(silu[c], n)
                    if b == C2:
                        pe.wait_ge(x1_ready, n)
                    if b == C0:
                        pe.wait_ge(rb_read, n)
                    transposes(b, src, tok_ps[c])
                fill("tok0")
                fill("tok")
                for c, b, src, ready in (("q", C2, qtok, qn_ready), ("k", C0, ktok, kn_ready), ("b", C1, kb, kb_ready)):
                    pe.wait_ge(ready, n)
                    transposes(b, src, nT_ps[c])
                fill("norm")
                for c in "qkb":
                    pe.wait_ge(nT[c], n)
                for h in range(H):
                    r = slice(DH * h, DH * h + DH)
                    if h == 3:
                        fill("L")
                        pe.wait_ge(lt_ready, i * H + 1)
                    for t in range(NT):
                        last = mm(tile(bank((C0, C1, C2, C0)[h]), t), tile(knT, t)[r, :], tile(kbT, t)[r, :], start=True, stop=True)
                    last.then_inc(l_ps, 1)
                fill("L3")
                pe.wait_ge(lt_ready, i * H + H)
                for a in range(HT):
                    last = mm(ps[:, C1, a * CH:(a + 1) * CH], LT[:, a, :], con("eye"), start=True, stop=True)
                last.then_inc(y_ps, 1)
                fill("A")
                for l in range(1, LEVELS):
                    fill(f"lv{l}a")
                    pe.wait_ge(xi_ready, i * LEVELS + l)
                    for a in range(HT):
                        last = mm(ps[:, C1, a * CH:(a + 1) * CH], LT[:, a, :], Xi[:, a * CH:(a + 1) * CH], start=True, stop=True)
                    last.then_inc(y_ps, 1)
                    fill(f"lv{l}b")
                    pe.wait_ge(y_ready, i * (LEVELS - 1) + l)
                    pe.wait_ge(tbd_ready, (i * LEVELS + l) * (P // CH))
                    for a in range(HT):
                        last = mm(ps[:, C2, a * CH:(a + 1) * CH], Tbd[:, a, :], Yi[:, a * CH:(a + 1) * CH], start=True, stop=True)
                    last.then_inc(z_ps, 1)
                fill("inv")
                pe.wait_ge(tbd_ready, (i * LEVELS + LEVELS) * (P // CH))
                pe.wait_ge(vb_ready, n)
                for h in range(H):
                    for t in range(NT):
                        c = slice(t * P + DH * h, t * P + DH * h + DH)
                        last = mm(ps[:, C0, c], Tbd[:, h * NT + t, :], vb[:, c], start=True, stop=True)
                last.then_inc(u_ps, 1)
                for h in range(H):
                    for t in range(NT):
                        c = slice(t * P + DH * h, t * P + DH * h + DH)
                        last = mm(ps[DH * h:DH * h + DH, C2, t * P:(t + 1) * P], kb[:, c], Tbd[:, h * NT + t, :], start=True, stop=True)
                last.then_inc(wt_ps, 1)
                fill("uw")
                pe.wait_ge(u_ready, n)
                pe.wait_ge(wt_ready, n)
                for c in range(NCH):
                    t, g = divmod(c, NT)
                    r = slice(CH * g, CH * g + CH)
                    if c == 0:
                        pe.wait_ge(s0_ready, n)
                    else:
                        pe.wait_ge(s_ready, i * (NCH - 1) + c)
                    if c >= 2:
                        pe.wait_ge(dq_ready, i * NCH + c - 1)
                    half = slice(2 * CH * (c % 2), 2 * CH * (c % 2) + 2 * CH)
                    mm(ps[half, C0, 0:P], WQ[:, c, :], Sbd[:, :], start=True, stop=True).then_inc(ws_ps, 1)
                    fill(f"sc{c}a")
                    if c % 4 == 1:
                        h = c // 4
                        if h:
                            pe.wait_ge(at_ready, i * H + h)
                        rh = slice(DH * h, DH * h + DH)
                        for tt_ in range(NT):
                            last = mm(tile(bank(C2), tt_), tile(knT, tt_)[rh, :], WQ[rh, NT * tt_:NT * tt_ + NT, CH:2 * CH], start=True, stop=True)
                        last.then_inc(a_ps, 1)
                    if c < NCH - 1:
                        pe.wait_ge(uadj_ready, i * NCH + c + 1)
                        mm(ps[:, C1, 0:P], tile(ktok, t)[r, :], tile(uadj, t)[r, :], start=(c == 0), stop=True, skip_group_check=True).then_inc(s_ps, 1)
                    fill(f"sc{c}b")
                pe.wait_ge(uadj_ready, i * NCH + NCH)
                pe.wait_ge(at_ready, i * H + H)
                for h in range(H):
                    for t in range(NT):
                        c = slice(t * P + DH * h, t * P + DH * h + DH)
                        last = mm(ps[:, C2, c], AT[:, h * NT + t, :], uadj[:, c], start=True, stop=True)
                last.then_inc(au_ps, 1)
                pe.wait_ge(fs_ready, n)
                pe.wait_ge(dq_ready, i * NCH + NCH)
                transposes(C0, fs, fsT_ps)
                pe.wait_ge(fl_ready, n)
                transposes(C1, fl, flT_ps)
                fill("au")
                fill("fir")
                HB = (C0, C1, C2, C0)
                pe.wait_ge(ls_ready, n)
                mm(bank(HB[0]), weight("w1x"), xnT[:, :], start=True, stop=False)
                pe.wait_ge(ll_ready, n)
                pe.wait_ge(stats_ready, n)
                pe.wait_ge(l2_ready, n)
                mm(bank(HB[1]), weight("w1x"), xnT[:, :], start=True, stop=False)
                transposes(C2, stats[:, :, :, :, :].rearrange("p t s j h -> p (t s j h)"), stT_ps, w=NST * H)
                fill("st")
                pe.wait_ge(stT_ready, n)
                for h, b in enumerate(HB):
                    if h == 3:
                        pe.wait_ge(hdn_ready, i * H + 1)
                    if h >= 2:
                        mm(bank(b), weight("w1x"), xnT[:, :], start=True, stop=False)
                    mm(bank(b), w1s_sb[:, h, :], statsT, start=False, stop=True).then_inc(hid_ps, 1)
                fill("hid")
                pe.wait_ge(hdn_ready, i * H + H)
                for h in range(H):
                    for t in range(NT):
                        a = (t * H + h) * 4
                        last = mm(ps[:, C1, a:a + 4], tile(hdn[h], t), col("w2T", 0, 4), start=True, stop=True)
                last.then_inc(lgt_ps, 1)
                fill("lgt")
                pe.wait_ge(x2_ready, n)
                pe.wait_ge(lgx_ready, n)
                front(n2)
                fill("front1")
                fill("front2")
                pe.wait_ge(on_ready, n)
                transposes(C2, o, oT_ps)
                fill("oT")
                pe.wait_ge(oT_ready, n)
                for t in range(NT):
                    last = mm(tile(bank(C2), t), tile(oT, t), weight("wo"), start=True, stop=True)
                last.then_inc(sp_ps, 1)
            for k in range(STEPS):
                layer1_step(k, B, B + 1)

        @block.scalar
        def _(act):
            f = nc.scalar.activation

            def front(m):
                act.wait_ge(xT_ps, m)
                f(xnN[:, :], bank(M0), ACT.Copy).then_inc(xnN_ready, 1)

            def own_xnT(m):
                act.wait_ge(xnN_ready, m)
                f(xnT[:, :], xnN[:, :], ACT.Copy).then_inc(xnT_ready, 1)

            def front_taps(m):
                for c, b, w, y in (("v", C1, "vc", yv), ("q", M0, "qc", yq), ("k", M1, "kc", yk)):
                    act.wait_ge(proj[c], m)
                    f(y[:, :], bank(b), ACT.Copy, scale=col(w, KC - 1)).then_inc(tap[c], 1)

            def front_router(m):
                act.wait_ge(lgs_ready, m)
                f(sc[:, :, 0:E], lg[:, :, :], ACT.Exp).then_inc(ex_ready, 1)
                f(beta[:, :, :], ps[:, C0, 0:NT * (E + H)].rearrange("p (t c) -> p t c", t=NT)[:, :, E:E + H], ACT.Exp, scale=-1.0).then_inc(rb_read, 1)

            def layer1_step(k, i, n):
                if k == 1:
                    act.wait_ge(x1T_ps, n)
                    f(xn1p[:, 4:4 + L], bank(M0), ACT.Copy).then_inc(x1T_ready, 1)
                elif 2 <= k <= 5:
                    act.wait_ge(ffg_ps, i * FF + k - 1)
                    f(fh[k - 2][:, :], bank(M0), ACT.Silu, scale=col("s1", k - 2)).then_inc(sgf_ready, 1)
                elif 6 <= k <= 8:
                    for j, b, dst, fn, s in (((0, M0, rg, ACT.Sigmoid, 1.0), (1, M1, dec, ACT.Sigmoid, -1.0)),
                                             ((2, M0, kt, ACT.Tanh, 1.0), (3, M1, vv, ACT.Copy, 1.0)),
                                             ((4, M0, al, ACT.Sigmoid, 1.0), (5, M1, gg, ACT.Sigmoid, 1.0)))[k - 6]:
                        act.wait_ge(pj_ps, i * 6 + j + 1)
                        f(dst[:, :], bank(b), fn, scale=s).then_inc(pj_act, 1)
                elif k in (9, 10):
                    for c, b in ((2 * k - 18, M0), (2 * k - 17, M1)):
                        act.wait_ge(h1_ps, i * FF + c + 1)
                        f(g1[c][:, :], bank(b), ACT.Gelu, scale=col("hs1", c)).then_inc(g1_ready, 1)
                elif 11 <= k <= 13:
                    if k == 13:
                        act.wait_ge(cen_ready, n)
                        f(sqc[:, :], cen[:, :], ACT.Square).then_inc(sqc_ready, 1)
                    for c, b in (((0, M0), (1, M1)), ((2, M1),), ((3, M1),))[k - 11]:
                        act.wait_ge(h2_ps, i * FF + c + 1)
                        f(g2[c][:, :], bank(b), ACT.Gelu, scale=col("hs2", c)).then_inc(g2_ready, 1)
                elif k == 16:
                    act.wait_ge(rvar_ready, n)
                    f(rvar[:, :], rvar[:, :], ACT.Sqrt).then_inc(rsd_ready, 1)
                elif k == 17:
                    act.wait_ge(g2r_ready, n)
                    f(g2r[:, :], g2r[:, :], ACT.Silu).then_inc(g2s_ready, 1)

            act.wait_ge(s_w, 16 * 5)
            f(tmp1[:, 0:1], col("temp"), ACT.Abs).then_inc(pre_act, 1)
            act.wait_ge(pre_act, 1)
            f(tmp1[:, 1:2], tmp1[:, 0:1], ACT.Exp, scale=-1.0).then_inc(pre_act, 1)
            act.wait_ge(pre_act, 2)
            f(tmp1[:, 2:3], tmp1[:, 1:2], ACT.Ln, bias=1.0).then_inc(pre_act, 1)
            f(tmp1[:, 3:4], col("temp"), ACT.Relu).then_inc(pre_act, 1)
            front(1)
            front_taps(1)
            own_xnT(1)
            front_router(1)
            with act.Fori(0, B) as i:
                n = act.snap(i + 1)
                n2 = act.snap(i + 2)
                ie = act.snap(i * EA)
                iq = act.snap(i * (EA // 2))
                at = {"e": 0, "m": 0}

                def expert_unit(k):
                    e, kind = divmod(k, 3)
                    if kind == 0 and e < EA:
                        act.wait_ge(g_ps, ie + e + 1)
                        f(sg[e % 2][:, :], bank(G), ACT.Silu).then_inc(sg_ready, 1)
                    elif kind == 2 and e > 0 or k == UNITS - 1:
                        d = e - 1
                        if on_vector(d):
                            return
                        if d == 1:
                            act.wait_ge(wsc_ready, n)
                        act.wait_ge(d_ps, ie + d + 1)
                        if d >= 3:
                            act.wait_ge(pacc, iq + d // 2)
                        for t in range(NT):
                            s = wsc[:, t, d:d + 1] if d < E else 1.0
                            last = f(tile(dt, t), tile(bank(Db), t), ACT.Copy, scale=s)
                        last.then_inc(dt_ready, 1)

                def fill(name):
                    for c in FILL[name]:
                        if c == "e":
                            expert_unit(at[c])
                        else:
                            layer1_step(at[c], i, n)
                        at[c] += 1

                def copy(dst, b, src_ready, done):
                    act.wait_ge(src_ready, n)
                    f(dst[:, 0:L], bank(b), ACT.Copy).then_inc(done, 1)

                fill("start")
                for c, y, dst in (("v", yv, vs), ("q", yq, qs), ("k", yk, ks)):
                    act.wait_ge(conv[c], n)
                    f(dst[:, :], y, ACT.Silu).then_inc(silu[c], 1)
                for c, b, dst, sq in (("q", C2, qtok, sq4[1]), ("k", C0, ktok, sq4[2])):
                    act.wait_ge(tok_ps[c], n)
                    f(sq, bank(b), ACT.Square).then_inc(sq_ready[c], 1)
                    f(dst[:, :], bank(b), ACT.Copy).then_inc(tok[c], 1)
                copy(vtok, C1, tok_ps["v"], tok["v"])
                act.wait_ge(x1_ready, n)
                f(xt[:, :], xin[:, :], ACT.Copy).then_inc(x_copied, 1)
                fill("tok0")
                fill("tok")
                act.wait_ge(ss_ready, n)
                f(rn[:, :, :], ss[:, :, :], ACT.Sqrt).then_inc(rn_ready, 1)
                act.wait_ge(silu["v"], n)
                f(fs[:, :], vs[:, :], ACT.Copy, scale=col("fs", KS - 1)).then_inc(fir0, 1)
                f(fl[:, :], vs[:, :], ACT.Copy, scale=col("fl", KL - 1)).then_inc(fir0, 1)
                act.wait_ge(nT_ps["q"], n)
                f(WQ[:, :, CH:2 * CH], bank(C2).rearrange("p (c k) -> p c k", k=CH), ACT.Copy).then_inc(nT["q"], 1)
                for c, b, dst in (("k", C0, knT), ("b", C1, kbT)):
                    copy(dst, b, nT_ps[c], nT[c])
                fill("norm")
                fill("L")
                fill("L3")
                fill("A")
                for l in range(1, LEVELS):
                    fill(f"lv{l}a")
                    act.wait_ge(y_ps, i * LEVELS + l + 1)
                    f(Yi[:, :], bank(C1), ACT.Copy).then_inc(y_ready, 1)
                    fill(f"lv{l}b")
                fill("inv")
                copy(U, C0, u_ps, u_ready)
                act.wait_ge(wt_ps, n)
                f(WQ[:, :, 0:CH], bank(C2).rearrange("p (c k) -> p c k", k=CH), ACT.Copy).then_inc(wt_ready, 1)
                fill("uw")
                for c in range(NCH):
                    t, g = divmod(c, NT)
                    act.wait_ge(ws_ps, i * NCH + c + 1)
                    qrow = 2 * CH * (c % 2) + CH
                    f(dq[CH * g:CH * g + CH, t * P:(t + 1) * P], ps[qrow:qrow + CH, C0, 0:P], ACT.Copy).then_inc(dq_ready, 1)
                    fill(f"sc{c}a")
                    fill(f"sc{c}b")
                copy(lstok, C0, fsT_ps, ls_ready)
                copy(lltok, C1, flT_ps, ll_ready)
                fill("au")
                fill("fir")
                act.wait_ge(stq_ready, i * 4 + 4)
                f(stat(3), flat(st_q[:, :, :, :]), ACT.Sqrt).then_inc(l2_ready, 1)
                act.wait_ge(stT_ps, n)
                f(statsT, ps[0:NST * H, C2, :], ACT.Copy).then_inc(stT_ready, 1)
                fill("st")
                for h, b in enumerate((C0, C1, C2, C0)):
                    act.wait_ge(hid_ps, i * H + h + 1)
                    f(hdn[h][:, :], bank(b), ACT.Gelu, bias=col("b1")).then_inc(hdn_ready, 1)
                fill("hid")
                act.wait_ge(lgx_ready, n)
                f(fe[:, :, :], lgx[:, :, :], ACT.Exp).then_inc(fe_ready, 1)
                fill("lgt")
                front(n2)
                front_taps(n2)
                fill("front1")
                fill("front2")
                front_router(n2)
                act.wait_ge(oT_ps, n)
                f(oT[:, :], bank(C2), ACT.Copy, scale=col("onorm")).then_inc(oT_ready, 1)
                fill("oT")
                own_xnT(n2)
                act.wait_ge(pacc, iq + EA // 2)
                f(gs[:, :], accp[:, :], ACT.Silu).then_inc(gs_ready, 1)
            for k in range(STEPS):
                layer1_step(k, B, B + 1)

        @block.vector
        def _(dve):
            v = nc.vector
            tt, ts, stt_ = v.tensor_tensor, v.tensor_scalar, v.scalar_tensor_tensor
            links = [0, 0]

            def link(ins):
                links[0] += 1
                ins.then_inc(dve_link, 1)
                dve.wait_ge(dve_link, links[1] + links[0])

            def end_links():
                assert links[0] < DVE_LINKS, links[0]
                dve.engine_nop().then_inc(dve_link, DVE_LINKS - links[0])
                links[0] = 0

            def over(ap, shape):
                return ap.unsqueeze(2).to_broadcast(shape)

            def norm_stats(src, j, vr_ready):
                for t in range(NT):
                    last = v.bn_stats(bst[j][:, t, :], tile(src, t))
                link(last)
                v.memset(spare[:, 0:1], 0.0)
                for t in range(NT):
                    last = v.bn_aggr(mv[j][:, t, :], bst[j][:, t, :])
                link(last)
                ts(vr[j][:, :], mv[j][:, :, 1], LN_EPS, None, ALU.add).then_inc(vr_ready, 1)

            def norm_apply(src, dst, j, rstd_ready, m, done):
                dve.wait_ge(rstd_ready, m)
                for t in range(NT):
                    last = ts(tile(dst, t), tile(src, t), mv[j][:, t, 0:1], rstd[j][:, t:t + 1], ALU.subtract, ALU.mult)
                last.then_inc(done, 1)

            def front_logits(m):
                dve.wait_ge(rb_ps, m)
                lgp = ps[:, C0, 0:NT * (E + H)].rearrange("p (t c) -> p t c", t=NT)[:, :, 0:E]
                link(tt(lg[:, :, :], lgp, col("rbias", 0, E).unsqueeze(1).to_broadcast([P, NT, E]), ALU.add))
                link(v.tensor_reduce(mx[:, :], lg[:, :, :], X, ALU.max))
                tt(lg[:, :, :], lg[:, :, :], over(mx[:, :], [P, NT, E]), ALU.subtract).then_inc(lgs_ready, 1)

            CONVS = [(lag, c) for lag in range(1, KC) for c in "vqk"]

            def front_conv(m, a, units):
                if a == 0:
                    for c in "vqk":
                        dve.wait_ge(tap[c], m)
                for lag, c in CONVS[a * len(CONVS) // units:(a + 1) * len(CONVS) // units]:
                    b, w, y = {"v": (C1, "vc", yv), "q": (M0, "qc", yq), "k": (M1, "kc", yk)}[c]
                    ins = stt_(y[:, lag:L], ps[:, b, 0:L - lag], col(w, KC - 1 - lag), y[:, lag:L], ALU.mult, ALU.add)
                    if lag == KC - 1:
                        ins.then_inc(conv[c], 1)
                    elif c == "k":
                        link(ins)

            def front_topk(m):
                dve.wait_ge(ex_ready, m)
                dve.wait_ge(rb_read, m)
                link(ts(beta[:, :, :], beta[:, :, :], 1.0, None, ALU.add))
                v.reciprocal(beta[:, :, :], beta[:, :, :]).then_inc(beta_ready, 1)
                link(v.tensor_reduce(ssum[:, :], sc[:, :, 0:E], X, ALU.add))
                link(v.reciprocal(ssum[:, :], ssum[:, :]))
                link(tt(sc[:, :, 0:E], sc[:, :, 0:E], over(ssum[:, :], [P, NT, E]), ALU.mult))
                v.memset(spare[:, 1:2], 0.0)
                for t in range(NT):
                    last = v.max(m8[:, t, :], sc[:, t, 0:E])
                link(last)
                v.tensor_copy(m4[:, :, 0:TOPK], m8[:, :, 0:TOPK])
                link(v.tensor_reduce(mx[:, :], m8[:, :, 0:TOPK], X, ALU.add))
                link(ts(mx[:, :], mx[:, :], 1e-12, None, ALU.max))
                v.reciprocal(mx[:, :], mx[:, :])
                for t in range(NT):
                    last = v.match_replace(rep[:, t, :], m4[:, t, :], sc[:, t, :], -2.0)
                link(last)
                link(tt(rep[:, :, 0:E], rep[:, :, 0:E], sc[:, :, 0:E], ALU.not_equal))
                link(tt(wsc[:, :, :], rep[:, :, 0:E], sc[:, :, 0:E], ALU.mult))
                tt(wsc[:, :, :], wsc[:, :, :], over(mx[:, :], [P, NT, E]), ALU.mult).then_inc(wsc_ready, 1)

            def mix(js):
                for j in js:
                    stt_(mixd[j][:, :], dT[:, :], col("mix", j), xn1p[:, 4:4 + L], ALU.mult, ALU.add).then_inc(mix_ready, 1)

            def layer1_late(k, i, n):
                if k == 0:
                    norm_apply(x1, xn1, 1, rstd1_ready, n, xn1_ready)
                elif 2 <= k <= 5:
                    c = k - 2
                    dve.wait_ge(sgf_ready, i * FF + c + 1)
                    dve.wait_ge(ffu_ps, i * FF + c + 1)
                    stt_(fh[c][:, :], bank(M1), col("s2", c), fh[c][:, :], ALU.mult, ALU.mult).then_inc(fh_ready, 1)
                    mix(((1,), (2, 3), (4,), (5,))[c])

            def layer1_step(k, i, n):
                rows = "p (t d) -> p t d"
                if k == 0:
                    norm_stats(x1, 1, vr1_ready)
                elif k == 2:
                    dve.wait_ge(x1T_ready, n)
                    link(tt(dT[:, :], xn1p[:, 3:3 + L], xn1p[:, 4:4 + L], ALU.subtract))
                    mix((0,))
                elif k == 10:
                    dve.wait_ge(uu_ready, n)
                    v.tensor_tensor_scan(stt[:, :], dec[:, :], uu[:, :], 0.0, ALU.mult, ALU.add).then_inc(st_ready, 1)
                elif k == 13:
                    dve.wait_ge(mu_ps, n)
                    tt(cen[:, :], mixed[:, :], bank(M0), ALU.subtract).then_inc(cen_ready, 1)
                elif k == 15:
                    dve.wait_ge(var_ps, n)
                    link(ts(rvar[:, :], bank(M0), GN_EPS, None, ALU.add))
                    v.reciprocal(rvar[:, 0:L // 2], rvar[:, 0:L // 2])
                elif k == 16:
                    v.reciprocal(rvar[:, L // 2:L], rvar[:, L // 2:L]).then_inc(rvar_ready, 1)
                elif k == 17:
                    dve.wait_ge(rsd_ready, n)
                    link(tt(cen[:, :], cen[:, :], rvar[:, :], ALU.mult))
                    ts(cen[:, :], cen[:, :], col("gnw"), col("gnb"), ALU.mult, ALU.add).then_inc(mn_ready, 1)
                    dve.wait_ge(w3_ps, n)
                    tt(g2r[:, :].rearrange(rows, d=D), bank(M1).rearrange(rows, d=D),
                       col("w3s", 0, D).unsqueeze(1).to_broadcast([P, NT, D]), ALU.mult).then_inc(g2r_ready, 1)
                elif k == 18:
                    dve.wait_ge(op_ps, n)
                    link(tt(s1[:, :].rearrange(rows, d=D), bank(M0).rearrange(rows, d=D),
                            col("bout", 0, D).unsqueeze(1).to_broadcast([P, NT, D]), ALU.add))
                    dve.wait_ge(g2s_ready, n)
                    link(tt(s1[:, :], s1[:, :], g2r[:, :], ALU.mult))
                    dve.wait_ge(x2_stored, 16 * n)
                    tt(x2[:, :], x1[:, :], s1[:, :], ALU.add).then_inc(x2_ready, 1)

            v.memset(sc[:, :, E:E + TOPK], -1.0)
            v.memset(m4[:, :, TOPK:8], -1.0)
            v.memset(xn1p[:, 0:4], 0.0)
            v.memset(x1[:, :], 0.0).then_inc(x1_ready, 1)
            v.memset(unit[:, 0:1], 0.0).then_inc(x2_stored, 32)
            v.memset(unit[:, 1:2], -0.5).then_inc(unit_ready, 1)
            dve.wait_ge(s_w, 16 * 5)
            dve.wait_ge(pre_act, 4)
            tt(tmp1[:, 0:1], tmp1[:, 2:3], tmp1[:, 3:4], ALU.add).then_inc(pre_dve, 1)
            dve.wait_ge(pre_dve, 1)
            ts(tmp1[:, 1:2], tmp1[:, 0:1], 0.0001, None, ALU.add).then_inc(pre_dve, 1)
            dve.wait_ge(pre_dve, 2)
            v.reciprocal(invt[:, :], tmp1[:, 1:2]).then_inc(pre_dve, 1)
            dve.wait_ge(pre_dve, 3)
            ts(b2t[:, :], col("b2", 0, 4), invt[:, :], None, ALU.mult).then_inc(pre_dve, 1)
            dve.wait_ge(pre_dve, 4)
            dve.wait_ge(x_loaded, 16)
            norm_stats(xin, 0, vr0_ready)
            norm_apply(xin, xn, 0, rstd0_ready, 1, xn_ready)
            front_logits(1)
            front_conv(1, 0, 1)
            end_links()
            with dve.Fori(0, B) as i:
                n = dve.snap(i + 1)
                n2 = dve.snap(i + 2)
                ie = dve.snap(i * EA)
                iq = dve.snap(i * (EA // 2))
                links[1] = dve.snap(n * DVE_LINKS)
                at = {"e": 0, "m": 0}
                taps = [("l", j) for j in range(1, KL)]
                for j in range(1, KS):
                    taps.insert(2 * j, ("s", j))
                tap_at = [0]

                def expert_unit(k):
                    e, kind = divmod(k, 3)
                    if kind == 1 and e < EA:
                        dve.wait_ge(sg_ready, ie + e + 1)
                        dve.wait_ge(up_ps, ie + e + 1)
                        tt(hx[e % 2][:, :], bank(Ub), sg[e % 2][:, :], ALU.mult).then_inc(h_ready, 1)
                    elif kind == 2 and e > 0 or k == UNITS - 1:
                        d = e - 1
                        if not on_vector(d):
                            return
                        dve.wait_ge(d_ps, ie + d + 1)
                        if d:
                            dve.wait_ge(dacc, iq + d // 2)
                        else:
                            dve.wait_ge(wsc_ready, n)
                        for t in range(NT):
                            s = wsc[:, t, d:d + 1] if d < E else 1.0
                            if d == 0:
                                last = ts(tile(acc, t), tile(bank(Db), t), s, None, ALU.mult)
                            else:
                                last = stt_(tile(acc, t), tile(bank(Db), t), s, tile(acc, t), ALU.mult, ALU.add)
                        last.then_inc(dacc, 1)

                def fir(m):
                    for _ in range(m):
                        if tap_at[0] == len(taps):
                            return
                        kind, lag = taps[tap_at[0]]
                        y, w, last_tap, done = (fs, "fs", KS - 1, fs_ready) if kind == "s" else (fl, "fl", KL - 1, fl_ready)
                        if tap_at[0] == 0:
                            dve.wait_ge(fir0, i * 2 + 2)
                        tap_at[0] += 1
                        ins = stt_(y[:, lag:L], vs[:, 0:L - lag], col(w, last_tap - lag), y[:, lag:L], ALU.mult, ALU.add)
                        if lag == last_tap:
                            ins.then_inc(done, 1)
                        else:
                            link(ins)

                def fill(name, taps_per_unit=0.0, between=None):
                    for u, c in enumerate(FILL[name]):
                        if between is not None:
                            between(u)
                        if c == "e":
                            expert_unit(at[c])
                        else:
                            layer1_step(at[c], i, n)
                        at[c] += 1
                        fir(int((u + 1) * taps_per_unit) - int(u * taps_per_unit))

                fill("start")
                front_topk(n)
                fill("tok0")
                for j, c in enumerate("qk"):
                    dve.wait_ge(sq_ready[c], n)
                    last = v.tensor_reduce(ss[:, j, :], byhead(sq4[1 + j]), X, ALU.add)
                link(last)
                v.reciprocal(ss[:, :, :], ss[:, :, :]).then_inc(ss_ready, 1)
                fill("tok")
                for c in "qk":
                    dve.wait_ge(tok[c], n)
                dve.wait_ge(rn_ready, n)
                for j, (buf, done) in enumerate(((qtok, qn_ready), (ktok, kn_ready))):
                    tt(byhead(buf[:, :]), byhead(buf[:, :]), over(rn[:, j, :], [P, HT, DH]), ALU.mult).then_inc(done, 1)
                fill("norm", 1.0)

                def lower(h):
                    dve.wait_ge(l_ps, i * H + h + 1)
                    tt(LT[:, h * NT:(h + 1) * NT, :], bank((C0, C1, C2, C0)[h]).rearrange("p (t s) -> p t s", t=NT),
                       con("strict").unsqueeze(1).to_broadcast([P, NT, P]), ALU.mult).then_inc(lt_ready, 1)

                for h in (0, 1, 2):
                    lower(h)
                fill("L", 1.0)
                lower(3)
                fill("L3", 1.0)
                chunks = "p (a j) -> p a j"

                def masked(b, l):
                    a = CONS["lvl"][0] + l * CH
                    link(tt(Yi[:, :].rearrange(chunks, j=CH), bank(b).rearrange(chunks, j=CH),
                            cn[:, a:a + CH].unsqueeze(1).to_broadcast([P, HT, CH]), ALU.mult))

                def transposed(l, c):
                    if c >= P // CH:
                        return
                    if c == 0:
                        dve.wait_ge(xi_ready, i * LEVELS + l)
                    r = slice(CH * c, CH * c + CH)
                    v.transpose(Tbd[r, :, CH * c:CH * c + CH], Xi[r, :].rearrange(chunks, j=CH)).then_inc(tbd_ready, 1)

                dve.wait_ge(tbd_clear, 1)
                dve.wait_ge(y_ps, i * LEVELS + 1)
                masked(C1, 0)
                tt(Xi[:, :].rearrange(chunks, j=CH), con("eye").unsqueeze(1).to_broadcast([P, HT, CH]),
                   Yi[:, :].rearrange(chunks, j=CH), ALU.subtract).then_inc(xi_ready, 1)
                fill("A", 1.0)
                for l in range(1, LEVELS):
                    units = len(FILL[f"lv{l}a"])
                    fill(f"lv{l}a", 1.0, lambda u: transposed(l, u))
                    for c in range(units, P // CH):
                        transposed(l, c)
                    fill(f"lv{l}b", 1.0)
                    dve.wait_ge(z_ps, i * (LEVELS - 1) + l)
                    masked(C2, l)
                    tt(Xi[:, :], Xi[:, :], Yi[:, :], ALU.subtract).then_inc(xi_ready, 1)
                for c in range(P // CH):
                    transposed(LEVELS, c)
                fill("inv", 1.0)
                fill("uw")
                layer1_late(0, i, n)
                srcs = (lstok, lltok, dl, vtok)

                def branch_stat(j, kind):
                    if kind == 0:
                        if j < 2:
                            dve.wait_ge((ls_ready, ll_ready)[j], n)
                        v.tensor_reduce(st_s[:, :, j, :], tilehead(srcs[j][:, :]), X, ALU.add)
                    elif kind == 1:
                        v.tensor_reduce(st_a[:, :, j, :], tilehead(srcs[j][:, :]), X, ALU.add, apply_absolute_value=True)
                    else:
                        dve.wait_ge(sq4_ready, i * 4 + (3, 2, 0, 1).index(j) + 1)
                        v.tensor_reduce(st_q[:, :, j, :], tilehead(sq4[j]), X, ALU.add).then_inc(stq_ready, 1)

                def branch_stats(js, a, units):
                    todo = [(j, kind) for j in js for kind in range(3)]
                    for j, kind in todo[a * len(todo) // units:(a + 1) * len(todo) // units]:
                        branch_stat(j, kind)

                dve.wait_ge(u_ready, n)
                for c in range(NCH):
                    t, g = divmod(c, NT)
                    r = slice(CH * g, CH * g + CH)
                    wrow = 2 * CH * (c % 2)
                    dve.wait_ge(ws_ps, i * NCH + c + 1)
                    tt(tile(uadj, t)[r, :], tile(U, t)[r, :], ps[wrow:wrow + CH, C0, 0:P], ALU.subtract).then_inc(uadj_ready, 1)
                    busy = c < 5
                    fill(f"sc{c}a", 0.0 if busy else 1.0)
                    if c < NCH - 1:
                        dve.wait_ge(s_ps, i * (NCH - 1) + c + 1)
                        tt(Sbd[:, :], ps[:, C1, 0:P], con("bd"), ALU.mult).then_inc(s_ready, 1)
                    if FILL[f"sc{c}a"] == "m":
                        layer1_late(at["m"] - 1, i, n)
                    if c % 4 == 1:
                        h = c // 4
                        dve.wait_ge(a_ps, i * H + h + 1)
                        tt(AT[:, h * NT:(h + 1) * NT, :], bank(C2).rearrange("p (t s) -> p t s", t=NT),
                           con("causal").unsqueeze(1).to_broadcast([P, NT, P]), ALU.mult).then_inc(at_ready, 1)
                    fill(f"sc{c}b", 0.0 if busy else 1.0)
                    if c == 9:
                        branch_stats((3,), 0, 1)
                    if c == 11:
                        dve.wait_ge(x_loaded, 16 * n2)
                        norm_stats(xin, 0, vr0_ready)
                fir(len(taps))
                dve.wait_ge(au_ps, n)
                dve.wait_ge(dq_ready, i * NCH + NCH)
                tt(dl[:, :], bank(C2), dq[:, :], ALU.add).then_inc(dl_ready, 1)
                dve.wait_ge(dl_ready, n)
                units = len(FILL["au"]) + len(FILL["fir"])
                fill("au", 0.0, lambda u: branch_stats((2, 0, 1), u, units))
                fill("fir", 0.0, lambda u: branch_stats((2, 0, 1), u + len(FILL["au"]), units))
                dve.wait_ge(stq_ready, i * 4 + 4)
                link(ts(stat(0), flat(st_s[:, :, :, :]), 1.0 / DH, None, ALU.mult))
                link(tt(m2_c[:, :, :], stat(0), stat(0), ALU.mult))
                stt_(stat(1), flat(st_q[:, :, :, :]), 1.0 / DH, m2_c[:, :, :], ALU.mult, ALU.subtract)
                ts(stat(2), flat(st_a[:, :, :, :]), 1.0 / DH, None, ALU.mult).then_inc(stats_ready, 1)
                fill("st")
                fill("hid")
                norm_apply(xin, xn, 0, rstd0_ready, n2, xn_ready)
                dve.wait_ge(lgt_ps, n)
                link(stt_(lgx[:, :, :], ps[:, C1, 0:HT * 4].rearrange("p (a k) -> p a k", k=4), invt[:, :],
                          b2t[:, :].unsqueeze(1).to_broadcast([P, HT, 4]), ALU.mult, ALU.add))
                link(v.tensor_reduce(lmx[:, :], lgx[:, :, :], X, ALU.max))
                tt(lgx[:, :, :], lgx[:, :, :], over(lmx[:, :], [P, HT, 4]), ALU.subtract).then_inc(lgx_ready, 1)
                fill("lgt")
                dve.wait_ge(fe_ready, n)
                link(v.tensor_reduce(fsum[:, :], fe[:, :, :], X, ALU.add))
                link(v.reciprocal(fsum[:, :], fsum[:, :]))
                link(tt(fw[:, :, :], fe[:, :, :], over(fsum[:, :], [P, HT, 4]), ALU.mult))
                ts(fw[:, :, 0], fw[:, :, 0], col("rss"), None, ALU.add)
                ts(fw[:, :, 1], fw[:, :, 1], col("rsl"), None, ALU.add).then_inc(fw_ready, 1)
                dve.wait_ge(fw_ready, n)
                for j in (0, 1):
                    last = tt(byhead(pr[j]), byhead(srcs[j][:, :]), over(fw[:, :, j], [P, HT, DH]), ALU.mult)
                link(last)
                link(tt(o[:, :], pr[0], pr[1], ALU.add))
                dve.wait_ge(p23_ready, n)
                tt(o[:, :], o[:, :], pr[2], ALU.add).then_inc(o_sum, 1)
                front_logits(n2)
                fill("front1")
                early = len(FILL["front2"])
                conv_units = early + len(FILL["oT"])
                dve.wait_ge(osq_ready, n)
                link(v.tensor_reduce(ms[:, :], byhead(osq[:, :]), X, ALU.add))
                ts(ms[:, :], ms[:, :], 1.0 / DH, RMS_EPS, ALU.mult, ALU.add).then_inc(ms_ready, 1)
                fill("front2", 0.0, lambda u: front_conv(n2, u, conv_units))
                dve.wait_ge(rms_ready, n)
                tt(byhead(o[:, :]), byhead(o[:, :]), over(rms[:, :], [P, HT, DH]), ALU.mult).then_inc(on_ready, 1)
                fill("oT", 0.0, lambda u: front_conv(n2, early + u, conv_units))
                dve.wait_ge(sp_ps, n)
                dve.wait_ge(gs_ready, n)
                dve.wait_ge(x_copied, n)
                link(tt(x1[:, :], bank(C2), gs[:, :], ALU.mult))
                tt(x1[:, :], x1[:, :], xt[:, :], ALU.add).then_inc(x1_ready, 1)
                dve.wait_ge(x1_ready, n2)
                end_links()
            links[1] = (B + 1) * DVE_LINKS
            for k in range(STEPS):
                layer1_step(k, B, B + 1)
                layer1_late(k, B, B + 1)

        @block.gpsimd
        def _(pool):
            g = nc.gpsimd
            tt = g.tensor_tensor
            g.memset(Tbd[:, :, :], 0.0).then_inc(tbd_clear, 1)

            def rsqrt(dst, src):
                return tt(dst, src, unit[:, 1:2].to_broadcast(list(dst.shape)), ALU.pow)

            def layer1_step(k, i, n):
                if k == 0:
                    pool.wait_ge(vr1_ready, n)
                    rsqrt(rstd[1][:, :], vr[1][:, :]).then_inc(rstd1_ready, 1)
                elif k == 9:
                    pool.wait_ge(pj_act, i * 6 + 5)
                    tt(kt[:, :], al[:, :], kt[:, :], ALU.mult).then_inc(ak_ready, 1)
                    pool.wait_ge(ak_ready, n)
                    tt(uu[:, :], kt[:, :], vv[:, :], ALU.mult).then_inc(uu_ready, 1)
                elif k == 11:
                    pool.wait_ge(st_ready, n)
                    tt(mixed[:, :], rg[:, :], stt[:, :], ALU.mult).then_inc(mixed_ready, 1)
                elif k == 17:
                    pool.wait_ge(mn_ready, n)
                    pool.wait_ge(pj_act, i * 6 + 6)
                    tt(mg[:, :], cen[:, :], gg[:, :], ALU.mult).then_inc(mg_ready, 1)

            pool.wait_ge(s_w, 16 * 5)
            pool.wait_ge(unit_ready, 1)
            pool.wait_ge(vr0_ready, 1)
            rsqrt(rstd[0][:, :], vr[0][:, :]).then_inc(rstd0_ready, 1)
            with pool.Fori(0, B) as i:
                n = pool.snap(i + 1)
                n2 = pool.snap(i + 2)
                iq = pool.snap(i * (EA // 2))
                at = {"e": 0, "m": 0}

                def expert_unit(k):
                    e, kind = divmod(k, 3)
                    if kind == 2 and e > 0 or k == UNITS - 1:
                        d = e - 1
                        if on_vector(d):
                            return
                        if d < EA - 1:
                            pool.wait_ge(dt_ready, iq + d // 2 + 1)
                        if d == 1:
                            tt(accp[:, :], dt[:, :], unit[:, 0:1].to_broadcast([P, L]), ALU.add).then_inc(pacc, 1)
                        else:
                            pool.wait_ge(pacc, iq + d // 2)
                            if d == EA - 1:
                                pool.wait_ge(dacc, iq + EA // 2)
                                tt(accp[:, :], accp[:, :], acc[:, :], ALU.add).then_inc(asum_one, 1)
                                pool.wait_ge(asum_one, n)
                                pool.wait_ge(dt_ready, iq + EA // 2)
                            last = tt(accp[:, :], accp[:, :], dt[:, :], ALU.add)
                            last.then_inc(pacc, 1)

                def fill(name):
                    for c in FILL[name]:
                        if c == "e":
                            expert_unit(at[c])
                        else:
                            layer1_step(at[c], i, n)
                        at[c] += 1

                def per_head(dst, src, scale, done):
                    tt(byhead(dst[:, :]), byhead(src[:, :]), scale.unsqueeze(2).to_broadcast([P, HT, DH]), ALU.mult).then_inc(done, 1)

                betas = beta[:, :, :].rearrange("p t h -> p (t h)")
                fill("start")
                pool.wait_ge(beta_ready, n)
                pool.wait_ge(tok["v"], n)
                per_head(vb, vtok, betas, vb_ready)
                fill("tok0")
                fill("tok")
                pool.wait_ge(kn_ready, n)
                per_head(kb, ktok, betas, kb_ready)
                g.memset(Sbd[:, :], 0.0).then_inc(s0_ready, 1)
                for name in ["norm", "L", "L3", "A"] + [f"lv{l}{ab}" for l in range(1, LEVELS) for ab in "ab"] + ["inv"]:
                    fill(name)
                squares = lambda j, src: tt(sq4[j], src[:, :], src[:, :], ALU.mult).then_inc(sq4_ready, 1)
                pool.wait_ge(y_ps, i * LEVELS + LEVELS)
                squares(3, vtok)
                fill("uw")
                for c in range(NCH):
                    fill(f"sc{c}a")
                    fill(f"sc{c}b")
                    if c == 12:
                        pool.wait_ge(vr0_ready, n2)
                        rsqrt(rstd[0][:, :], vr[0][:, :]).then_inc(rstd0_ready, 1)
                for j, src, ready in ((2, dl, dl_ready), (0, lstok, ls_ready), (1, lltok, ll_ready)):
                    pool.wait_ge(ready, n)
                    squares(j, src)
                fill("au")
                fill("fir")
                fill("st")
                fill("hid")
                fill("lgt")
                pool.wait_ge(fw_ready, n)
                for j, src in ((2, dl), (3, vtok)):
                    last = tt(byhead(pr[j]), byhead(src[:, :]), fw[:, :, j].unsqueeze(2).to_broadcast([P, HT, DH]), ALU.mult)
                last.then_inc(p23_one, 1)
                pool.wait_ge(p23_one, n)
                tt(pr[2], pr[2], pr[3], ALU.add).then_inc(p23_ready, 1)
                pool.wait_ge(o_sum, n)
                tt(osq[:, :], o[:, :], o[:, :], ALU.mult).then_inc(osq_ready, 1)
                fill("front1")
                pool.wait_ge(ms_ready, n)
                rsqrt(rms[:, :], ms[:, :]).then_inc(rms_ready, 1)
                fill("front2")
                fill("oT")
            for k in range(STEPS):
                layer1_step(k, B, B + 1)


def constants():
    p = np.arange(P)
    same = p[:, None] // CH == p[None, :] // CH
    c = np.zeros((P, NCON), np.float32)

    def put(name, a):
        c[:, CONS[name][0]:CONS[name][1]] = a

    put("ident", np.eye(P))
    put("bd", same)
    put("avg", (p[:, None] // 8 == p[None, :] // 8) / 8.0)
    put("strict", same & (p[:, None] < p[None, :]))
    put("causal", same & (p[:, None] <= p[None, :]))
    r, j = p[:, None] % CH, np.arange(CH)[None, :]
    put("eye", r == j)
    put("lvl", np.concatenate([(r // (2 * s) == j // (2 * s)) & (r // s % 2 == 1) & (j // s % 2 == 0)
                               for s in (1 << l for l in range(LEVELS))], axis=1))
    return c


def kernel(**inputs):
    import concourse.bacc as _bacc
    from concourse.bass_utils import run_bass_kernel_spmd as _run

    a = {k: np.asarray(v) for k, v in inputs.items()}
    l0, ff0, l1, ff1 = (lambda k, p=p: a[p + k] for p in ("L0_attn_", "L0_ffn_", "L1_attn_", "L1_ffn_"))

    def rows(vec, n=P):
        return np.broadcast_to(vec.reshape(1, -1), (n, vec.size))

    small = np.zeros((P, NCOL), np.float32)
    for name, val in (("qc", l0("q_conv_w")), ("kc", l0("k_conv_w")), ("vc", l0("v_conv_w")), ("fs", l0("fir_short_w").reshape(D, KS)),
                      ("fl", l0("fir_long_w").reshape(D, KL)), ("b1", l0("fuse_b1").reshape(P, 1)),
                      ("mix", np.stack([l1(f"x_{c}").reshape(D) for c in "rwkvag"], axis=1)),
                      ("gnw", l1("gn_w").reshape(D, 1)), ("gnb", l1("gn_b").reshape(D, 1)),
                      ("s1", ff1("w1_s").reshape(FF, P).T), ("s2", ff1("w2_s").reshape(FF, P).T),
                      ("hs1", ff1("h1_s").reshape(FF, P).T), ("hs2", ff1("h2_s").reshape(FF, P).T),
                      ("temp", rows(l0("logit_temp"))), ("rss", rows(l0("res_scale_short"))), ("rsl", rows(l0("res_scale_long"))),
                      ("b2", rows(l0("fuse_b2"))), ("onorm", np.tile(l0("o_norm_w"), H).reshape(D, 1)), ("rbias", rows(ff0("router_bias"))),
                      ("bout", rows(l1("b_out"))), ("w3s", rows(ff1("w3_s"))), ("w2T", l0("fuse_w2").T)):
        small[:, COLS[name][0]:COLS[name][1]] = val
    w1 = l0("fuse_w1")
    w1s = np.zeros((NST, H, H, P), np.float32)
    for h in range(H):
        w1s[:, h, h, :] = w1[:, D:].T
    arrays = {
        "x": np.concatenate([l0("hidden_states"), np.zeros((1, L, D), np.float32)]),
        "small": small,
        "cons": constants(),
        "wsq": np.stack([l0("q_proj_w").T, l0("k_proj_w").T, l0("v_proj_w").T, w1[:, :D].T, l0("o_proj_w").T]
                        + [l1(f"W_{c}").T for c in ("r", "w", "k", "v", "a", "g", "out")], axis=1),
        "wrb": np.concatenate([ff0("router_w").T, l0("b_proj_w").T], axis=1),
        "w1s": w1s.reshape(4, 4, H, H, P).transpose(1, 0, 2, 3, 4).reshape(NST * H, H, P),
        "moe_g": np.concatenate([ff0("gate_w").transpose(2, 0, 1), ff0("sgate_w").T.reshape(D, ES, P)], axis=1),
        "moe_u": np.concatenate([ff0("up_w").transpose(2, 0, 1), ff0("sup_w").T.reshape(D, ES, P)], axis=1),
        "moe_d": np.concatenate([ff0("down_w").transpose(2, 0, 1), ff0("sdown_w").T.reshape(ES, P, D).transpose(1, 0, 2)], axis=1),
        "f1": ff1("w1_w").T.reshape(D, FF, P),
        "f2": ff1("w2_w").T.reshape(D, FF, P),
        "h1w": ff1("h1_w").T.reshape(FF, P, FF * P).transpose(1, 0, 2),
        "h2w": ff1("h2_w").T.reshape(FF, P, FF * P).transpose(1, 0, 2),
        "w3": ff1("w3_w").T.reshape(FF, P, D).transpose(1, 0, 2),
    }
    arrays = {k: np.ascontiguousarray(v) for k, v in arrays.items()}
    nc = _bacc.Bacc("TRN2", target_bir_lowering=False, num_devices=1)
    args = [nc.dram_tensor(k, v.shape, mybir.dt.float32, kind="ExternalInput").ap() for k, v in arrays.items()]
    args.append(nc.dram_tensor("out", (B, L, D), mybir.dt.float32, kind="ExternalOutput").ap())
    build(nc, *args)
    r = _run(nc, [arrays], core_ids=[0])
    return r.results[0]["out"]
```

```python
import numpy as np
import concourse.bass as bass
from concourse import mybir
from contextlib import ExitStack

P = 128
B, L, D = 16, 512, 128
NT = L // P
H = 4
DH = D // H
CH = 32
NCH = L // CH
HT = H * NT
E, TOPK = 32, 4
ES = 4
EA = E + ES
KS, KL, KC = 5, 64, 4
NST = 16
FF = 4
LEVELS = 5
LN_EPS, RMS_EPS, GN_EPS = 1e-5, 1e-5, 0.00064

FILL = {"start": "eeeee", "tok0": "e", "tok": "eeeee", "norm": "eeeee", "L": "ee", "L3": "eee", "A": "eee", "inv": "eeeee", "uw": "meeeme",
        "au": "eeeee", "fir": "eemeee", "st": "eeem", "hid": "eee", "lgT": "e", "lgt": "eee", "front1": "eee", "front2": "eeeee"}
for _l in range(1, LEVELS):
    for _part, _units in (("a", "e"), ("b", "ee"), ("c", "ee"), ("d", "e")):
        FILL[f"lv{_l}{_part}"] = _units
for _c in range(NCH):
    FILL[f"sc{_c}a"] = "m" if _c < 15 else "e"
    FILL[f"sc{_c}b"] = "e"
UNITS = 3 * EA + 1
OFF_VECTOR = (6, 8, 10, 12, 14, 16, 30)
ON_VECTOR = [d for d in range(0, EA, 2) if d not in OFF_VECTOR]
NV = len(ON_VECTOR)
SCAN_TAPS = [0,0,0,0,0,1,1,9,5,7,5,2,1,2,0,0]
STEPS = 19
FILL["oT"] = "e" * (UNITS - sum(f.count("e") for f in FILL.values()))
assert sum(f.count("e") for f in FILL.values()) == UNITS
assert sum(f.count("m") for f in FILL.values()) == STEPS
DVE_LINKS = 192

COLS = {}
_at = 0
for _n, _w in (("qc", KC), ("kc", KC), ("vc", KC), ("fs", KS), ("fl", KL), ("b1", 1), ("mix", 6), ("gnw", 1), ("gnb", 1),
               ("s1", FF), ("s2", FF), ("hs1", FF), ("hs2", FF), ("temp", 1), ("rss", 1), ("rsl", 1), ("b2", 4),
               ("onorm", 1), ("rbias", E), ("bout", D), ("w3s", D), ("w2T", CH)):
    COLS[_n] = (_at, _at + _w)
    _at += _w
NCOL = _at

CONS = {}
_at = 0
for _n, _w in (("ident", P), ("bd", P), ("avg", P), ("strict", P), ("causal", P), ("eye", CH), ("lvl0", CH), ("lvlT", (LEVELS - 1) * CH)):
    CONS[_n] = (_at, _at + _w)
    _at += _w
NCON = _at

WNAMES = ["wq", "wk", "wv", "w1x", "wo", "Wr", "Ww", "Wk", "Wv", "Wa", "Wg", "Wout"]


def build(nc, x, small, cons, wsq, wrb, w1s, moe_g, moe_u, moe_d, f1, f2, h1w, h2w, w3, out):
    f32 = mybir.dt.float32
    ACT = mybir.ActivationFunctionType
    ALU = mybir.AluOpType
    X = mybir.AxisListType.X

    x_v = x.rearrange("b (t p) d -> b p t d", p=P)
    out_v = out.rearrange("b (t p) d -> b p t d", p=P)

    ctx = ExitStack()
    with ctx:
        def sb(name, shape):
            return ctx.enter_context(nc.sbuf_tensor(name, shape, f32))

        def sem(name):
            return ctx.enter_context(nc.semaphore(name))

        sm = sb("sm", [P, NCOL])
        cn = sb("cn", [P, NCON])
        wm = sb("wm", [P, len(WNAMES), D])
        wrb_sb = sb("wrb_sb", [P, E + H])
        w1s_sb = sb("w1s_sb", [NST * H, H, P])
        eg = sb("eg", [P, EA, P])
        eu = sb("eu", [P, EA, P])
        ed = sb("ed", [P, EA, P])
        f1_sb = sb("f1_sb", [P, FF, P])
        f2_sb = sb("f2_sb", [P, FF, P])
        h1_sb = sb("h1_sb", [P, FF, FF * P])
        h2_sb = sb("h2_sb", [P, FF, FF * P])
        w3_sb = sb("w3_sb", [P, FF, D])

        def col(name, j=0, w=1):
            a, b = COLS[name]
            return sm[:, a + j:a + j + w]

        def con(name):
            a, b = CONS[name]
            return cn[:, a:b]

        def weight(name):
            return wm[:, WNAMES.index(name), :]

        ident = con("ident")

        xin = sb("xin", [P, L])
        xt = sb("xt", [P, L])
        xnT = sb("xnT", [P, L])
        vs = sb("vs", [P, L])
        Xi, ks, Yi = sb("Xi", [P, HT * CH]), sb("ks", [P, L]), sb("Yi", [P, HT * CH])
        vtok, qtok, ktok = sb("vtok", [P, L]), sb("qtok", [P, L]), sb("ktok", [P, L])
        vb, kb = sb("vb", [P, L]), sb("kb", [P, L])
        WQ = sb("WQ", [P, NCH, 2 * CH])
        knT, kbT = sb("knT", [P, L]), sb("kbT", [P, L])
        LT, Tbd = sb("LT", [P, HT, P]), sb("Tbd", [P, HT, P])
        U, uadj = sb("U", [P, L]), sb("uadj", [P, L])
        Sbd = sb("Sbd", [P, P])
        fs, fl = sb("fs", [P, L]), sb("fl", [P, L])
        sg = [sb(f"sg{j}", [P, L]) for j in range(2)]
        hx = [sb(f"hx{j}", [P, L]) for j in range(2)]
        dt = sb("dt", [P, L])
        acc, accp = sb("acc", [P, L]), sb("accp", [P, L])
        x1 = sb("x1", [P, L])
        x2 = sb("x2", [P, L])
        quarter = lambda ap, c: ap[:, 4 * c:4 * c + 4, :].rearrange("p a b -> p (a b)")
        sq4 = [quarter(LT, c) for c in range(4)]
        yv, yq, yk = sq4[0], sq4[1], sq4[2]
        qs, xn, xnN, AT, dl, dq = Xi, knT, ks, Tbd, qtok, Yi
        lstok, lltok, gs = kb, vb, kbT
        hdn = [Xi, kbT, Yi, fs]
        WQf = WQ[:, :, :].rearrange("p c k -> p (c k)")
        pr = [WQf[:, 0:L], WQf[:, L:2 * L], fl[:, :], ktok[:, :]]
        o, osq, oT = U, fl, uadj
        statsT = ktok[0:NST * H, :]
        YT, ZT, auT, lgT = U, uadj, U, Xi
        xn1 = sb("xn1", [P, L])
        xn1p = sb("xn1p", [P, L + 4])
        mixd = [sb(f"mixd{j}", [P, L]) for j in range(6)]
        fh = [sb(f"fh{c}", [P, L]) for c in range(FF)]
        rg, dec, kt, al, gg, vv = (sb(n, [P, L]) for n in ("rg", "dec", "kt", "al", "gg", "vv"))
        dT, g1, g2, g2r = xn1, mixd[0:4], fh, rg
        uu, stt, mixed, cen, sqc, rvar, mg, s1 = vv, al, kt, al, vv, dec, mixd[4], mixd[5]

        bst = [sb(f"bst{j}", [P, NT, 6]) for j in range(2)]
        mv = [sb(f"mv{j}", [P, NT, 2]) for j in range(2)]
        vr = [sb(f"vr{j}", [P, NT]) for j in range(2)]
        rstd = [sb(f"rstd{j}", [P, NT]) for j in range(2)]
        lg = sb("lg", [P, NT, E])
        mx = sb("mx", [P, NT])
        sc = sb("sc", [P, NT, E + TOPK])
        ssum = sb("ssum", [P, NT])
        m8 = sb("m8", [P, NT, 8])
        m4 = sb("m4", [P, NT, 8])
        rep = sb("rep", [P, NT, E + TOPK])
        wsc = sb("wsc", [P, NT, E])
        beta = sb("beta", [P, NT, H])
        ss = sb("ss", [P, 2, HT])
        rn = sb("rn", [P, 2, HT])
        st_s, st_a, st_q = (sb(n, [P, NT, 4, H]) for n in ("st_s", "st_a", "st_q"))
        m2_c = sb("m2_c", [P, NT, 4 * H])
        stats = sb("stats", [P, NT, 4, 4, H])
        lgx = sb("lgx", [P, HT, 4])
        lmx = sb("lmx", [P, HT])
        fe = sb("fe", [P, HT, 4])
        fsum = sb("fsum", [P, HT])
        fw = sb("fw", [P, HT, 4])
        ms = sb("ms", [P, HT])
        rms = sb("rms", [P, HT])
        spare = sb("spare", [P, 2])
        unit = sb("unit", [P, 2])
        tmp1 = sb("tmp1", [P, 4])
        invt = sb("invt", [P, 1])
        b2t = sb("b2t", [P, 4])

        ps = ctx.enter_context(nc.psum_tensor("ps", [P, 8, L], f32))
        G, Ub, Db, M0, M1, C0, C1, C2 = range(8)

        def bank(b):
            return ps[:, b, :]

        def tile(ap, t):
            return ap[:, t * P:(t + 1) * P]

        def byhead(ap):
            return ap.rearrange("p (a d) -> p a d", d=DH)

        def tilehead(ap):
            return ap.rearrange("p (t h d) -> p t h d", h=H, d=DH)

        def flat(ap):
            return ap.rearrange("p t j h -> p t (j h)")

        def stat(s):
            return flat(stats[:, :, s, :, :])

        def on_vector(d):
            return d in ON_VECTOR

        def before(d):
            return sum(on_vector(j) == on_vector(d) for j in range(d))

        s_w = sem("weights_loaded")
        s_moe = [sem(f"expert_weights_loaded{j}") for j in range(3)]
        s_l1 = sem("layer1_weights_loaded")
        unit_ready = sem("unit_ready")
        temp_ready, tbd_clear = sem("temp_ready"), sem("tbd_clear")
        x_loaded, x_copied, x1_ready, x2_ready, x2_stored = sem("x_loaded"), sem("x_copied"), sem("x1_ready"), sem("x2_ready"), sem("x2_stored")
        xnT_ready = sem("xnT_ready")
        vr0_ready, rstd0_ready, xn_ready, xT_ps, xnN_ready = sem("vr0_ready"), sem("rstd0_ready"), sem("xn_ready"), sem("xT_ps"), sem("xnN_ready")
        proj, tap, conv, silu = (sem(n) for n in ("proj", "tap", "conv", "silu"))
        tok_ps = {c: sem(f"tok_ps_{c}") for c in "vqk"}
        tok = {c: sem(f"tok_{c}") for c in "vqk"}
        rb_ps, rb_read, beta_ready, lgs_ready, ex_ready, rep_ready, wsc_ready = sem("rb_ps"), sem("rb_read"), sem("beta_ready"), sem("lgs_ready"), sem("ex_ready"), sem("rep_ready"), sem("wsc_ready")
        sq_ready = {c: sem(f"sq_{c}") for c in "qk"}
        ss_ready, rn_ready, qn_ready, kn_ready, kb_ready, vb_ready = (sem(n) for n in ("ss_ready", "rn_ready", "qn_ready", "kn_ready", "kb_ready", "vb_ready"))
        nT_ps = {c: sem(f"nT_ps_{c}") for c in "qkb"}
        nT = {c: sem(f"nT_{c}") for c in "qkb"}
        l_ps, lt_ready, a_ps, at_ready = sem("l_ps"), sem("lt_ready"), sem("a_ps"), sem("at_ready")
        xi_ready, tbd_ready = sem("xi_ready"), sem("tbd_ready")
        yT_ps, yT_ready, y_ps, y_ready, zT_ps, zT_ready, z_ps = (sem(n) for n in ("yT_ps", "yT_ready", "y_ps", "y_ready", "zT_ps", "zT_ready", "z_ps"))
        u_ps, wt_ps, u_ready, wt_ready, s0_ready = sem("u_ps"), sem("wt_ps"), sem("u_ready"), sem("wt_ready"), sem("s0_ready")
        ws_ps, uadj_ready, dq_ready = sem("ws_ps"), sem("uadj_ready"), sem("dq_ready")
        s_ps, s_ready = sem("s_ps"), sem("s_ready")
        auT_ps, auT_ready, au_ps, dl_ready = sem("auT_ps"), sem("auT_ready"), sem("au_ps"), sem("dl_ready")
        fir0 = sem("fir0")
        fs_ready, fl_ready, fsT_ps, flT_ps, ls_ready, ll_ready = (sem(n) for n in ("fs_ready", "fl_ready", "fsT_ps", "flT_ps", "ls_ready", "ll_ready"))
        sq4_ready = sem("sq4_ready")
        stq_ready, l2_ready, stats_ready, stT_ps, stT_ready = (sem(n) for n in ("stq_ready", "l2_ready", "stats_ready", "stT_ps", "stT_ready"))
        hid_ps, hdn_ready = sem("hid_ps"), sem("hdn_ready")
        lgT_ps, lgT_ready, lgt_ps, lgx_ready, fe_ready, fw_ready, p3_ready, o_sum, osq_ready, ms_ready, rms_ready, on_ready, oT_ps, oT_ready, sp_ps = (
            sem(n) for n in ("lgT_ps", "lgT_ready", "lgt_ps", "lgx_ready", "fe_ready", "fw_ready", "p3_ready", "o_sum", "osq_ready", "ms_ready", "rms_ready", "on_ready", "oT_ps", "oT_ready", "sp_ps"))
        asum_one, gs_ready = sem("asum_one"), sem("gs_ready")
        g_ps, up_ps, d_ps, sg_ready, h_ready, dacc, dt_ready, pacc = (sem(n) for n in ("g_ps", "up_ps", "d_ps", "sg_ready", "h_ready", "dacc", "dt_ready", "pacc"))
        vr1_ready, rstd1_ready, xn1_ready, x1T_ps, x1T_ready = (sem(n) for n in ("vr1_ready", "rstd1_ready", "xn1_ready", "x1T_ps", "x1T_ready"))
        ffg_ps, ffu_ps, sgf_ready, fh_ready, h1_ps, g1_ready, h2_ps, g2_ready = (sem(n) for n in ("ffg_ps", "ffu_ps", "sgf_ready", "fh_ready", "h1_ps", "g1_ready", "h2_ps", "g2_ready"))
        mix_ready, pj_ps, pj_act = sem("mix_ready"), sem("pj_ps"), sem("pj_act")
        ak_ready, uu_ready, st_ready, mixed_ready, mu_ps, cen_ready, sqc_ready, var_ps, vare_ready, rvar_ready, rsd_ready, mn_ready, mg_ready, op_ps, w3_ps, g2r_ready, g2s_ready = (
            sem(n) for n in ("ak_ready", "uu_ready", "st_ready", "mixed_ready", "mu_ps", "cen_ready", "sqc_ready", "var_ps", "vare_ready", "rvar_ready", "rsd_ready", "mn_ready", "mg_ready", "op_ps", "w3_ps", "g2r_ready", "g2s_ready"))
        sp_read, rows_ready = sem("sp_read"), sem("rows_ready")
        dve_link = sem("dve_link")

        block = ctx.enter_context(nc.Block())

        @block.sync
        def _(sp):
            xin_v = xin[:, :].rearrange("p (t d) -> p t d", d=D)
            x2_v = x2[:, :].rearrange("p (t d) -> p t d", d=D)
            sp.dma_start(xin_v, x_v[0]).then_inc(x_loaded, 16)
            for dst, src in ((sm[:, :], small), (cn[:, :], cons), (wm[:, :, :], wsq), (wrb_sb[:, :], wrb), (w1s_sb[:, :, :], w1s)):
                sp.dma_start(dst, src).then_inc(s_w, 16)
            for e0 in range(0, EA, 12):
                for dst, src in ((eg, moe_g), (eu, moe_u), (ed, moe_d)):
                    sp.dma_start(dst[:, e0:e0 + 12, :], src[:, e0:e0 + 12, :]).then_inc(s_moe[e0 // 12], 16)
            for dst, src in ((f1_sb, f1), (f2_sb, f2), (h1_sb, h1w), (h2_sb, h2w), (w3_sb, w3)):
                sp.dma_start(dst[:, :, :], src).then_inc(s_l1, 16)
            sp.wait_ge(x_copied, 1)
            sp.dma_start(xin_v, x_v[1]).then_inc(x_loaded, 16)
            with sp.Fori(1, B) as i:
                n = sp.snap(i + 1)
                sp.wait_ge(x_copied, n)
                sp.dma_start(xin_v, x_v[bass.ds(n, 1), :, :, :].rearrange("b p t d -> p (b t) d")).then_inc(x_loaded, 16)
                sp.wait_ge(x2_ready, n)
                sp.dma_start(out_v[bass.ds(i - 1, 1), :, :, :].rearrange("b p t d -> p (b t) d"), x2_v).then_inc(x2_stored, 16)
            sp.wait_ge(x2_ready, B + 1)
            sp.dma_start(out_v[B - 1], x2_v).then_inc(x2_stored, 16)
            sp.wait_ge(x2_stored, 16 * (B + 2))

        @block.tensor
        def _(pe):
            mm = nc.tensor.matmul

            def transposes(b, src, done, w=P):
                for t in range(NT):
                    last = nc.tensor.transpose(ps[0:w, b, t * P:(t + 1) * P], src[:, t * w:(t + 1) * w], ident)
                last.then_inc(done, 1)

            def front_x(m):
                pe.wait_ge(xn_ready, m)
                transposes(M0, xn, xT_ps)

            def front_router(m):
                pe.wait_ge(xnN_ready, m)
                for t in range(NT):
                    last = mm(ps[:, M1, t * (E + H):(t + 1) * (E + H)], tile(xnN, t), wrb_sb[:, :], start=True, stop=True)
                last.then_inc(rb_ps, 1)

            def front_proj(m):
                pe.wait_ge(rb_read, m)
                for c, b, w in (("v", C1, "wv"), ("q", M0, "wq"), ("k", M1, "wk")):
                    mm(bank(b), weight(w), xnN[:, :], start=True, stop=True).then_inc(proj, 1)

            def layer1_step(k, i, n):
                x1T = xn1p[:, 4:4 + L]

                def hidden(b, w_sb, src, c, done):
                    for kk in range(FF):
                        last = mm(bank(b), w_sb[:, kk, c * P:(c + 1) * P], src[kk][:, :], start=(kk == 0), stop=(kk == FF - 1))
                    last.then_inc(done, 1)

                if k == 1:
                    pe.wait_ge(xn1_ready, n)
                    transposes(M0, xn1, x1T_ps)
                elif 2 <= k <= 5:
                    c = k - 2
                    if c == 0:
                        pe.wait_ge(s_l1, 16 * 5)
                        pe.wait_ge(x1T_ready, n)
                    else:
                        pe.wait_ge(sgf_ready, i * FF + c)
                    mm(bank(M0), f1_sb[:, c, :], x1T, start=True, stop=True).then_inc(ffg_ps, 1)
                    if c:
                        pe.wait_ge(fh_ready, i * FF + c)
                    mm(bank(M1), f2_sb[:, c, :], x1T, start=True, stop=True).then_inc(ffu_ps, 1)
                elif 6 <= k <= 8:
                    for j, b, w in (((0, M0, "Wr"), (1, M1, "Ww")), ((2, M0, "Wk"), (3, M1, "Wv")), ((4, M0, "Wa"), (5, M1, "Wg")))[k - 6]:
                        if k == 6:
                            pe.wait_ge(fh_ready, i * FF + FF)
                        else:
                            pe.wait_ge(pj_act, i * 6 + j - 1)
                        pe.wait_ge(mix_ready, i * 6 + j + 1)
                        mm(bank(b), weight(w), mixd[j][:, :], start=True, stop=True).then_inc(pj_ps, 1)
                elif k in (9, 10):
                    for c, b in ((2 * k - 18, M0), (2 * k - 17, M1)):
                        if k == 9:
                            pe.wait_ge(pj_act, i * 6 + 5 + c)
                        else:
                            pe.wait_ge(g1_ready, i * FF + c - 1)
                        hidden(b, h1_sb, fh, c, h1_ps)
                elif k == 11:
                    pe.wait_ge(g1_ready, i * FF + FF)
                    hidden(M0, h2_sb, g1, 0, h2_ps)
                    hidden(M1, h2_sb, g1, 1, h2_ps)
                elif k == 12:
                    pe.wait_ge(g2_ready, i * FF + 1)
                    pe.wait_ge(mixed_ready, n)
                    mm(bank(M0), con("avg"), mixed[:, :], start=True, stop=True).then_inc(mu_ps, 1)
                    pe.wait_ge(g2_ready, i * FF + 2)
                    hidden(M1, h2_sb, g1, 2, h2_ps)
                elif k == 13:
                    pe.wait_ge(g2_ready, i * FF + 3)
                    hidden(M1, h2_sb, g1, 3, h2_ps)
                elif k == 14:
                    pe.wait_ge(sqc_ready, n)
                    mm(bank(M0), con("avg"), sqc[:, :], start=True, stop=True).then_inc(var_ps, 1)
                elif k in (15, 16):
                    pe.wait_ge(g2_ready, i * FF + FF)
                    for t in ((0, 1), (2, 3))[k - 15]:
                        for kk in range(FF):
                            last = mm(tile(bank(M1), t), g2[kk][:, t * P:(t + 1) * P], w3_sb[:, kk, :], start=(kk == 0), stop=(kk == FF - 1))
                    last.then_inc(w3_ps, 1)
                elif k == 17:
                    pe.wait_ge(mg_ready, n)
                    for t in range(NT):
                        last = mm(tile(bank(M0), t), tile(mg, t), weight("Wout"), start=True, stop=True)
                    last.then_inc(op_ps, 1)

            pe.wait_ge(s_w, 16 * 5)
            front_x(1)
            front_router(1)
            front_proj(1)
            with pe.Fori(0, B) as i:
                n = pe.snap(i + 1)
                n2 = pe.snap(i + 2)
                ie = pe.snap(i * EA)
                iv, ia = pe.snap(i * NV), pe.snap(i * (EA - NV))
                at = {"e": 0, "m": 0}

                def expert_unit(k):
                    e, kind = divmod(k, 3)
                    if kind == 0 and e < EA:
                        if e % 12 == 0:
                            pe.wait_ge(s_moe[e // 12], 16 * 3)
                        if e:
                            pe.wait_ge(sg_ready, ie + e)
                        else:
                            pe.wait_ge(xnT_ready, n)
                        mm(bank(G), eg[:, e, :], xnT[:, :], start=True, stop=True).then_inc(g_ps, 1)
                    elif kind == 1:
                        if e:
                            pe.wait_ge(h_ready, ie + e)
                        mm(bank(Ub), eu[:, e, :], xnT[:, :], start=True, stop=True).then_inc(up_ps, 1)
                    elif e > 0 or kind == 0:
                        d = e - 1
                        pe.wait_ge(h_ready, ie + d + 1)
                        if d:
                            pe.wait_ge(*((dacc, iv + before(d - 1) + 1) if on_vector(d - 1) else (dt_ready, ia + before(d - 1) + 1)))
                        for t in range(NT):
                            last = mm(tile(bank(Db), t), tile(hx[d % 2], t), ed[:, d, :], start=True, stop=True)
                        last.then_inc(d_ps, 1)

                def fill(name):
                    for c in FILL[name]:
                        if c == "e":
                            expert_unit(at[c])
                        else:
                            layer1_step(at[c], i, n)
                        at[c] += 1

                fill("start")
                for c, b, src in (("v", C1, vs), ("q", C2, qs), ("k", C0, ks)):
                    pe.wait_ge(silu, i * 3 + 1 + "vqk".index(c))
                    if b == C2:
                        pe.wait_ge(sp_read, n)
                    transposes(b, src, tok_ps[c])
                fill("tok0")
                fill("tok")
                for c, b, src, ready in (("q", C2, qtok, qn_ready), ("k", C0, ktok, kn_ready), ("b", C1, kb, kb_ready)):
                    pe.wait_ge(ready, n)
                    transposes(b, src, nT_ps[c])
                fill("norm")
                for c in "qkb":
                    pe.wait_ge(nT[c], n)
                for h in range(H):
                    r = slice(DH * h, DH * h + DH)
                    if h == 3:
                        fill("L")
                        pe.wait_ge(lt_ready, i * H + 1)
                    for t in range(NT):
                        last = mm(tile(bank((C0, C1, C2, C0)[h]), t), tile(knT, t)[r, :], tile(kbT, t)[r, :], start=True, stop=True)
                    last.then_inc(l_ps, 1)
                fill("L3")
                fill("A")
                quads = [(a, slice(CH * (a % NT), CH * (a % NT) + CH), a // NT) for a in range(HT)]
                for l in range(1, LEVELS):
                    fill(f"lv{l}a")
                    pe.wait_ge(xi_ready, i * LEVELS + l)
                    for a, r, q in quads:
                        last = mm(tile(bank(C1), q)[r, :], Xi[:, a * CH:(a + 1) * CH], LT[:, a, :], start=True, stop=True)
                    last.then_inc(yT_ps, 1)
                    fill(f"lv{l}b")
                    pe.wait_ge(yT_ready, i * (LEVELS - 1) + l)
                    transposes(C2, YT, y_ps)
                    fill(f"lv{l}c")
                    pe.wait_ge(y_ready, i * (LEVELS - 1) + l)
                    pe.wait_ge(tbd_ready, (i * LEVELS + l) * (P // CH))
                    for a, r, q in quads:
                        last = mm(tile(bank(C0), q)[r, :], Yi[:, a * CH:(a + 1) * CH], Tbd[:, a, :], start=True, stop=True)
                    last.then_inc(zT_ps, 1)
                    fill(f"lv{l}d")
                    pe.wait_ge(zT_ready, i * (LEVELS - 1) + l)
                    transposes(C2, ZT, z_ps)
                fill("inv")
                pe.wait_ge(tbd_ready, (i * LEVELS + LEVELS) * (P // CH))
                pe.wait_ge(vb_ready, n)
                for h in range(H):
                    for t in range(NT):
                        c = slice(t * P + DH * h, t * P + DH * h + DH)
                        last = mm(ps[:, C0, c], Tbd[:, h * NT + t, :], vb[:, c], start=True, stop=True)
                last.then_inc(u_ps, 1)
                for h in range(H):
                    for t in range(NT):
                        c = slice(t * P + DH * h, t * P + DH * h + DH)
                        last = mm(ps[DH * h:DH * h + DH, C2, t * P:(t + 1) * P], kb[:, c], Tbd[:, h * NT + t, :], start=True, stop=True)
                last.then_inc(wt_ps, 1)
                fill("uw")
                pe.wait_ge(u_ready, n)
                pe.wait_ge(wt_ready, n)
                for c in range(NCH):
                    t, g = divmod(c, NT)
                    r = slice(CH * g, CH * g + CH)
                    if c == 0:
                        pe.wait_ge(s0_ready, n)
                    else:
                        pe.wait_ge(s_ready, i * (NCH - 1) + c)
                    if c >= 2:
                        pe.wait_ge(dq_ready, i * NCH + c - 1)
                    half = slice(2 * CH * (c % 2), 2 * CH * (c % 2) + 2 * CH)
                    mm(ps[half, C0, 0:P], WQ[:, c, :], Sbd[:, :], start=True, stop=True).then_inc(ws_ps, 1)
                    fill(f"sc{c}a")
                    if c % 4 == 1:
                        h = c // 4
                        if h:
                            pe.wait_ge(at_ready, i * H + h)
                        rh = slice(DH * h, DH * h + DH)
                        for tt_ in range(NT):
                            last = mm(tile(bank(C2), tt_), tile(knT, tt_)[rh, :], WQ[rh, NT * tt_:NT * tt_ + NT, CH:2 * CH], start=True, stop=True)
                        last.then_inc(a_ps, 1)
                    if c < NCH - 1:
                        pe.wait_ge(uadj_ready, i * NCH + c + 1)
                        mm(ps[:, C1, 0:P], tile(ktok, t)[r, :], tile(uadj, t)[r, :], start=(c == 0), stop=True, skip_group_check=True).then_inc(s_ps, 1)
                    fill(f"sc{c}b")
                pe.wait_ge(uadj_ready, i * NCH + NCH)
                pe.wait_ge(at_ready, i * H + H)
                for h in range(H):
                    for t in range(NT):
                        c = slice(t * P + DH * h, t * P + DH * h + DH)
                        last = mm(tile(bank(C2), t)[DH * h:DH * h + DH, :], uadj[:, c], AT[:, h * NT + t, :], start=True, stop=True)
                last.then_inc(auT_ps, 1)
                pe.wait_ge(fs_ready, n)
                pe.wait_ge(dq_ready, i * NCH + NCH)
                transposes(C0, fs, fsT_ps)
                pe.wait_ge(fl_ready, n)
                transposes(C1, fl, flT_ps)
                pe.wait_ge(auT_ready, n)
                transposes(C2, auT, au_ps)
                fill("au")
                fill("fir")
                HB = (C0, C1, C2, C0)
                pe.wait_ge(ls_ready, n)
                mm(bank(HB[0]), weight("w1x"), xnT[:, :], start=True, stop=False)
                pe.wait_ge(ll_ready, n)
                mm(ps[:, HB[1], 0:L - P], weight("w1x"), xnT[:, 0:L - P], start=True, stop=False)
                pe.wait_ge(stats_ready, n)
                pe.wait_ge(l2_ready, n)
                mm(ps[:, HB[1], L - P:L], weight("w1x"), xnT[:, L - P:L], start=False, stop=False)
                transposes(C2, stats[:, :, :, :, :].rearrange("p t s j h -> p (t s j h)"), stT_ps, w=NST * H)
                fill("st")
                pe.wait_ge(stT_ready, n)
                for h, b in enumerate(HB):
                    if h == 3:
                        pe.wait_ge(hdn_ready, i * H + 1)
                    if h >= 2:
                        mm(bank(b), weight("w1x"), xnT[:, :], start=True, stop=False)
                    mm(bank(b), w1s_sb[:, h, :], statsT, start=False, stop=True).then_inc(hid_ps, 1)
                pe.wait_ge(x2_ready, n)
                front_x(n2)
                fill("hid")
                pe.wait_ge(hdn_ready, i * H + H)
                for h in range(H):
                    last = mm(ps[CH * h:CH * h + CH, C1, :], col("w2T", 0, CH), hdn[h][:, :], start=True, stop=True)
                last.then_inc(lgT_ps, 1)
                front_router(n2)
                fill("lgT")
                pe.wait_ge(lgT_ready, n)
                transposes(C2, lgT, lgt_ps)
                fill("lgt")
                front_proj(n2)
                fill("front1")
                fill("front2")
                pe.wait_ge(on_ready, n)
                transposes(C2, o, oT_ps)
                fill("oT")
                pe.wait_ge(oT_ready, n)
                for t in range(NT):
                    last = mm(tile(bank(C2), t), tile(oT, t), weight("wo"), start=True, stop=True)
                last.then_inc(sp_ps, 1)
            for k in range(STEPS):
                layer1_step(k, B, B + 1)

        @block.scalar
        def _(act):
            f = nc.scalar.activation

            def front(m):
                act.wait_ge(xT_ps, m)
                f(xnN[:, :], bank(M0), ACT.Copy).then_inc(xnN_ready, 1)

            def own_xnT(m):
                act.wait_ge(xnN_ready, m)
                f(xnT[:, :], xnN[:, :], ACT.Copy).then_inc(xnT_ready, 1)

            def moe_gate(m):
                act.wait_ge(pacc, m * (EA - NV))
                f(gs[:, :], accp[:, :], ACT.Silu).then_inc(gs_ready, 1)

            def front_taps(m):
                for c, b, w, y in (("v", C1, "vc", yv), ("q", M0, "qc", yq), ("k", M1, "kc", yk)):
                    act.wait_ge(proj, m * 3 - 2 + "vqk".index(c))
                    f(y[:, :], bank(b), ACT.Copy, scale=col(w, KC - 1)).then_inc(tap, 1)

            def front_router(m):
                act.wait_ge(lgs_ready, m)
                f(sc[:, :, 0:E], lg[:, :, :], ACT.Exp).then_inc(ex_ready, 1)
                f(beta[:, :, :], ps[:, M1, 0:NT * (E + H)].rearrange("p (t c) -> p t c", t=NT)[:, :, E:E + H], ACT.Exp, scale=-1.0).then_inc(rb_read, 1)

            def layer1_step(k, i, n):
                if k == 1:
                    act.wait_ge(x1T_ps, n)
                    f(xn1p[:, 4:4 + L], bank(M0), ACT.Copy).then_inc(x1T_ready, 1)
                elif 2 <= k <= 5:
                    act.wait_ge(ffg_ps, i * FF + k - 1)
                    f(fh[k - 2][:, :], bank(M0), ACT.Silu, scale=col("s1", k - 2)).then_inc(sgf_ready, 1)
                elif 6 <= k <= 8:
                    for j, b, dst, fn, s in (((0, M0, rg, ACT.Sigmoid, 1.0), (1, M1, dec, ACT.Sigmoid, -1.0)),
                                             ((2, M0, kt, ACT.Tanh, 1.0), (3, M1, vv, ACT.Copy, 1.0)),
                                             ((4, M0, al, ACT.Sigmoid, 1.0), (5, M1, gg, ACT.Sigmoid, 1.0)))[k - 6]:
                        act.wait_ge(pj_ps, i * 6 + j + 1)
                        f(dst[:, :], bank(b), fn, scale=s).then_inc(pj_act, 1)
                elif k in (9, 10):
                    for c, b in ((2 * k - 18, M0), (2 * k - 17, M1)):
                        act.wait_ge(h1_ps, i * FF + c + 1)
                        f(g1[c][:, :], bank(b), ACT.Gelu, scale=col("hs1", c)).then_inc(g1_ready, 1)
                elif 11 <= k <= 13:
                    if k == 13:
                        act.wait_ge(cen_ready, n)
                        f(sqc[:, :], cen[:, :], ACT.Square).then_inc(sqc_ready, 1)
                    for c, b in (((0, M0), (1, M1)), ((2, M1),), ((3, M1),))[k - 11]:
                        act.wait_ge(h2_ps, i * FF + c + 1)
                        f(g2[c][:, :], bank(b), ACT.Gelu, scale=col("hs2", c)).then_inc(g2_ready, 1)
                elif k == 15:
                    act.wait_ge(var_ps, n)
                    f(rvar[:, :], bank(M0), ACT.Copy, bias=GN_EPS).then_inc(vare_ready, 1)
                elif k == 17:
                    act.wait_ge(g2r_ready, n)
                    f(g2r[:, :], g2r[:, :], ACT.Silu).then_inc(g2s_ready, 1)

            def layer1_rsd(n):
                act.wait_ge(rvar_ready, n)
                f(rvar[:, :], rvar[:, :], ACT.Sqrt).then_inc(rsd_ready, 1)

            act.wait_ge(s_w, 16 * 5)
            f(tmp1[:, 0:1], col("temp"), ACT.Abs).then_inc(temp_ready, 1)
            act.wait_ge(temp_ready, 1)
            f(tmp1[:, 1:2], tmp1[:, 0:1], ACT.Exp, scale=-1.0).then_inc(temp_ready, 1)
            act.wait_ge(temp_ready, 2)
            f(tmp1[:, 2:3], tmp1[:, 1:2], ACT.Ln, bias=1.0).then_inc(temp_ready, 1)
            f(tmp1[:, 3:4], col("temp"), ACT.Relu).then_inc(temp_ready, 1)
            front(1)
            front_router(1)
            front_taps(1)
            own_xnT(1)
            with act.Fori(0, B) as i:
                n = act.snap(i + 1)
                n2 = act.snap(i + 2)
                ie = act.snap(i * EA)
                ina = act.snap((i + 1) * (EA - NV))
                at = {"e": 0, "m": 0}

                def expert_unit(k):
                    e, kind = divmod(k, 3)
                    if kind == 0 and e < EA:
                        act.wait_ge(g_ps, ie + e + 1)
                        f(sg[e % 2][:, :], bank(G), ACT.Silu).then_inc(sg_ready, 1)
                    elif kind == 2 and e > 0 or k == UNITS - 1:
                        d = e - 1
                        if on_vector(d):
                            return
                        if before(d) == 0:
                            act.wait_ge(wsc_ready, n)
                        if d == EA - 1:
                            act.wait_ge(up_ps, ie + EA)
                            own_xnT(n2)
                        act.wait_ge(d_ps, ie + d + 1)
                        if before(d):
                            act.wait_ge(pacc, ina + before(d))
                        for t in range(NT):
                            s = wsc[:, t, d:d + 1] if d < E else 1.0
                            last = f(tile(dt, t), tile(bank(Db), t), ACT.Copy, scale=s)
                        last.then_inc(dt_ready, 1)

                def fill(name, between=None):
                    for u, c in enumerate(FILL[name]):
                        if between is not None:
                            between(u)
                        if c == "e":
                            expert_unit(at[c])
                        else:
                            layer1_step(at[c], i, n)
                        at[c] += 1

                def copy(dst, b, src_ready, done):
                    act.wait_ge(src_ready, n)
                    f(dst[:, 0:L], bank(b), ACT.Copy).then_inc(done, 1)

                fill("start", lambda u: u == 1 and moe_gate(n))
                for c, y, dst in (("v", yv, vs), ("q", yq, qs), ("k", yk, ks)):
                    act.wait_ge(conv, i * 3 + 1 + "vqk".index(c))
                    f(dst[:, :], y, ACT.Silu).then_inc(silu, 1)
                for c, b, dst, sq in (("q", C2, qtok, sq4[1]), ("k", C0, ktok, sq4[2])):
                    act.wait_ge(tok_ps[c], n)
                    f(sq, bank(b), ACT.Square).then_inc(sq_ready[c], 1)
                    f(dst[:, :], bank(b), ACT.Copy).then_inc(tok[c], 1)
                copy(vtok, C1, tok_ps["v"], tok["v"])
                fill("tok0")

                def norms():
                    act.wait_ge(ss_ready, n)
                    f(rn[:, :, :], ss[:, :, :], ACT.Sqrt).then_inc(rn_ready, 1)

                fill("tok", lambda u: u == 2 and norms())
                act.wait_ge(silu, i * 3 + 1)
                f(fs[:, :], vs[:, :], ACT.Copy, scale=col("fs", KS - 1)).then_inc(fir0, 1)
                f(fl[:, :], vs[:, :], ACT.Copy, scale=col("fl", KL - 1)).then_inc(fir0, 1)
                act.wait_ge(nT_ps["q"], n)
                f(WQ[:, :, CH:2 * CH], bank(C2).rearrange("p (c k) -> p c k", k=CH), ACT.Copy).then_inc(nT["q"], 1)
                for c, b, dst in (("k", C0, knT), ("b", C1, kbT)):
                    copy(dst, b, nT_ps[c], nT[c])
                fill("norm")
                act.wait_ge(x1_ready, n)
                f(xt[:, :], xin[:, :], ACT.Copy).then_inc(x_copied, 1)
                fill("L")
                fill("L3")
                fill("A")
                for l in range(1, LEVELS):
                    fill(f"lv{l}a")
                    act.wait_ge(yT_ps, i * (LEVELS - 1) + l)
                    f(YT[:, :], bank(C1), ACT.Copy).then_inc(yT_ready, 1)
                    fill(f"lv{l}b")
                    act.wait_ge(y_ps, i * (LEVELS - 1) + l)
                    f(Yi[:, :], bank(C2), ACT.Copy).then_inc(y_ready, 1)
                    fill(f"lv{l}c")
                    fill(f"lv{l}d")
                fill("inv")
                copy(U, C0, u_ps, u_ready)
                act.wait_ge(wt_ps, n)
                f(WQ[:, :, 0:CH], bank(C2).rearrange("p (c k) -> p c k", k=CH), ACT.Copy).then_inc(wt_ready, 1)
                fill("uw")
                for c in range(NCH):
                    t, g = divmod(c, NT)
                    act.wait_ge(ws_ps, i * NCH + c + 1)
                    qrow = 2 * CH * (c % 2) + CH
                    f(dq[CH * g:CH * g + CH, t * P:(t + 1) * P], ps[qrow:qrow + CH, C0, 0:P], ACT.Copy).then_inc(dq_ready, 1)
                    fill(f"sc{c}a")
                    fill(f"sc{c}b")
                    if c == NCH - 2:
                        layer1_rsd(n)
                copy(auT, C2, auT_ps, auT_ready)
                copy(lstok, C0, fsT_ps, ls_ready)
                copy(lltok, C1, flT_ps, ll_ready)
                fill("au")
                fill("fir")
                act.wait_ge(stq_ready, i * 4 + 4)
                f(stat(3), flat(st_q[:, :, :, :]), ACT.Sqrt).then_inc(l2_ready, 1)
                act.wait_ge(stT_ps, n)
                f(statsT, ps[0:NST * H, C2, :], ACT.Copy).then_inc(stT_ready, 1)
                fill("st")
                for h, b in enumerate((C0, C1, C2, C0)):
                    act.wait_ge(hid_ps, i * H + h + 1)
                    f(hdn[h][:, :], bank(b), ACT.Gelu, bias=col("b1")).then_inc(hdn_ready, 1)
                front(n2)
                fill("hid")
                copy(lgT, C1, lgT_ps, lgT_ready)
                fill("lgT")
                act.wait_ge(lgx_ready, n)
                f(fe[:, :, :], lgx[:, :, :], ACT.Exp).then_inc(fe_ready, 1)
                front_router(n2)
                fill("lgt")
                front_taps(n2)
                fill("front1")
                fill("front2")
                act.wait_ge(oT_ps, n)
                f(oT[:, :], bank(C2), ACT.Copy, scale=col("onorm")).then_inc(oT_ready, 1)
                fill("oT")
            moe_gate(B + 1)
            for k in range(STEPS):
                layer1_step(k, B, B + 1)
                if k == 16:
                    layer1_rsd(B + 1)

        @block.vector
        def _(dve):
            v = nc.vector
            tt, ts, stt_ = v.tensor_tensor, v.tensor_scalar, v.scalar_tensor_tensor
            links = [0, 0]

            def link(ins):
                links[0] += 1
                ins.then_inc(dve_link, 1)
                dve.wait_ge(dve_link, links[1] + links[0])

            def end_links():
                assert links[0] < DVE_LINKS, links[0]
                dve.engine_nop().then_inc(dve_link, DVE_LINKS - links[0])
                links[0] = 0

            def over(ap, shape):
                return ap.unsqueeze(2).to_broadcast(shape)

            def norm_stats(src, j, vr_ready):
                for t in range(NT):
                    last = v.bn_stats(bst[j][:, t, :], tile(src, t))
                link(last)
                v.memset(spare[:, 0:1], 0.0)
                for t in range(NT):
                    last = v.bn_aggr(mv[j][:, t, :], bst[j][:, t, :])
                link(last)
                ts(vr[j][:, :], mv[j][:, :, 1], LN_EPS, None, ALU.add).then_inc(vr_ready, 1)

            def norm_apply(src, dst, j, rstd_ready, m, done):
                dve.wait_ge(rstd_ready, m)
                for t in range(NT):
                    last = ts(tile(dst, t), tile(src, t), mv[j][:, t, 0:1], rstd[j][:, t:t + 1], ALU.subtract, ALU.mult)
                last.then_inc(done, 1)

            def front_logits(m):
                dve.wait_ge(rb_ps, m)
                lgp = ps[:, M1, 0:NT * (E + H)].rearrange("p (t c) -> p t c", t=NT)[:, :, 0:E]
                link(tt(lg[:, :, :], lgp, col("rbias", 0, E).unsqueeze(1).to_broadcast([P, NT, E]), ALU.add))
                link(v.tensor_reduce(mx[:, :], lg[:, :, :], X, ALU.max))
                tt(lg[:, :, :], lg[:, :, :], over(mx[:, :], [P, NT, E]), ALU.subtract).then_inc(lgs_ready, 1)

            CONVS = [(lag, c) for lag in range(1, KC) for c in "vqk"]

            def front_conv(m, a, units):
                if a == 0:
                    dve.wait_ge(tap, m * 3)
                for lag, c in CONVS[a * len(CONVS) // units:(a + 1) * len(CONVS) // units]:
                    b, w, y = {"v": (C1, "vc", yv), "q": (M0, "qc", yq), "k": (M1, "kc", yk)}[c]
                    ins = stt_(y[:, lag:L], ps[:, b, 0:L - lag], col(w, KC - 1 - lag), y[:, lag:L], ALU.mult, ALU.add)
                    if lag == KC - 1:
                        ins.then_inc(conv, 1)
                    elif c == "k":
                        link(ins)

            def front_topk(m):
                dve.wait_ge(ex_ready, m)
                dve.wait_ge(rb_read, m)
                link(ts(beta[:, :, :], beta[:, :, :], 1.0, None, ALU.add))
                v.reciprocal(beta[:, :, :], beta[:, :, :]).then_inc(beta_ready, 1)
                link(v.tensor_reduce(ssum[:, :], sc[:, :, 0:E], X, ALU.add))
                link(v.reciprocal(ssum[:, :], ssum[:, :]))
                link(tt(sc[:, :, 0:E], sc[:, :, 0:E], over(ssum[:, :], [P, NT, E]), ALU.mult))
                v.memset(spare[:, 1:2], 0.0)
                for t in range(NT):
                    last = v.max(m8[:, t, :], sc[:, t, 0:E])
                link(last)
                v.tensor_copy(m4[:, :, 0:TOPK], m8[:, :, 0:TOPK])
                link(v.tensor_reduce(mx[:, :], m8[:, :, 0:TOPK], X, ALU.add))
                link(ts(mx[:, :], mx[:, :], 1e-12, None, ALU.max))
                v.reciprocal(mx[:, :], mx[:, :])
                for t in range(NT):
                    last = v.match_replace(rep[:, t, :], m4[:, t, :], sc[:, t, :], -2.0)
                link(last)
                tt(rep[:, :, 0:E], rep[:, :, 0:E], sc[:, :, 0:E], ALU.not_equal).then_inc(rep_ready, 1)

            def routing_weights(m):
                dve.wait_ge(rep_ready, m)
                link(tt(wsc[:, :, :], rep[:, :, 0:E], sc[:, :, 0:E], ALU.mult))
                tt(wsc[:, :, :], wsc[:, :, :], over(mx[:, :], [P, NT, E]), ALU.mult).then_inc(wsc_ready, 1)

            def mix(js):
                for j in js:
                    stt_(mixd[j][:, :], dT[:, :], col("mix", j), xn1p[:, 4:4 + L], ALU.mult, ALU.add).then_inc(mix_ready, 1)

            def recip(t):
                return v.reciprocal(tile(rvar, t), tile(rvar, t))

            def layer1_groupnorm(n):
                dve.wait_ge(rsd_ready, n)
                link(tt(cen[:, :], cen[:, :], rvar[:, :], ALU.mult))
                ts(cen[:, :], cen[:, :], col("gnw"), col("gnb"), ALU.mult, ALU.add).then_inc(mn_ready, 1)

            def gated(m):
                dve.wait_ge(sp_ps, m)
                dve.wait_ge(gs_ready, m)
                tt(x1[:, :], bank(C2), gs[:, :], ALU.mult).then_inc(sp_read, 1)

            def layer1_late(k, i, n):
                if k == 0:
                    norm_apply(x1, xn1, 1, rstd1_ready, n, xn1_ready)
                elif k == 15:
                    recip(1)
                elif k == 16:
                    recip(3).then_inc(rvar_ready, 1)
                elif 2 <= k <= 5:
                    c = k - 2
                    dve.wait_ge(sgf_ready, i * FF + c + 1)
                    dve.wait_ge(ffu_ps, i * FF + c + 1)
                    stt_(fh[c][:, :], bank(M1), col("s2", c), fh[c][:, :], ALU.mult, ALU.mult).then_inc(fh_ready, 1)
                    mix(((1,), (2, 3), (4,), (5,))[c])

            def layer1_step(k, i, n):
                rows = "p (t d) -> p t d"
                if k == 0:
                    dve.wait_ge(x1_ready, n)
                    norm_stats(x1, 1, vr1_ready)
                elif k == 2:
                    dve.wait_ge(x1T_ready, n)
                    link(tt(dT[:, :], xn1p[:, 3:3 + L], xn1p[:, 4:4 + L], ALU.subtract))
                    mix((0,))
                elif k == 10:
                    dve.wait_ge(uu_ready, n)
                    v.tensor_tensor_scan(stt[:, :], dec[:, :], uu[:, :], 0.0, ALU.mult, ALU.add).then_inc(st_ready, 1)
                elif k == 13:
                    dve.wait_ge(mu_ps, n)
                    tt(cen[:, :], mixed[:, :], bank(M0), ALU.subtract).then_inc(cen_ready, 1)
                elif k == 15:
                    dve.wait_ge(vare_ready, n)
                    recip(0)
                elif k == 16:
                    recip(2)
                elif k == 17:
                    dve.wait_ge(w3_ps, i * 2 + 2)
                    tt(g2r[:, :].rearrange(rows, d=D), bank(M1).rearrange(rows, d=D),
                       col("w3s", 0, D).unsqueeze(1).to_broadcast([P, NT, D]), ALU.mult).then_inc(g2r_ready, 1)
                elif k == 18:
                    dve.wait_ge(op_ps, n)
                    link(tt(s1[:, :].rearrange(rows, d=D), bank(M0).rearrange(rows, d=D),
                            col("bout", 0, D).unsqueeze(1).to_broadcast([P, NT, D]), ALU.add))
                    dve.wait_ge(g2s_ready, n)
                    link(tt(s1[:, :], s1[:, :], g2r[:, :], ALU.mult))
                    dve.wait_ge(x2_stored, 16 * n)
                    tt(x2[:, :], x1[:, :], s1[:, :], ALU.add).then_inc(x2_ready, 1)

            v.memset(sc[:, :, E:E + TOPK], -1.0)
            v.memset(m4[:, :, TOPK:8], -1.0)
            v.memset(xn1p[:, 0:4], 0.0)
            v.memset(spare[:, :], 0.0)
            v.memset(xt[:, :], 0.0)
            v.memset(bank(C2), 0.0).then_inc(sp_ps, 1)
            v.memset(unit[:, 0:1], 0.0).then_inc(x2_stored, 32)
            v.memset(unit[:, 1:2], -0.5).then_inc(unit_ready, 1)
            dve.wait_ge(s_w, 16 * 5)
            dve.wait_ge(temp_ready, 4)
            tt(tmp1[:, 0:1], tmp1[:, 2:3], tmp1[:, 3:4], ALU.add).then_inc(temp_ready, 1)
            dve.wait_ge(temp_ready, 5)
            ts(tmp1[:, 1:2], tmp1[:, 0:1], 0.0001, None, ALU.add).then_inc(temp_ready, 1)
            dve.wait_ge(temp_ready, 6)
            v.reciprocal(invt[:, :], tmp1[:, 1:2]).then_inc(temp_ready, 1)
            dve.wait_ge(temp_ready, 7)
            ts(b2t[:, :], col("b2", 0, 4), invt[:, :], None, ALU.mult).then_inc(temp_ready, 1)
            dve.wait_ge(temp_ready, 8)
            dve.wait_ge(x_loaded, 16)
            norm_stats(xin, 0, vr0_ready)
            norm_apply(xin, xn, 0, rstd0_ready, 1, xn_ready)
            front_logits(1)
            front_conv(1, 0, 1)
            front_topk(1)
            end_links()
            with dve.Fori(0, B) as i:
                n = dve.snap(i + 1)
                n2 = dve.snap(i + 2)
                ie = dve.snap(i * EA)
                iv = dve.snap(i * NV)
                links[1] = dve.snap(n * DVE_LINKS)
                at = {"e": 0, "m": 0}
                taps = [("l", j) for j in range(1, KL)]
                for j in range(1, KS):
                    taps.insert(2 * j, ("s", j))
                tap_at = [0]

                def expert_unit(k):
                    e, kind = divmod(k, 3)
                    if kind == 1 and e < EA:
                        dve.wait_ge(sg_ready, ie + e + 1)
                        dve.wait_ge(up_ps, ie + e + 1)
                        tt(hx[e % 2][:, :], bank(Ub), sg[e % 2][:, :], ALU.mult).then_inc(h_ready, 1)
                    elif kind == 2 and e > 0 or k == UNITS - 1:
                        d = e - 1
                        if not on_vector(d):
                            return
                        dve.wait_ge(d_ps, ie + d + 1)
                        if d:
                            dve.wait_ge(dacc, iv + before(d))
                        else:
                            dve.wait_ge(wsc_ready, n)
                        for t in range(NT):
                            s = wsc[:, t, d:d + 1] if d < E else 1.0
                            if d == 0:
                                last = ts(tile(acc, t), tile(bank(Db), t), s, None, ALU.mult)
                            else:
                                last = stt_(tile(acc, t), tile(bank(Db), t), s, tile(acc, t), ALU.mult, ALU.add)
                        last.then_inc(dacc, 1)

                def fir(m):
                    for _ in range(m):
                        if tap_at[0] == len(taps):
                            return
                        kind, lag = taps[tap_at[0]]
                        y, w, last_tap, done = (fs, "fs", KS - 1, fs_ready) if kind == "s" else (fl, "fl", KL - 1, fl_ready)
                        if tap_at[0] == 0:
                            dve.wait_ge(fir0, i * 2 + 2)
                        tap_at[0] += 1
                        ins = stt_(y[:, lag:L], vs[:, 0:L - lag], col(w, last_tap - lag), y[:, lag:L], ALU.mult, ALU.add)
                        if lag == last_tap:
                            ins.then_inc(done, 1)
                        else:
                            link(ins)

                def fill(name, taps_per_unit=0.0, between=None):
                    for u, c in enumerate(FILL[name]):
                        if between is not None:
                            between(u)
                        if c == "e":
                            expert_unit(at[c])
                        else:
                            layer1_step(at[c], i, n)
                        at[c] += 1
                        fir(int((u + 1) * taps_per_unit) - int(u * taps_per_unit))

                fill("start", 0.0, lambda u: u == 2 and gated(n))
                routing_weights(n)
                fill("tok0")
                for j, c in enumerate("qk"):
                    dve.wait_ge(sq_ready[c], n)
                    last = v.tensor_reduce(ss[:, j, :], byhead(sq4[1 + j]), X, ALU.add)
                link(last)
                v.reciprocal(ss[:, :, :], ss[:, :, :]).then_inc(ss_ready, 1)

                def normalised(j, c, buf, done):
                    dve.wait_ge(tok[c], n)
                    dve.wait_ge(rn_ready, n)
                    tt(byhead(buf[:, :]), byhead(buf[:, :]), over(rn[:, j, :], [P, HT, DH]), ALU.mult).then_inc(done, 1)

                fill("tok", 0.0, lambda u: u == len(FILL["tok"]) - 1 and
                     (normalised(0, "q", qtok, qn_ready), normalised(1, "k", ktok, kn_ready)))
                fill("norm", 1.0)

                def lower(h):
                    dve.wait_ge(l_ps, i * H + h + 1)
                    tt(LT[:, h * NT:(h + 1) * NT, :], bank((C0, C1, C2, C0)[h]).rearrange("p (t s) -> p t s", t=NT),
                       con("strict").unsqueeze(1).to_broadcast([P, NT, P]), ALU.mult).then_inc(lt_ready, 1)

                for h in (0, 1, 2):
                    lower(h)
                fill("L")
                lower(3)
                chunks = "p (a j) -> p a j"

                def masked(dst, src, name, l):
                    a = CONS[name][0] + l * CH
                    return tt(dst.rearrange(chunks, j=CH), src.rearrange(chunks, j=CH),
                              cn[:, a:a + CH].unsqueeze(1).to_broadcast([P, HT, CH]), ALU.mult)

                def transposed(l, c):
                    if c >= P // CH:
                        return
                    if c == 0:
                        dve.wait_ge(xi_ready, i * LEVELS + l)
                    r = slice(CH * c, CH * c + CH)
                    v.transpose(Tbd[r, :, CH * c:CH * c + CH], Xi[r, :].rearrange(chunks, j=CH)).then_inc(tbd_ready, 1)

                dve.wait_ge(tbd_clear, 1)
                dve.wait_ge(lt_ready, i * H + H)
                def rows_of_l(c):
                    if c < P // CH:
                        r = slice(CH * c, CH * c + CH)
                        v.transpose(Yi[r, :].rearrange(chunks, j=CH), LT[r, :, CH * c:CH * c + CH]).then_inc(rows_ready, 1)

                fill("L3", 0.0, rows_of_l)
                for c in range(len(FILL["L3"]), P // CH):
                    rows_of_l(c)
                dve.wait_ge(rows_ready, (i + 1) * (P // CH))
                link(masked(Yi[:, :], Yi[:, :], "lvl0", 0))
                tt(Xi[:, :].rearrange(chunks, j=CH), con("eye").unsqueeze(1).to_broadcast([P, HT, CH]),
                   Yi[:, :].rearrange(chunks, j=CH), ALU.subtract).then_inc(xi_ready, 1)
                fill("A", 0.67)
                for l in range(1, LEVELS):
                    done = 0
                    for part in "abc":
                        fill(f"lv{l}{part}", {"a": 0.0, "b": 0.0, "c": 1.0}[part], lambda u: transposed(l, done + u))
                        done += len(FILL[f"lv{l}{part}"])
                    for c in range(done, P // CH):
                        transposed(l, c)
                    dve.wait_ge(zT_ps, i * (LEVELS - 1) + l)
                    masked(ZT[:, :], bank(C0), "lvlT", l - 1).then_inc(zT_ready, 1)
                    fill(f"lv{l}d", 1.0)
                    dve.wait_ge(z_ps, i * (LEVELS - 1) + l)
                    tt(Xi[:, :], Xi[:, :], bank(C2), ALU.subtract).then_inc(xi_ready, 1)
                fill("inv", 0.4, lambda u: u < P // CH and transposed(LEVELS, u))
                fill("uw", 0.0, lambda u: u == 2 and layer1_late(0, i, n))
                srcs = (lstok, lltok, dl, vtok)

                def branch_stat(j, kind):
                    if kind == 0:
                        if j < 2:
                            dve.wait_ge((ls_ready, ll_ready)[j], n)
                        v.tensor_reduce(st_s[:, :, j, :], tilehead(srcs[j][:, :]), X, ALU.add)
                    elif kind == 1:
                        v.tensor_reduce(st_a[:, :, j, :], tilehead(srcs[j][:, :]), X, ALU.add, apply_absolute_value=True)
                    else:
                        dve.wait_ge(sq4_ready, i * 4 + (3, 2, 0, 1).index(j) + 1)
                        v.tensor_reduce(st_q[:, :, j, :], tilehead(sq4[j]), X, ALU.add).then_inc(stq_ready, 1)

                def branch_stats(js, a, units):
                    todo = [(j, kind) for j in js for kind in range(3)]
                    for j, kind in todo[a * len(todo) // units:(a + 1) * len(todo) // units]:
                        branch_stat(j, kind)

                dve.wait_ge(u_ready, n)
                for c in range(NCH):
                    t, g = divmod(c, NT)
                    r = slice(CH * g, CH * g + CH)
                    wrow = 2 * CH * (c % 2)
                    dve.wait_ge(ws_ps, i * NCH + c + 1)
                    tt(tile(uadj, t)[r, :], tile(U, t)[r, :], ps[wrow:wrow + CH, C0, 0:P], ALU.subtract).then_inc(uadj_ready, 1)
                    if c % 4 == 2:
                        h = c // 4
                        dve.wait_ge(a_ps, i * H + h + 1)
                        tt(AT[:, h * NT:(h + 1) * NT, :], bank(C2).rearrange("p (t s) -> p t s", t=NT),
                           con("causal").unsqueeze(1).to_broadcast([P, NT, P]), ALU.mult).then_inc(at_ready, 1)
                    fill(f"sc{c}a", SCAN_TAPS[c])
                    if c < NCH - 1:
                        dve.wait_ge(s_ps, i * (NCH - 1) + c + 1)
                        tt(Sbd[:, :], ps[:, C1, 0:P], con("bd"), ALU.mult).then_inc(s_ready, 1)
                    if "m" in FILL[f"sc{c}a"] and c < NCH - 1:
                        layer1_late(at["m"] - 1, i, n)
                    fill(f"sc{c}b", 0.0 if c < 3 else 1.0)
                    if c == 7:
                        branch_stats((3,), 0, 1)
                    if c == 8:
                        dve.wait_ge(x_loaded, 16 * n2)
                        norm_stats(xin, 0, vr0_ready)
                layer1_groupnorm(n)
                fir(len(taps))
                dve.wait_ge(au_ps, n)
                dve.wait_ge(dq_ready, i * NCH + NCH)
                tt(dl[:, :], bank(C2), dq[:, :], ALU.add).then_inc(dl_ready, 1)
                dve.wait_ge(dl_ready, n)
                units = len(FILL["au"]) + len(FILL["fir"])

                def fir_part(u):
                    branch_stats((2, 0, 1), u + len(FILL["au"]), units)
                    if u == len(FILL["fir"]) - 1:
                        dve.wait_ge(stq_ready, i * 4 + 4)
                        link(ts(stat(0), flat(st_s[:, :, :, :]), 1.0 / DH, None, ALU.mult))
                        link(tt(m2_c[:, :, :], stat(0), stat(0), ALU.mult))
                        stt_(stat(1), flat(st_q[:, :, :, :]), 1.0 / DH, m2_c[:, :, :], ALU.mult, ALU.subtract)
                        ts(stat(2), flat(st_a[:, :, :, :]), 1.0 / DH, None, ALU.mult).then_inc(stats_ready, 1)

                fill("au", 0.0, lambda u: branch_stats((2, 0, 1), u, units))
                fill("fir", 0.0, fir_part)
                fill("st")
                norm_apply(xin, xn, 0, rstd0_ready, n2, xn_ready)
                fill("hid")
                fill("lgT")
                front_logits(n2)
                dve.wait_ge(lgt_ps, n)
                link(stt_(lgx[:, :, :], bank(C2).rearrange("p (a k) -> p a k", k=CH)[:, :, 0:4], invt[:, :],
                          b2t[:, :].unsqueeze(1).to_broadcast([P, HT, 4]), ALU.mult, ALU.add))
                link(v.tensor_reduce(lmx[:, :], lgx[:, :, :], X, ALU.max))
                tt(lgx[:, :, :], lgx[:, :, :], over(lmx[:, :], [P, HT, 4]), ALU.subtract).then_inc(lgx_ready, 1)
                fill("lgt")
                dve.wait_ge(fe_ready, n)
                link(v.tensor_reduce(fsum[:, :], fe[:, :, :], X, ALU.add))
                link(v.reciprocal(fsum[:, :], fsum[:, :]))
                link(tt(fw[:, :, :], fe[:, :, :], over(fsum[:, :], [P, HT, 4]), ALU.mult))
                ts(fw[:, :, 0], fw[:, :, 0], col("rss"), None, ALU.add)
                ts(fw[:, :, 1], fw[:, :, 1], col("rsl"), None, ALU.add).then_inc(fw_ready, 1)
                dve.wait_ge(fw_ready, n)
                for j in (0, 1, 2):
                    last = tt(byhead(pr[j]), byhead(srcs[j][:, :]), over(fw[:, :, j], [P, HT, DH]), ALU.mult)
                link(last)
                link(tt(o[:, :], pr[0], pr[1], ALU.add))
                link(tt(o[:, :], o[:, :], pr[2], ALU.add))
                dve.wait_ge(p3_ready, n)
                tt(o[:, :], o[:, :], pr[3], ALU.add).then_inc(o_sum, 1)
                conv_units = len(CONVS) + 3
                early = 3 + len(FILL["front1"])
                fill("front1", 0.0, lambda u: front_conv(n2, u, conv_units))

                def o_normalised():
                    dve.wait_ge(rms_ready, n)
                    tt(byhead(o[:, :]), byhead(o[:, :]), over(rms[:, :], [P, HT, DH]), ALU.mult).then_inc(on_ready, 1)

                dve.wait_ge(osq_ready, n)
                link(v.tensor_reduce(ms[:, :], byhead(osq[:, :]), X, ALU.add))
                ts(ms[:, :], ms[:, :], 1.0 / DH, RMS_EPS, ALU.mult, ALU.add).then_inc(ms_ready, 1)
                fill("front2", 0.0, lambda u: u < 3 and front_conv(n2, early - 3 + u, conv_units) or u == len(FILL["front2"]) - 1 and o_normalised())
                fill("oT", 0.0, lambda u: u < 4 and front_conv(n2, early + u, conv_units))
                for u in range(early + 4, conv_units):
                    front_conv(n2, u, conv_units)
                front_topk(n2)
                end_links()
            links[1] = (B + 1) * DVE_LINKS
            gated(B + 1)
            for k in range(STEPS):
                layer1_step(k, B, B + 1)
                layer1_late(k, B, B + 1)
                if k == 16:
                    layer1_groupnorm(B + 1)

        @block.gpsimd
        def _(pool):
            g = nc.gpsimd
            tt = g.tensor_tensor
            g.memset(Tbd[:, :, :], 0.0).then_inc(tbd_clear, 1)

            def rsqrt(dst, src):
                return tt(dst, src, unit[:, 1:2].to_broadcast(list(dst.shape)), ALU.pow)

            def layer1_step(k, i, n):
                if k == 0:
                    pool.wait_ge(vr1_ready, n)
                    rsqrt(rstd[1][:, :], vr[1][:, :]).then_inc(rstd1_ready, 1)
                elif k == 9:
                    pool.wait_ge(pj_act, i * 6 + 5)
                    tt(kt[:, :], al[:, :], kt[:, :], ALU.mult).then_inc(ak_ready, 1)
                    pool.wait_ge(ak_ready, n)
                    tt(uu[:, :], kt[:, :], vv[:, :], ALU.mult).then_inc(uu_ready, 1)
                elif k == 11:
                    pool.wait_ge(st_ready, n)
                    tt(mixed[:, :], rg[:, :], stt[:, :], ALU.mult).then_inc(mixed_ready, 1)

            def residual(m):
                pool.wait_ge(sp_read, m)
                pool.wait_ge(x_copied, m - 1)
                tt(x1[:, :], x1[:, :], xt[:, :], ALU.add).then_inc(x1_ready, 1)

            def layer1_gate(i, n):
                pool.wait_ge(mn_ready, n)
                pool.wait_ge(pj_act, i * 6 + 6)
                tt(mg[:, :], cen[:, :], gg[:, :], ALU.mult).then_inc(mg_ready, 1)

            g.memset(accp[:, :], 0.0).then_inc(pacc, EA - NV)
            pool.wait_ge(s_w, 16 * 5)
            pool.wait_ge(unit_ready, 1)
            pool.wait_ge(vr0_ready, 1)
            rsqrt(rstd[0][:, :], vr[0][:, :]).then_inc(rstd0_ready, 1)
            with pool.Fori(0, B) as i:
                n = pool.snap(i + 1)
                n2 = pool.snap(i + 2)
                iv, ia, ina = pool.snap(i * NV), pool.snap(i * (EA - NV)), pool.snap((i + 1) * (EA - NV))
                at = {"e": 0, "m": 0}

                def expert_unit(k):
                    e, kind = divmod(k, 3)
                    if kind == 2 and e > 0 or k == UNITS - 1:
                        d = e - 1
                        if on_vector(d):
                            return
                        if d < EA - 1:
                            pool.wait_ge(dt_ready, ia + before(d) + 1)
                        if before(d) == 0:
                            tt(accp[:, :], dt[:, :], unit[:, 0:1].to_broadcast([P, L]), ALU.add).then_inc(pacc, 1)
                        else:
                            pool.wait_ge(pacc, ina + before(d))
                            if d == EA - 1:
                                pool.wait_ge(dacc, iv + NV)
                                tt(accp[:, :], accp[:, :], acc[:, :], ALU.add).then_inc(asum_one, 1)
                                pool.wait_ge(asum_one, n)
                                pool.wait_ge(dt_ready, ia + EA - NV)
                            last = tt(accp[:, :], accp[:, :], dt[:, :], ALU.add)
                            last.then_inc(pacc, 1)

                def fill(name):
                    for c in FILL[name]:
                        if c == "e":
                            expert_unit(at[c])
                        else:
                            layer1_step(at[c], i, n)
                        at[c] += 1

                def per_head(dst, src, scale, done):
                    tt(byhead(dst[:, :]), byhead(src[:, :]), scale.unsqueeze(2).to_broadcast([P, HT, DH]), ALU.mult).then_inc(done, 1)

                betas = beta[:, :, :].rearrange("p t h -> p (t h)")
                fill("start")
                residual(n)
                pool.wait_ge(beta_ready, n)
                pool.wait_ge(tok["v"], n)
                per_head(vb, vtok, betas, vb_ready)
                fill("tok0")
                fill("tok")
                pool.wait_ge(kn_ready, n)
                per_head(kb, ktok, betas, kb_ready)
                g.memset(Sbd[:, :], 0.0).then_inc(s0_ready, 1)
                for name in ["norm", "L", "L3", "A"] + [f"lv{l}{part}" for l in range(1, LEVELS) for part in "abcd"] + ["inv"]:
                    fill(name)
                squares = lambda j, src: tt(sq4[j], src[:, :], src[:, :], ALU.mult).then_inc(sq4_ready, 1)
                pool.wait_ge(yT_ps, (i + 1) * (LEVELS - 1))
                squares(3, vtok)
                fill("uw")
                for c in range(NCH):
                    fill(f"sc{c}a")
                    fill(f"sc{c}b")
                    if c == 12:
                        pool.wait_ge(vr0_ready, n2)
                        rsqrt(rstd[0][:, :], vr[0][:, :]).then_inc(rstd0_ready, 1)
                layer1_gate(i, n)
                for j, src, ready in ((2, dl, dl_ready), (0, lstok, ls_ready), (1, lltok, ll_ready)):
                    pool.wait_ge(ready, n)
                    squares(j, src)
                fill("au")
                fill("fir")
                fill("st")
                fill("hid")
                fill("lgT")
                fill("lgt")
                pool.wait_ge(fw_ready, n)
                tt(byhead(pr[3]), byhead(vtok[:, :]), fw[:, :, 3].unsqueeze(2).to_broadcast([P, HT, DH]), ALU.mult).then_inc(p3_ready, 1)
                pool.wait_ge(o_sum, n)
                tt(osq[:, :], o[:, :], o[:, :], ALU.mult).then_inc(osq_ready, 1)
                fill("front1")
                pool.wait_ge(ms_ready, n)
                rsqrt(rms[:, :], ms[:, :]).then_inc(rms_ready, 1)
                fill("front2")
                fill("oT")
            residual(B + 1)
            for k in range(STEPS):
                layer1_step(k, B, B + 1)
                if k == 16:
                    layer1_gate(B, B + 1)


def constants():
    p = np.arange(P)
    same = p[:, None] // CH == p[None, :] // CH
    c = np.zeros((P, NCON), np.float32)

    def put(name, a):
        c[:, CONS[name][0]:CONS[name][1]] = a

    put("ident", np.eye(P))
    put("bd", same)
    put("avg", (p[:, None] // 8 == p[None, :] // 8) / 8.0)
    put("strict", same & (p[:, None] < p[None, :]))
    put("causal", same & (p[:, None] <= p[None, :]))
    r, j = p[:, None] % CH, np.arange(CH)[None, :]
    put("eye", r == j)
    level = lambda r, j, s: (r // (2 * s) == j // (2 * s)) & (r // s % 2 == 1) & (j // s % 2 == 0)
    put("lvl0", level(r, j, 1))
    put("lvlT", np.concatenate([level(j, r, 1 << l) for l in range(1, LEVELS)], axis=1))
    return c


def kernel(**inputs):
    import concourse.bacc as _bacc
    from concourse.bass_utils import run_bass_kernel_spmd as _run

    a = {k: np.asarray(v) for k, v in inputs.items()}
    l0, ff0, l1, ff1 = (lambda k, p=p: a[p + k] for p in ("L0_attn_", "L0_ffn_", "L1_attn_", "L1_ffn_"))

    def rows(vec, n=P):
        return np.broadcast_to(vec.reshape(1, -1), (n, vec.size))

    small = np.zeros((P, NCOL), np.float32)
    for name, val in (("qc", l0("q_conv_w")), ("kc", l0("k_conv_w")), ("vc", l0("v_conv_w")), ("fs", l0("fir_short_w").reshape(D, KS)),
                      ("fl", l0("fir_long_w").reshape(D, KL)), ("b1", l0("fuse_b1").reshape(P, 1)),
                      ("mix", np.stack([l1(f"x_{c}").reshape(D) for c in "rwkvag"], axis=1)),
                      ("gnw", l1("gn_w").reshape(D, 1)), ("gnb", l1("gn_b").reshape(D, 1)),
                      ("s1", ff1("w1_s").reshape(FF, P).T), ("s2", ff1("w2_s").reshape(FF, P).T),
                      ("hs1", ff1("h1_s").reshape(FF, P).T), ("hs2", ff1("h2_s").reshape(FF, P).T),
                      ("temp", rows(l0("logit_temp"))), ("rss", rows(l0("res_scale_short"))), ("rsl", rows(l0("res_scale_long"))),
                      ("b2", rows(l0("fuse_b2"))), ("onorm", np.tile(l0("o_norm_w"), H).reshape(D, 1)), ("rbias", rows(ff0("router_bias"))),
                      ("bout", rows(l1("b_out"))), ("w3s", rows(ff1("w3_s"))), ("w2T", np.concatenate([l0("fuse_w2").T, np.zeros((P, CH - 4), np.float32)], axis=1))):
        small[:, COLS[name][0]:COLS[name][1]] = val
    w1 = l0("fuse_w1")
    w1s = np.zeros((NST, H, H, P), np.float32)
    for h in range(H):
        w1s[:, h, h, :] = w1[:, D:].T
    arrays = {
        "x": np.concatenate([l0("hidden_states"), np.zeros((1, L, D), np.float32)]),
        "small": small,
        "cons": constants(),
        "wsq": np.stack([l0("q_proj_w").T, l0("k_proj_w").T, l0("v_proj_w").T, w1[:, :D].T, l0("o_proj_w").T]
                        + [l1(f"W_{c}").T for c in ("r", "w", "k", "v", "a", "g", "out")], axis=1),
        "wrb": np.concatenate([ff0("router_w").T, l0("b_proj_w").T], axis=1),
        "w1s": w1s.reshape(4, 4, H, H, P).transpose(1, 0, 2, 3, 4).reshape(NST * H, H, P),
        "moe_g": np.concatenate([ff0("gate_w").transpose(2, 0, 1), ff0("sgate_w").T.reshape(D, ES, P)], axis=1),
        "moe_u": np.concatenate([ff0("up_w").transpose(2, 0, 1), ff0("sup_w").T.reshape(D, ES, P)], axis=1),
        "moe_d": np.concatenate([ff0("down_w").transpose(2, 0, 1), ff0("sdown_w").T.reshape(ES, P, D).transpose(1, 0, 2)], axis=1),
        "f1": ff1("w1_w").T.reshape(D, FF, P),
        "f2": ff1("w2_w").T.reshape(D, FF, P),
        "h1w": ff1("h1_w").T.reshape(FF, P, FF * P).transpose(1, 0, 2),
        "h2w": ff1("h2_w").T.reshape(FF, P, FF * P).transpose(1, 0, 2),
        "w3": ff1("w3_w").T.reshape(FF, P, D).transpose(1, 0, 2),
    }
    arrays = {k: np.ascontiguousarray(v) for k, v in arrays.items()}
    nc = _bacc.Bacc("TRN2", target_bir_lowering=False, num_devices=1)
    args = [nc.dram_tensor(k, v.shape, mybir.dt.float32, kind="ExternalInput").ap() for k, v in arrays.items()]
    args.append(nc.dram_tensor("out", (B, L, D), mybir.dt.float32, kind="ExternalOutput").ap())
    build(nc, *args)
    r = _run(nc, [arrays], core_ids=[0])
    return r.results[0]["out"]
```
